# Optimizing a Trainium2 kernel written in Bass

```python
import numpy as np
import jax
import jax.numpy as jnp

def _softmax(x, axis=-1):
    return jax.nn.softmax(x, axis=axis)

def _gelu(x):
    return jax.nn.gelu(x, approximate=True)

def _silu(x):
    return jax.nn.silu(x)

def _sigmoid(x):
    return jax.nn.sigmoid(x)

def _layernorm(x, axis=-1, eps=1e-05):
    m = jnp.mean(x, axis=axis, keepdims=True)
    v = jnp.var(x, axis=axis, keepdims=True)
    return (x - m) / jnp.sqrt(v + eps)

def _scatter_add(tgt, idx, src, axis=0):
    return tgt.at[idx].add(src)

def _segment_sum(src, seg, n):
    return jax.ops.segment_sum(src, seg, n)
kernel_name = 'mk_decoder_postln_d1_seqx_r8_f8f59e'

def setup_inputs(seed: int=0):
    np.random.seed(seed)
    _w = jnp.asarray

    def _rec_inputs():
        import jax
        import jax.numpy as jnp
        _rk = jax.random.key(seed)
        x = 0.0002279 + 0.9999 * jax.random.normal(jax.random.fold_in(_rk, 1), (16, 100, 128), jnp.float32)
        _lenS = 100 - jax.random.randint(jax.random.fold_in(_rk, 7), (16,), 0, max(1, 100 // 4) + 1, jnp.int32)
        _lenS2 = 1444 - jax.random.randint(jax.random.fold_in(_rk, 8), (16,), 0, max(1, 1444 // 4) + 1, jnp.int32)
        _ctx_1024P = jax.random.normal(jax.random.fold_in(_rk, 11), (16, 16, 128), jnp.float32)
        _ctx_1024c = jax.random.dirichlet(jax.random.fold_in(_rk, 511), 0.3 * jnp.ones((16,), jnp.float32), (16, 1444))
        _ctx_1024t = jnp.einsum('bsk,bkd->bsd', _ctx_1024c, _ctx_1024P)
        _ctx_1024t = _ctx_1024t * jax.lax.rsqrt(jnp.mean(jnp.square(_ctx_1024t)) + 1e-12) * 0.953939
        ctx_1024 = -0.000392918 + 0.999932 * (_ctx_1024t + 0.3 * jax.random.normal(jax.random.fold_in(_rk, 611), (16, 1444, 128), jnp.float32))
        fside_Bx16_0 = 0.119436 + 0.907674 * jax.random.normal(jax.random.fold_in(_rk, 12), (16, 16), jnp.float32)
        return (x, ctx_1024, fside_Bx16_0)
    x, ctx_1024, fside_Bx16_0 = _rec_inputs()

    def _L0_attn_setup():
        import jax, jax.numpy as jnp
        import numpy as np
        EPS = 1e-06
        LN3 = 1.0986122886681098
        ROPE_BASE = 10000.0

        def exact_rmsnorm(x, g):
            ms = jnp.mean(jnp.square(x), axis=-1, keepdims=True)
            return x * jax.lax.rsqrt(ms + EPS) * g

        def ternary_rope(t):
            S, D = (t.shape[-2], t.shape[-1])
            half = D // 2
            inv_freq = 1.0 / ROPE_BASE ** (jnp.arange(half, dtype=jnp.float32) / half)
            ang = jnp.arange(S, dtype=jnp.float32)[:, None] * inv_freq[None, :]
            cos = jnp.round(jnp.cos(ang))
            sin = jnp.round(jnp.sin(ang))
            cos = jnp.concatenate([cos, cos], axis=-1)
            sin = jnp.concatenate([sin, sin], axis=-1)
            rot = jnp.concatenate([-t[..., half:], t[..., :half]], axis=-1)
            return t * cos + rot * sin

        def ternary_softmax(x, axis=-1):
            return jax.nn.softmax(x * LN3, axis=axis)
        key = jax.random.key(seed)
        ks = jax.random.split(key, 6)
        B, S, D = (4, 512, 128)
        x = jax.random.normal(ks[0], (B, S, D), dtype=jnp.float32)
        g_norm = jnp.ones((D,), dtype=jnp.float32)
        w_qkv = jax.random.normal(ks[1], (D, 3 * D), dtype=jnp.float32) * 0.02
        b_qkv = jnp.zeros((3 * D,), dtype=jnp.float32)
        w_proj = jax.random.normal(ks[2], (D, D), dtype=jnp.float32) * 0.02
        b_proj = jnp.zeros((D,), dtype=jnp.float32)
        return {'x': x, 'g_norm': g_norm, 'w_qkv': w_qkv, 'b_qkv': b_qkv, 'w_proj': w_proj, 'b_proj': b_proj}
    _L0_attn_all = _L0_attn_setup()
    _L0_attn_in = {k: v for k, v in _L0_attn_all.items() if k in ('g_norm', 'w_qkv', 'b_qkv', 'w_proj', 'b_proj')}
    del _L0_attn_all

    def _L0_xattn_setup():
        import jax, jax.numpy as jnp
        import numpy as np
        DIM = 128
        HEADS = 16
        DIM_HEAD = 64
        INNER = HEADS * DIM_HEAD
        EPS = 1e-05

        def layernorm(x, w, b):
            mu = jnp.mean(x, axis=-1, keepdims=True)
            var = jnp.mean(jnp.square(x - mu), axis=-1, keepdims=True)
            return (x - mu) * jax.lax.rsqrt(var + EPS) * w + b
        key = jax.random.key(seed)
        ks = jax.random.split(key, 9)
        b, n1, n2 = (4, 512, 32)
        x = jax.random.normal(ks[0], (b, n1, DIM), dtype=jnp.float32)
        latents = jax.random.normal(ks[1], (b, n2, DIM), dtype=jnp.float32)
        shift = jax.random.normal(ks[2], (b, HEADS), dtype=jnp.float32)
        scale = jax.random.normal(ks[3], (b, HEADS), dtype=jnp.float32)
        s = 1.0 / np.sqrt(DIM)
        Wq = jax.random.normal(ks[4], (DIM, INNER), dtype=jnp.float32) * s
        Wkv = jax.random.normal(ks[5], (DIM, 2 * INNER), dtype=jnp.float32) * s
        Wout = jax.random.normal(ks[6], (INNER, DIM), dtype=jnp.float32) * (1.0 / np.sqrt(INNER))
        ln1_w = jnp.ones((DIM,), jnp.float32)
        ln1_b = jnp.zeros((DIM,), jnp.float32)
        ln2_w = jnp.ones((DIM,), jnp.float32)
        ln2_b = jnp.zeros((DIM,), jnp.float32)
        return {'x': x, 'latents': latents, 'shift': shift, 'scale': scale, 'ln1_w': ln1_w, 'ln1_b': ln1_b, 'ln2_w': ln2_w, 'ln2_b': ln2_b, 'Wq': Wq, 'Wkv': Wkv, 'Wout': Wout}
    _L0_xattn_all = _L0_xattn_setup()
    _L0_xattn_in = {k: v for k, v in _L0_xattn_all.items() if k in ('ln1_w', 'ln1_b', 'ln2_w', 'ln2_b', 'Wq', 'Wkv', 'Wout')}
    del _L0_xattn_all

    def _L0_ffn_setup():
        import jax, jax.numpy as jnp
        import numpy as np
        H = 8
        KD = 128
        TOPK = 8
        NUM_KEYS = 32
        N_EXPERTS = NUM_KEYS * NUM_KEYS
        N_DIM = 128
        BN_EPS = 1e-05

        def gelu_new(x):
            c = jnp.sqrt(jnp.asarray(2.0 / jnp.pi, x.dtype))
            return 0.5 * x * (1.0 + jnp.tanh(c * (x + 0.044715 * x * x * x)))
        key = jax.random.key(seed)
        ks = jax.random.split(key, 5)
        b, s = (2, 128)
        x = jax.random.normal(ks[0], (b, s, N_DIM), dtype=jnp.float32)
        w_q = jax.random.normal(ks[1], (N_DIM, 2 * H * KD), dtype=jnp.float32) * 0.02
        bn_gamma = jnp.ones((2 * H * KD,), dtype=jnp.float32)
        bn_beta = jnp.zeros((2 * H * KD,), dtype=jnp.float32)
        keys = jax.random.normal(ks[2], (H, NUM_KEYS, 2, KD), dtype=jnp.float32) * 0.02
        down_embed = jax.random.normal(ks[3], (N_EXPERTS, N_DIM), dtype=jnp.float32) * 0.02
        up_embed = jax.random.normal(ks[4], (N_EXPERTS, N_DIM), dtype=jnp.float32) * 0.02
        return {'x': x, 'w_q': w_q, 'bn_gamma': bn_gamma, 'bn_beta': bn_beta, 'keys': keys, 'down_embed': down_embed, 'up_embed': up_embed}
    _L0_ffn_all = _L0_ffn_setup()
    _L0_ffn_in = {k: v for k, v in _L0_ffn_all.items() if k in ('w_q', 'bn_gamma', 'bn_beta', 'keys', 'down_embed', 'up_embed')}
    del _L0_ffn_all
    return {'x': x, 'ctx_1024': ctx_1024, 'fside_Bx16_0': fside_Bx16_0, 'L0_attn_g_norm': _L0_attn_in['g_norm'], 'L0_attn_w_qkv': _L0_attn_in['w_qkv'], 'L0_attn_b_qkv': _L0_attn_in['b_qkv'], 'L0_attn_w_proj': _L0_attn_in['w_proj'], 'L0_attn_b_proj': _L0_attn_in['b_proj'], 'L0_xattn_ln1_w': _L0_xattn_in['ln1_w'], 'L0_xattn_ln1_b': _L0_xattn_in['ln1_b'], 'L0_xattn_ln2_w': _L0_xattn_in['ln2_w'], 'L0_xattn_ln2_b': _L0_xattn_in['ln2_b'], 'L0_xattn_Wq': _L0_xattn_in['Wq'], 'L0_xattn_Wkv': _L0_xattn_in['Wkv'], 'L0_xattn_Wout': _L0_xattn_in['Wout'], 'L0_ffn_w_q': _L0_ffn_in['w_q'], 'L0_ffn_bn_gamma': _L0_ffn_in['bn_gamma'], 'L0_ffn_bn_beta': _L0_ffn_in['bn_beta'], 'L0_ffn_keys': _L0_ffn_in['keys'], 'L0_ffn_down_embed': _L0_ffn_in['down_embed'], 'L0_ffn_up_embed': _L0_ffn_in['up_embed']}

def reference(x, ctx_1024, fside_Bx16_0, L0_attn_g_norm, L0_attn_w_qkv, L0_attn_b_qkv, L0_attn_w_proj, L0_attn_b_proj, L0_xattn_ln1_w, L0_xattn_ln1_b, L0_xattn_ln2_w, L0_xattn_ln2_b, L0_xattn_Wq, L0_xattn_Wkv, L0_xattn_Wout, L0_ffn_w_q, L0_ffn_bn_gamma, L0_ffn_bn_beta, L0_ffn_keys, L0_ffn_down_embed, L0_ffn_up_embed):
    import jax
    import jax.numpy as jnp

    def _L0_attn_ref(x, g_norm, w_qkv, b_qkv, w_proj, b_proj):
        import jax, jax.numpy as jnp
        import numpy as np
        EPS = 1e-06
        LN3 = 1.0986122886681098
        ROPE_BASE = 10000.0

        def exact_rmsnorm(x, g):
            ms = jnp.mean(jnp.square(x), axis=-1, keepdims=True)
            return x * jax.lax.rsqrt(ms + EPS) * g

        def ternary_rope(t):
            S, D = (t.shape[-2], t.shape[-1])
            half = D // 2
            inv_freq = 1.0 / ROPE_BASE ** (jnp.arange(half, dtype=jnp.float32) / half)
            ang = jnp.arange(S, dtype=jnp.float32)[:, None] * inv_freq[None, :]
            cos = jnp.round(jnp.cos(ang))
            sin = jnp.round(jnp.sin(ang))
            cos = jnp.concatenate([cos, cos], axis=-1)
            sin = jnp.concatenate([sin, sin], axis=-1)
            rot = jnp.concatenate([-t[..., half:], t[..., :half]], axis=-1)
            return t * cos + rot * sin

        def ternary_softmax(x, axis=-1):
            return jax.nn.softmax(x * LN3, axis=axis)
        D = x.shape[-1]
        scale = 1.0 / jnp.sqrt(jnp.float32(D))
        residual = x
        h = exact_rmsnorm(x, g_norm)
        qkv = h @ w_qkv + b_qkv
        q, k, v = jnp.split(qkv, 3, axis=-1)
        q = ternary_rope(q)
        k = ternary_rope(k)
        scores = jnp.einsum('bsd,btd->bst', q, k) * scale
        attn = ternary_softmax(scores, axis=-1)
        o = jnp.einsum('bst,btd->bsd', attn, v)
        return o @ w_proj + b_proj + residual

    def _L0_xattn_ref(x, latents, shift, scale, ln1_w, ln1_b, ln2_w, ln2_b, Wq, Wkv, Wout):
        import jax, jax.numpy as jnp
        import numpy as np
        DIM = 128
        HEADS = 16
        DIM_HEAD = 64
        INNER = HEADS * DIM_HEAD
        EPS = 1e-05

        def layernorm(x, w, b):
            mu = jnp.mean(x, axis=-1, keepdims=True)
            var = jnp.mean(jnp.square(x - mu), axis=-1, keepdims=True)
            return (x - mu) * jax.lax.rsqrt(var + EPS) * w + b
        b = x.shape[0]
        xn = layernorm(x, ln1_w, ln1_b)
        ln = layernorm(latents, ln2_w, ln2_b)
        q = ln @ Wq
        kv = xn @ Wkv
        k, v = jnp.split(kv, 2, axis=-1)
        q = q.reshape(b, -1, HEADS, DIM_HEAD)
        k = k.reshape(b, -1, HEADS, DIM_HEAD)
        v = v.reshape(b, -1, HEADS, DIM_HEAD)
        q = q * (1.0 + scale[:, None, :, None]) + shift[:, None, :, None]
        attn_scale = DIM_HEAD ** (-0.5)
        qk = jnp.einsum('bihd,bjhd->bhij', q.astype(jnp.float32), k.astype(jnp.float32)) * attn_scale
        attn = jax.nn.softmax(qk, axis=-1).astype(v.dtype)
        out = jnp.einsum('bhij,bjhd->bihd', attn, v)
        out = out.reshape(b, -1, INNER)
        return out @ Wout

    def _L0_ffn_ref(x, w_q, bn_gamma, bn_beta, keys, down_embed, up_embed):
        import jax, jax.numpy as jnp
        import numpy as np
        H = 8
        KD = 128
        TOPK = 8
        NUM_KEYS = 32
        N_EXPERTS = NUM_KEYS * NUM_KEYS
        N_DIM = 128
        BN_EPS = 1e-05

        def gelu_new(x):
            c = jnp.sqrt(jnp.asarray(2.0 / jnp.pi, x.dtype))
            return 0.5 * x * (1.0 + jnp.tanh(c * (x + 0.044715 * x * x * x)))
        b, n, d = x.shape
        q = jnp.einsum('bnd,de->bne', x, w_q)
        mean = jnp.mean(q, axis=(0, 1))
        var = jnp.var(q, axis=(0, 1))
        q = (q - mean) * jax.lax.rsqrt(var + BN_EPS) * bn_gamma + bn_beta
        q = q.reshape(b, n, 2, H, KD).transpose(2, 0, 1, 3, 4)
        sim = jnp.einsum('pbnhd,hkpd->pbnhk', q, keys)
        sx, ix = jax.lax.top_k(sim[0], TOPK)
        sy, iy = jax.lax.top_k(sim[1], TOPK)
        all_scores = (sx[..., :, None] + sy[..., None, :]).reshape(b, n, H, TOPK * TOPK)
        all_indices = (ix[..., :, None] * NUM_KEYS + iy[..., None, :]).reshape(b, n, H, TOPK * TOPK)
        scores, pk = jax.lax.top_k(all_scores, TOPK)
        indices = jnp.take_along_axis(all_indices, pk, axis=-1)
        wd = down_embed[indices]
        wu = up_embed[indices]
        h = jnp.einsum('bnd,bnhkd->bnhk', x, wd)
        h = gelu_new(h)
        h = jax.nn.softmax(scores, axis=-1) * h
        out = jnp.einsum('bnhk,bnhkd->bnd', h, wu)
        return out
    x = _layernorm(x + _L0_attn_ref(x, L0_attn_g_norm, L0_attn_w_qkv, L0_attn_b_qkv, L0_attn_w_proj, L0_attn_b_proj), axis=-1)
    x = _layernorm(x + _L0_xattn_ref(ctx_1024, x, fside_Bx16_0, fside_Bx16_0, L0_xattn_ln1_w, L0_xattn_ln1_b, L0_xattn_ln2_w, L0_xattn_ln2_b, L0_xattn_Wq, L0_xattn_Wkv, L0_xattn_Wout), axis=-1)
    x = _layernorm(x + _L0_ffn_ref(x, L0_ffn_w_q, L0_ffn_bn_gamma, L0_ffn_bn_beta, L0_ffn_keys, L0_ffn_down_embed, L0_ffn_up_embed), axis=-1)
    return x

_drawn_inputs = setup_inputs


def setup_inputs(seed=0):
    import zlib

    import numpy as np

    out = dict(_drawn_inputs(seed))
    spreads = {'L0_attn_g_norm': (1.0, 0.6),
     'L0_attn_b_qkv': (0.0, 0.767),
     'L0_attn_b_proj': (0.0, 0.1),
     'L0_xattn_ln1_w': (1.0, 0.2),
     'L0_xattn_ln1_b': (0.0, 0.1),
     'L0_xattn_ln2_w': (1.0, 0.2),
     'L0_xattn_ln2_b': (0.0, 0.314),
     'L0_ffn_bn_gamma': (1.0, 0.6),
     'L0_ffn_bn_beta': (0.0, 0.8)}
    factors = {'L0_attn_w_qkv': 8.0,
     'L0_attn_w_proj': 4.821,
     'L0_ffn_w_q': 8.0,
     'L0_ffn_keys': 8.0,
     'L0_ffn_down_embed': 8.0,
     'L0_ffn_up_embed': 8.0}
    for name, (base, spread) in spreads.items():
        noise = np.random.default_rng([zlib.crc32(name.encode()), seed]).standard_normal(out[name].shape)
        drawn = base * np.exp(spread * noise) if base else spread * noise
        out[name] = jnp.asarray(drawn.astype(out[name].dtype))
    for name, factor in factors.items():
        out[name] = (out[name] * factor).astype(out[name].dtype)
    return out
```

```python
from contextlib import ExitStack

import concourse.bass as bass
from concourse import mybir

F32 = mybir.dt.float32
F16 = mybir.dt.float16
BF16 = mybir.dt.bfloat16
U32 = mybir.dt.uint32
ALU = mybir.AluOpType
ACT = mybir.ActivationFunctionType
AX_X = mybir.AxisListType.X

P = 128
B, S, D = 16, 100, 128
NT = B * S
G = 4
NG = B // G
T = 1444
TF = T // P
TR = T - TF * P
NTILE = TF + 1
H, DH = 16, 64
HQ = H * S
HALF = HQ // 2
CH = HALF // 2
NM = (HQ + P - 1) // P
LN3 = 1.0986122886681098
ATT_SCALE = LN3 / float(D) ** 0.5
EPS_RMS, EPS = 1e-6, 1e-5
HEADROOM = 6.0
FH, KEYS, KD, NE = 8, 32, 128, 1024
NB = 2 * FH


def front(nc, a, m, ps):
    with ExitStack() as ctx:
        def sb(name, shape, dt=F32):
            return ctx.enter_context(nc.sbuf_tensor(name, shape, dt))

        def sem(name):
            return ctx.enter_context(nc.semaphore(name))

        x_tok = sb("x_tok", [S, B, D])
        w_qkv = sb("w_qkv", [D, 3 * D])
        w_swap = sb("w_swap", [D, 2 * D])
        b_qkv = sb("b_qkv", [D, 3])
        b_swap = sb("b_swap", [D, 2])
        g_col = sb("g_col", [D, 1])
        w_proj = sb("w_proj", [D, D])
        bp_row = sb("bp_row", [S, D])
        cos_t = sb("cos_t", [D, S])
        sin_t = sb("sin_t", [D, S])
        w2_col = sb("w2_col", [D, 1])
        b2_col = sb("b2_col", [D, 1])
        sq = sb("sq", [S, B, D])
        ms = sb("ms", [S, B])
        rr = sb("rr", [S, B])
        xr = sb("xr", [S, B, D])
        x2b = sb("x2b", [S, B, D])
        hT = sb("hT", [D, NT])
        rot_a = sb("rot_a", [D, G, S])
        rot_b = sb("rot_b", [D, G, S])
        qT = sb("qT", [D, NT])
        kT = sb("kT", [D, NT])
        v_sb = sb("v_sb", [S, B, D])
        mx = sb("mx", [S, B])
        nb = sb("nb", [S, B])
        rs = sb("rs", [S, B])
        rc = sb("rc", [S, B])
        prob = sb("prob", [S, B, S])
        probT = sb("probT", [S, B, S])
        oT = sb("oT", [D, NT])
        z = sb("z", [S, B, D])
        bst = sb("bst", [S, B, 6])
        mv = sb("mv", [S, B, 2])
        ve = sb("ve", [S, B])
        rstd = sb("rstd", [S, B])
        wq_t = sb("wq_t", [DH, H, D])
        wk_t = sb("wk_t", [DH, H, D])
        wv_t = sb("wv_t", [DH, H, D])
        wout = sb("wout", [DH, H, D])
        wk_f = sb("wk_f", [DH, H, D])
        wv_f = sb("wv_f", [DH, H, D])
        wtmp = sb("wtmp", [DH, H, D])
        vb = sb("vb", [DH, H])
        w1_row = sb("w1_row", [DH, D])
        b1_row = sb("b1_row", [DH, D])
        ones_c = sb("ones_c", [DH, 1])
        side = sb("side", [D, B, H])
        kbar = sb("kbar", [D, H])

        ident, ident16, nhalf = m["ident"], m["ident16"], m["nhalf"]
        qa, w2h, sc1, kb, x1, lnT = m["qa"], m["w2h"], m["sc1"], m["kb"], m["x1"], m["lnT"]

        ld_x, ld_att, ld_fold, ld_side = sem("ld_x"), sem("ld_att"), sem("ld_fold"), sem("ld_side")
        ident_done, const_done = sem("ident_done"), sem("const_done")
        sq_done, ms_done, rr_done, xr_done = sem("sq_done"), sem("ms_done"), sem("rr_done"), sem("xr_done")
        x2b_done = sem("x2b_done")
        hT_ps, hT_done = sem("hT_ps"), sem("hT_done")
        qk_ps, rot_done, qk_done = sem("qk_ps"), sem("rot_done"), sem("qk_done")
        v_ps, v_done = sem("v_ps"), sem("v_done")
        sc_ps, mx_done, nb_done, exp_done = sem("sc_ps"), sem("mx_done"), sem("nb_done"), sem("exp_done")
        rc_done, prob_done, pT_ps, pT_done = sem("rc_done"), sem("prob_done"), sem("pT_ps"), sem("pT_done")
        o_ps, o_done, y_ps, z_done = sem("o_ps"), sem("o_done"), sem("y_ps"), sem("z_done")
        st_done, ag_done, ve_done = sem("st_done"), sem("ag_done"), sem("ve_done")
        rstd_done, norm_done = sem("rstd_done"), sem("norm_done")
        ln_ps, ln_done = sem("ln_ps"), sem("ln_done")
        kmul_done, kfold_done, vmul_done, vfold_done = sem("kmul_done"), sem("kfold_done"), sem("vmul_done"), sem("vfold_done")
        qa_ps, qa_done, kb_ps, kbar_done, w2_ps, w2_done = (sem(n) for n in ("qa_ps", "qa_done", "kb_ps", "kbar_done", "w2_ps", "w2_done"))
        side_done = sem("side_done")

        block = ctx.enter_context(nc.Block())

        def bank(k, parts, shape):
            names = " ".join("abc"[: len(shape)])
            n = 1
            for s in shape:
                n *= s
            v = ps[0:parts, k, 0:n]
            if len(shape) == 1:
                return v
            return v.rearrange(f"p ({names}) -> p {names}", **dict(zip("abc", shape)))

        @block.sync
        def _(sp):
            sp.dma_start(x_tok[:, :, :], a["x"].rearrange("b s d -> s b d")).then_inc(ld_x, 16)
            sp.dma_start(w_qkv[:, :], a["L0_attn_w_qkv"]).then_inc(ld_att, 16)
            for n in range(2):
                for half in range(2):
                    src = n * D + (1 - half) * (D // 2)
                    dst = n * D + half * (D // 2)
                    sp.dma_start(w_swap[:, dst:dst + D // 2],
                                 a["L0_attn_w_qkv"][:, src:src + D // 2]).then_inc(ld_att, 16)
                    sp.dma_start(b_swap[half * (D // 2):(half + 1) * (D // 2), n:n + 1],
                                 a["L0_attn_b_qkv"][src:src + D // 2, :]).then_inc(ld_att, 16)
            for n in range(3):
                sp.dma_start(b_qkv[:, n:n + 1], a["L0_attn_b_qkv"][n * D:(n + 1) * D, :]).then_inc(ld_att, 16)
            sp.dma_start(g_col[:, :], a["L0_attn_g_norm"]).then_inc(ld_att, 16)
            sp.dma_start(cos_t[:, :], a["cos_t"]).then_inc(ld_att, 16)
            sp.dma_start(sin_t[:, :], a["sin_t"]).then_inc(ld_att, 16)
            sp.dma_start(w_proj[:, :], a["L0_attn_w_proj"]).then_inc(ld_att, 16)
            sp.dma_start(bp_row[:, :], a["L0_attn_b_proj"].rearrange("d a -> a d").to_broadcast([S, D])).then_inc(ld_att, 16)
            sp.dma_start(w2_col[:, :], a["L0_xattn_ln2_w"]).then_inc(ld_att, 16)
            sp.dma_start(b2_col[:, :], a["L0_xattn_ln2_b"]).then_inc(ld_att, 16)
            ld = [(wk_t, a["wk_t"].rearrange("(h c) d -> c h d", c=DH)),
                  (wq_t, a["wq_t"].rearrange("(h c) d -> c h d", c=DH)),
                  (wv_t, a["wv_t"].rearrange("(h c) d -> c h d", c=DH)),
                  (wout, a["L0_xattn_Wout"].rearrange("(h c) n -> c h n", c=DH))]
            sp.dma_start(w1_row[:, :], a["L0_xattn_ln1_w"].rearrange("d a -> a d").to_broadcast([DH, D])).then_inc(ld_fold, 16)
            sp.dma_start(b1_row[:, :], a["L0_xattn_ln1_b"].rearrange("d a -> a d").to_broadcast([DH, D])).then_inc(ld_fold, 16)
            for dst, src in ld:
                sp.dma_start(dst[:, :, :], src).then_inc(ld_fold, 16)
            sp.dma_start(side[:, :, :].rearrange("p b h -> p (b h)"),
                         a["fside_Bx16_0"].rearrange("b h -> (b h)").rearrange("(a n) -> a n", a=1).to_broadcast([D, B * H])).then_inc(ld_side, 16)

        LD_ATT, LD_FOLD = 16 * 19, 16 * 6

        @block.gpsimd
        def _(pool):
            pool.memset(ident[:, :], 0.0).then_inc(ident_done, 1)
            pool.memset(ident16[:, :], 0.0).then_inc(ident_done, 1)
            pool.memset(nhalf[:, :], -0.5).then_inc(ident_done, 1)
            pool.memset(ones_c[:, :], 1.0).then_inc(ident_done, 1)
            pool.wait_ge(ident_done, 4)
            for t in (ident, ident16):
                pool.affine_select(out=t[:, :], in_=t[:, :], compare_op=ALU.not_equal, fill=1.0, base=0,
                                   pattern=[[-1, P]], channel_multiplier=1).then_inc(const_done, 1)
            pool.wait_ge(ms_done, 1)
            pool.tensor_tensor(out=rr[:, :], in0=ms[:, :], in1=nhalf[0:S, 0:B], op=ALU.pow).then_inc(rr_done, 1)
            pool.wait_ge(ld_fold, LD_FOLD)
            pool.tensor_tensor(out=wtmp[:, :, :], in0=wk_t[:, :, :],
                               in1=w1_row[:, :].rearrange("c (a d) -> c a d", a=1).to_broadcast([DH, H, D]), op=ALU.mult).then_inc(kmul_done, 1)
            pool.wait_ge(kmul_done, 1)
            pool.memset(wk_f[:, :, 0:1], 0.0).then_inc(kfold_done, 1)
            pool.tensor_tensor(out=wk_f[:, :, 1:D], in0=wtmp[:, :, 1:D],
                               in1=wtmp[:, :, 0:1].to_broadcast([DH, H, D - 1]), op=ALU.subtract).then_inc(kfold_done, 1)
            for c in range(NG):
                for k in range(2):
                    pool.wait_ge(ve_done, 2 * c + k + 1)
                    pool.tensor_tensor(out=rstd[:, c * G:(c + 1) * G], in0=ve[:, c * G:(c + 1) * G],
                                       in1=nhalf[0:S, 0:G], op=ALU.pow).then_inc(rstd_done, 1)

        @block.scalar
        def _(act):
            for k in range(NG):
                act.wait_ge(qa_ps, k + 1)
                act.activation(qa[:, 4 * k:4 * k + 4, :], bank(4 + k, D, (4, D)), ACT.Copy, scale=DH ** -0.5).then_inc(qa_done, 1)
            act.wait_ge(kb_ps, 1)
            act.activation(kbar[:, :], bank(3, D, (H,)), ACT.Copy, scale=DH ** -0.5).then_inc(kbar_done, 1)
            for c in range(NG):
                act.wait_ge(v_ps, c + 1)
                act.activation(v_sb[:, c * G:(c + 1) * G, :], bank(c, S, (G, D)), ACT.Copy).then_inc(v_done, 1)
            for c in range(NG):
                act.wait_ge(nb_done, c + 1)
                for j in range(G):
                    b = c * G + j
                    act.activation(prob[:, b, :], bank(c, S, (G, S))[:, j, :], ACT.Exp, bias=nb[:, b:b + 1],
                                   scale=ATT_SCALE, accum_out=rs[:, b:b + 1]).then_inc(exp_done, 1)
            for c in range(NG):
                act.wait_ge(pT_ps, c + 1)
                act.activation(probT[:, c * G:(c + 1) * G, :], bank(4 + c, S, (G, S)), ACT.Copy).then_inc(pT_done, 1)
                act.wait_ge(o_ps, c + 1)
                act.activation(oT[:, c * G * S:(c + 1) * G * S], bank(c, D, (G * S,)), ACT.Identity,
                               bias=b_qkv[:, 2:3]).then_inc(o_done, 1)
            for k in range(NG):
                act.wait_ge(w2_ps, k + 1)
                act.activation(w2h[:, 4 * k:4 * k + 4, 0:D], bank(k, D, (4, D)), ACT.Copy).then_inc(w2_done, 1)

        @block.vector
        def _(dve):
            dve.wait_ge(ld_x, 16)
            dve.tensor_tensor(out=sq[:, :, :], in0=x_tok[:, :, :], in1=x_tok[:, :, :], op=ALU.mult).then_inc(sq_done, 1)
            dve.wait_ge(sq_done, 1)
            dve.tensor_reduce(ms[:, :], sq[:, :, :], AX_X, ALU.add).then_inc(sq_done, 1)
            dve.wait_ge(sq_done, 2)
            dve.tensor_scalar(ms[:, :], ms[:, :], 1.0 / D, EPS_RMS, ALU.mult, ALU.add).then_inc(ms_done, 1)
            dve.wait_ge(ld_att, LD_ATT)
            dve.scalar_tensor_tensor(out=x2b[:, :, :], in0=x_tok[:, :, :], scalar=2.0,
                                     in1=bp_row[:, :].rearrange("s (a d) -> s a d", a=1).to_broadcast([S, B, D]),
                                     op0=ALU.mult, op1=ALU.add).then_inc(x2b_done, 1)
            dve.wait_ge(rr_done, 1)
            dve.tensor_tensor(out=xr[:, :, :], in0=x_tok[:, :, :],
                              in1=rr[:, :].rearrange("s (b a) -> s b a", a=1).to_broadcast([S, B, D]), op=ALU.mult).then_inc(xr_done, 1)
            for c in range(NG):
                dve.wait_ge(hT_ps, c + 1)
                dve.tensor_scalar(hT[:, c * G * S:(c + 1) * G * S], bank(c, D, (G * S,)), g_col[:, 0:1], None, ALU.mult).then_inc(hT_done, 1)
            dve.wait_ge(ld_fold, LD_FOLD)
            dve.tensor_tensor(out=wv_f[:, :, :], in0=wv_t[:, :, :],
                              in1=b1_row[:, :].rearrange("c (a d) -> c a d", a=1).to_broadcast([DH, H, D]), op=ALU.mult).then_inc(vmul_done, 1)
            dve.wait_ge(vmul_done, 1)
            dve.tensor_reduce(vb[:, :], wv_f[:, :, :], AX_X, ALU.add).then_inc(vmul_done, 1)
            dve.tensor_tensor(out=wv_t[:, :, :], in0=wv_t[:, :, :],
                              in1=w1_row[:, :].rearrange("c (a d) -> c a d", a=1).to_broadcast([DH, H, D]), op=ALU.mult).then_inc(vmul_done, 1)
            dve.wait_ge(vmul_done, 3)
            dve.tensor_tensor(out=wv_f[:, :, 1:D], in0=wv_t[:, :, 1:D],
                              in1=wv_t[:, :, 0:1].to_broadcast([DH, H, D - 1]), op=ALU.subtract).then_inc(vfold_done, 1)
            dve.tensor_copy(wv_f[:, :, 0:1], vb[:, :].rearrange("c (h a) -> c h a", a=1)).then_inc(vfold_done, 1)
            dve.memset(w2h[:, :, D:D + 1], 0.0).then_inc(vfold_done, 1)
            dve.wait_ge(vfold_done, 3)
            dve.memset(w2h[0:1, :, D:D + 1], 1.0).then_inc(vfold_done, 1)
            for c in range(NG):
                for n, dst in enumerate((qT, kT)):
                    dve.wait_ge(qk_ps, 2 * c + n + 1)
                    if c or n:
                        dve.wait_ge(qk_done, 2 * c + n)
                    dve.scalar_tensor_tensor(out=rot_a[:, :, :], in0=bank(4 + 2 * n, D, (G, S)), scalar=b_qkv[:, n:n + 1],
                                             in1=cos_t[:, :].rearrange("d (a s) -> d a s", a=1).to_broadcast([D, G, S]),
                                             op0=ALU.add, op1=ALU.mult).then_inc(rot_done, 1)
                    dve.scalar_tensor_tensor(out=rot_b[:, :, :], in0=bank(5 + 2 * n, D, (G, S)), scalar=b_swap[:, n:n + 1],
                                             in1=sin_t[:, :].rearrange("d (a s) -> d a s", a=1).to_broadcast([D, G, S]),
                                             op0=ALU.add, op1=ALU.mult).then_inc(rot_done, 1)
                    dve.wait_ge(rot_done, 4 * c + 2 * n + 2)
                    dve.tensor_tensor(out=dst[:, c * G * S:(c + 1) * G * S].rearrange("d (a s) -> d a s", a=G),
                                      in0=rot_a[:, :, :], in1=rot_b[:, :, :], op=ALU.add).then_inc(qk_done, 1)
            for c in range(NG):
                cs = slice(c * G, (c + 1) * G)
                dve.wait_ge(sc_ps, c + 1)
                dve.tensor_reduce(mx[:, cs], bank(c, S, (G, S)), AX_X, ALU.max).then_inc(mx_done, 1)
                dve.wait_ge(mx_done, c + 1)
                dve.tensor_scalar(nb[:, cs], mx[:, cs], -ATT_SCALE, None, ALU.mult).then_inc(nb_done, 1)
            for c in range(NG):
                cs = slice(c * G, (c + 1) * G)
                dve.wait_ge(exp_done, (c + 1) * G)
                dve.reciprocal(rc[:, cs], rs[:, cs]).then_inc(rc_done, 1)
                dve.wait_ge(rc_done, c + 1)
                dve.tensor_tensor(out=prob[:, cs, :], in0=prob[:, cs, :],
                                  in1=rc[:, cs].rearrange("s (b a) -> s b a", a=1).to_broadcast([S, G, S]),
                                  op=ALU.mult).then_inc(prob_done, 1)
            for c in range(NG):
                cs = slice(c * G, (c + 1) * G)
                dve.wait_ge(y_ps, c + 1)
                dve.tensor_tensor(out=z[:, cs, :], in0=bank(4 + c, S, (G, D)), in1=x2b[:, cs, :], op=ALU.add).then_inc(z_done, 1)
                dve.wait_ge(z_done, c + 1)
                for k, (src, dst) in enumerate(((z, x1), (x1, sq))):
                    n = 2 * c + k
                    if n:
                        dve.wait_ge(norm_done, G * n)
                    for j in range(G):
                        dve.bn_stats(bst[:, c * G + j, :], src[:, c * G + j, :]).then_inc(st_done, 1)
                    dve.wait_ge(st_done, G * (n + 1))
                    for j in range(G):
                        dve.bn_aggr(mv[:, c * G + j, :], bst[:, c * G + j, :]).then_inc(ag_done, 1)
                    dve.wait_ge(ag_done, G * (n + 1))
                    dve.tensor_scalar(ve[:, cs], mv[:, cs, 1], EPS, None, ALU.add).then_inc(ve_done, 1)
                    dve.wait_ge(rstd_done, n + 1)
                    for j in range(G):
                        b = c * G + j
                        dve.tensor_scalar(dst[:, b, :], src[:, b, :], mv[:, b, 0:1], rstd[:, b:b + 1],
                                          ALU.subtract, ALU.mult).then_inc(norm_done, 1)
                dve.wait_ge(ln_ps, c + 1)
                dve.tensor_scalar(lnT[:, c * G * S:(c + 1) * G * S], bank(c, D, (G * S,)), w2_col[:, 0:1], b2_col[:, 0:1],
                                  ALU.mult, ALU.add).then_inc(ln_done, 1)
            dve.wait_ge(ld_side, 16)
            dve.tensor_scalar(sc1[:, :, :], side[:, :, :], 1.0, None, ALU.add).then_inc(side_done, 1)
            dve.wait_ge(kbar_done, 1)
            dve.tensor_tensor(out=kb[:, :, :], in0=side[:, :, :],
                              in1=kbar[:, :].rearrange("d (a h) -> d a h", a=1).to_broadcast([D, B, H]), op=ALU.mult).then_inc(side_done, 1)

        @block.tensor
        def _(pe):
            pe.wait_ge(const_done, 2)
            pe.wait_ge(xr_done, 1)
            for c in range(NG):
                for j in range(G):
                    last = pe.transpose(bank(c, D, (G, S))[:, j, :], xr[:, c * G + j, :], ident[0:S, 0:S])
                last.then_inc(hT_ps, 1)
            pe.wait_ge(kfold_done, 2)
            for k in range(NG):
                for j in range(4):
                    last = pe.matmul(bank(4 + k, D, (4, D))[:, j, :], wq_t[:, 4 * k + j, :], wk_f[:, 4 * k + j, :], start=True, stop=True)
                last.then_inc(qa_ps, 1)
            pe.wait_ge(hT_done, NG)
            for h in range(H):
                last = pe.matmul(bank(3, D, (H,))[:, h:h + 1], wk_f[:, h, :], ones_c[:, 0:1], start=True, stop=True)
            last.then_inc(kb_ps, 1)
            for c in range(NG):
                if c == NG - 1:
                    pe.wait_ge(kbar_done, 1)
                for j in range(G):
                    b = c * G + j
                    last = pe.matmul(bank(c, S, (G, D))[:, j, :], hT[:, b * S:(b + 1) * S], w_qkv[:, 2 * D:3 * D], start=True, stop=True)
                last.then_inc(v_ps, 1)
            pe.wait_ge(qa_done, NG)
            for c in range(NG):
                for n in range(2):
                    if c:
                        pe.wait_ge(qk_done, 2 * (c - 1) + n + 1)
                    cols = slice(c * G * S, (c + 1) * G * S)
                    pe.matmul(bank(4 + 2 * n, D, (G * S,)), w_qkv[:, n * D:(n + 1) * D], hT[:, cols], start=True, stop=True)
                    pe.matmul(bank(5 + 2 * n, D, (G * S,)), w_swap[:, n * D:(n + 1) * D], hT[:, cols], start=True, stop=True).then_inc(qk_ps, 1)
            for c in range(NG):
                pe.wait_ge(qk_done, 2 * (c + 1))
                pe.wait_ge(v_done, c + 1)
                for j in range(G):
                    bs = slice((c * G + j) * S, (c * G + j + 1) * S)
                    last = pe.matmul(bank(c, S, (G, S))[:, j, :], qT[:, bs], kT[:, bs], start=True, stop=True)
                last.then_inc(sc_ps, 1)
            for c in range(NG):
                pe.wait_ge(prob_done, c + 1)
                for j in range(G):
                    last = pe.transpose(bank(4 + c, S, (G, S))[:, j, :], prob[:, c * G + j, :], ident[0:S, 0:S])
                last.then_inc(pT_ps, 1)
                pe.wait_ge(pT_done, c + 1)
                for j in range(G):
                    b = c * G + j
                    last = pe.matmul(bank(c, D, (G, S))[:, j, :], v_sb[:, b, :], probT[:, b, :], start=True, stop=True)
                last.then_inc(o_ps, 1)
                pe.wait_ge(o_done, c + 1)
                for j in range(G):
                    b = c * G + j
                    last = pe.matmul(bank(4 + c, S, (G, D))[:, j, :], oT[:, b * S:(b + 1) * S], w_proj[:, :], start=True, stop=True)
                last.then_inc(y_ps, 1)
            for c in range(NG):
                pe.wait_ge(norm_done, G * (2 * c + 2))
                for j in range(G):
                    last = pe.transpose(bank(c, D, (G, S))[:, j, :], sq[:, c * G + j, :], ident[0:S, 0:S])
                last.then_inc(ln_ps, 1)
            pe.wait_ge(vfold_done, 4)
            for k in range(NG):
                pe.wait_ge(ln_done, k + 1)
                for j in range(4):
                    last = pe.matmul(bank(k, D, (4, D))[:, j, :], wv_f[:, 4 * k + j, :], wout[:, 4 * k + j, :], start=True, stop=True)
                last.then_inc(w2_ps, 1)


class Batch:

    def __init__(self, i, off):
        self.i, self.off = i, off

    def val(self, coef, const):
        v = coef * self.off + const
        return v if self.i is None else self.i * (2 * coef) + v

    def next(self, n=1):
        return Batch(self.i, self.off + n)

    def is_last(self):
        return self.i is None and self.off == B - 1

    @property
    def par(self):
        return self.off % 2

    def index(self):
        return self.val(1, 0)


def over_batches(eng, body):
    body(Batch(None, 0), True, False)
    with eng.Fori(0, (B - 2) // 2) as i:
        body(Batch(i, 1), False, False)
        body(Batch(i, 2), False, False)
    body(Batch(None, B - 1), False, True)


def side_work(first, last):
    own = [("M", m, c) for m in range(7, NM) for c in range(3)]
    nxt = [("M", m, c) for m in range(7) for c in range(3)]
    w = {(u, n): [] for u in range(2) for n in range(NTILE)}
    if not last:
        for g in range(4):
            w[0, 1 + g // 2].append(("q", g))
        w[0, 9].append(("T", 0))
        w[0, 10].append(("T", 1))
        w[1, 0] += [("T", 2), ("T", 3)]
        for n, k in ((1, 3), (2, 3), (3, 3), (4, 3), (5, 3), (6, 3), (7, 3)):
            w[1, n] += [nxt.pop(0) for _ in range(k)]
        w[1, 8] += [("R", 0), ("R", 1)]
    if not first:
        for g in range(3):
            w[0, g + 3].append(("Y", 1, g))
    for n, k in ((0, 2), (1, 1), (2, 1), (3, 3), (4, 3), (5, 3), (6, 3), (7, 2)):
        w[0, n] += [own.pop(0) for _ in range(k)]
    w[0, 8] += [("R", 2), ("R", 3)]
    for g in range(3):
        w[1, 9 + g].append(("Y", 0, g))
    return w


START_WORK = ([("q", g) for g in range(4)] + [("T", j) for j in range(4)]
              + [("M", m, c) for m in range(7) for c in range(3)] + [("R", 0), ("R", 1)])
WORKS = 57
TAIL_WORK = [("Y", 1, g) for g in range(3)]


class Works:

    def __init__(self, bt, first, last, start=False, tail=False):
        self.bt, self.tail = bt, tail
        if start:
            self.base, self.base_dve, self.base_act = (0, 0), (0, 0), (0, 0)
            flat = [(None, w) for w in START_WORK]
        else:
            n = len(START_WORK)
            if first:
                self.base, self.base_dve = (0, n), (0, n - 4)
            else:
                self.base, self.base_dve = (WORKS, n - 3), (WORKS - 4, n - 7)
            self.base_act = (4, 4)
            if tail:
                lost = 4 + 4 + 21 + 2
                self.base = (WORKS, n - 3 - lost)
                self.base_dve = (WORKS - 4, n - 7 - (lost - 4))
                self.base_act = (4, 0)
                flat = [(None, w) for w in TAIL_WORK]
            else:
                plan = side_work(first, last)
                flat = [(k, w) for k in sorted(plan) for w in plan[k]]
        self.flat = flat

    def number(self, k):
        return self.bt.val(self.base[0], self.base[1] + k)

    def bank(self, k):
        c, n = self.base
        return (c * self.bt.off + n + k) % 2

    def is_act(self, k):
        return self.flat[k][1][0] == "T"

    def taken(self, k):
        acts = sum(self.is_act(j) for j in range(k + 1)) if k >= 0 else 0
        if k >= 0 and self.is_act(k):
            return self.bt.val(self.base_act[0], self.base_act[1] + acts)
        return self.bt.val(self.base_dve[0], self.base_dve[1] + k + 1 - acts)

    def at(self, key):
        return [(k, w) for k, (s, w) in enumerate(self.flat) if s == key]

    def find(self, work):
        return next(k for k, (_, w) in enumerate(self.flat) if w == work)


POOL_TILES = (1, 4, 7, 10)
MCUT = (0, 482, 963, T)
Y_HEADS = ((0, 1, 2), (3, 4, 5), (6, 7))


def lo_count(bt, u, n):
    pool = sum(k <= n for k in POOL_TILES)
    if n in POOL_TILES:
        return bt.val(2 * len(POOL_TILES), len(POOL_TILES) * u + pool)
    mine = NTILE - len(POOL_TILES)
    return bt.val(2 * mine, mine * u + (n + 1 - pool))


def tile_number(bt, u, n):
    return bt.val(2 * NTILE, NTILE * u + n)


def rows_of(n):
    return P if n < TF else TR


def cross(nc, a, m, ps):
    with ExitStack() as ctx:
        def sb(name, shape, dt=F32):
            return ctx.enter_context(nc.sbuf_tensor(name, shape, dt))

        def sem(name):
            return ctx.enter_context(nc.semaphore(name))

        ident16, nhalf = m["ident16"], m["nhalf"]
        qa, w2h, sc1, kb, x1, lnT, x2 = m["qa"], m["w2h"], m["sc1"], m["kb"], m["x1"], m["lnT"], m["x2"]
        raw = [sb(f"raw{i}", [P, NTILE, D]) for i in range(2)]
        cst = sb("cst", [P, NTILE, 6])
        cmv = [sb(f"cmv{i}", [P, NTILE, 2]) for i in range(2)]
        cve = sb("cve", [P, NTILE])
        crs = [sb(f"crs{i}", [P, NTILE]) for i in range(2)]
        xh = sb("xh", [P, NTILE, D])
        xa_hi = [sb(f"xa_hi{i}", [P, NTILE, D], F16) for i in range(2)]
        xa_lo = [sb(f"xa_lo{i}", [P, NTILE, D], F16) for i in range(2)]
        xT_hi = [sb(f"xT_hi{i}", [D, NTILE * P], F16) for i in range(2)]
        xT_lo = [sb(f"xT_lo{i}", [D, NTILE * P], F16) for i in range(2)]
        ln_cur, sc_cur, kb_cur = sb("ln_cur", [D, S]), sb("sc_cur", [D, H]), sb("kb_cur", [D, H])
        q32 = sb("q32", [D, HQ])
        q_hi = [sb(f"q_hi{i}", [D, HQ], F16) for i in range(2)]
        q_lo = [sb(f"q_lo{i}", [D, HQ], F16) for i in range(2)]
        mxp = sb("mxp", [P, NM, 3])
        nm = sb("nm", [P, NM], F16)
        e32 = [sb(f"e32_{i}", [P, 2, CH]) for i in range(3)]
        p_hi = [sb(f"p_hi{i}", [P, 2, CH], F16) for i in range(4)]
        p_lo = [sb(f"p_lo{i}", [P, 2, CH], F16) for i in range(4)]
        uT = [sb(f"uT{i}", [D, 2, CH]) for i in range(2)]
        ry = sb("ry", [S, H])
        acc = sb("acc", [S, D])
        yst, ymv, yve, yrs = sb("yst", [S, 6]), sb("ymv", [S, 2]), sb("yve", [S, 1]), sb("yrs", [S, 1])

        ctx_ld = [sem(f"ctx_ld{i}") for i in range(2)]
        init_done, ctx_stat, ctx_rstd, xh_done = sem("init_done"), sem("ctx_stat"), sem("ctx_rstd"), sem("xh_done")
        xa_done, cur_done, q_split = sem("xa_done"), sem("cur_done"), sem("q_split")
        work_rdy, work_dve, work_act, nm_done = sem("work_rdy"), sem("work_dve"), sem("work_act"), sem("nm_done")
        s_rdy, exp_done, lo_dve, lo_pool = sem("s_rdy"), sem("exp_done"), sem("lo_dve"), sem("lo_pool")
        pv_done, u_done, y_chain, y_norm, y_rstd = (sem(n) for n in ("pv_done", "u_done", "y_chain", "y_norm", "y_rstd"))

        pool_waited, dve_waited = sem("pool_waited"), sem("dve_waited")

        block = ctx.enter_context(nc.Block())

        def s_banks(n, rows):
            return ps[0:rows, 2 * (n % 2):2 * (n % 2) + 2, 0:CH]

        def wbank(w, k):
            return ps[:, 6 + w.bank(k), :]

        @block.sync
        def _(sp):
            def load(bt):
                src = a["ctx_1024"][bass.ds(bt.index(), 1), :, :].rearrange("a t d -> (a t) d")
                sp.dma_start(raw[bt.par][:, 0:TF, :],
                             src[0:TF * P, :].rearrange("(p j) d -> p j d", j=TF)).then_inc(ctx_ld[bt.par], 16)
                sp.dma_start(raw[bt.par][0:TR, TF, :], src[TF * P:T, :]).then_inc(ctx_ld[bt.par], 16)

            load(Batch(None, 0))
            load(Batch(None, 1))
            with sp.Fori(1, B // 2) as i:
                for off in range(2):
                    bt = Batch(i, off)
                    sp.wait_ge(xh_done, bt.val(1, -1))
                    load(bt)

        @block.gpsimd
        def _(pool):
            def current(bt):
                x = bt.index()
                pool.tensor_copy(ln_cur[:, :], lnT[:, bass.ds(bt.val(S, 0), S)])
                pool.tensor_copy(sc_cur[:, :], sc1[:, bass.ds(x, 1), :].rearrange("d a h -> d (a h)"))
                pool.tensor_copy(kb_cur[:, :], kb[:, bass.ds(x, 1), :].rearrange("d a h -> d (a h)")).then_inc(cur_done, 1)

            def rstd_ctx(bt):
                pool.wait_ge(ctx_stat, bt.val(3, 3))
                if bt.off >= 2:
                    pool.wait_ge(xh_done, bt.val(1, -1))
                pool.tensor_tensor(out=crs[bt.par][:, :], in0=cve[:, :], in1=nhalf[:, 0:NTILE], op=ALU.pow).then_inc(ctx_rstd, 1)

            def split_q(bt, w, g):
                cols = slice(g * CH, (g + 1) * CH)
                pool.wait_ge(work_dve, w.taken(w.find(("q", g))))
                if bt.off >= 2:
                    pool.wait_ge(s_rdy, bt.val(2 * NTILE, -2 * NTILE))
                pool.sem_inc(pool_waited, 1)
                pool.tensor_copy(q_hi[bt.par][:, cols], q32[:, cols]).then_inc(q_split, 1)
                pool.wait_ge(q_split, bt.val(8, 2 * g + 1))
                pool.tensor_tensor(out=q_lo[bt.par][:, cols], in0=q32[:, cols], in1=q_hi[bt.par][:, cols],
                                   op=ALU.subtract).then_inc(q_split, 1)

            def split_hi(bt):
                pool.wait_ge(xh_done, bt.val(1, 1))
                if bt.off >= 2:
                    pool.wait_ge(pv_done, bt.val(2 * NTILE, -2 * NTILE))
                pool.sem_inc(pool_waited, 1)
                pool.tensor_copy(xa_hi[bt.par][:, :, :], xh[:, :, :]).then_inc(xa_done, 1)

            def split_lo(bt):
                pool.wait_ge(xa_done, bt.val(2, 1))
                pool.tensor_tensor(out=xa_lo[bt.par][:, :, :], in0=xh[:, :, :], in1=xa_hi[bt.par][:, :, :],
                                   op=ALU.subtract).then_inc(xa_done, 1)

            def low_half(bt, u, n):
                t, r = NTILE * u + n, rows_of(n)
                pool.wait_ge(exp_done, bt.val(4 * NTILE, 2 * t + 2))
                if bt.off or t >= 4:
                    pool.wait_ge(pv_done, bt.val(2 * NTILE, t - 3))
                pool.tensor_tensor(out=p_lo[t % 4][0:r, :, :], in0=e32[t % 3][0:r, :, :], in1=p_hi[t % 4][0:r, :, :],
                                   op=ALU.subtract).then_inc(lo_pool, 1)

            def y_rstd_pow(bt):
                pool.wait_ge(y_norm, bt.val(4, 3))
                pool.tensor_tensor(out=yrs[:, :], in0=yve[:, :], in1=nhalf[0:S, 0:1], op=ALU.pow).then_inc(y_rstd, 1)

            def one_batch(bt, first, last):
                w, nx = Works(bt, first, last), bt.next()
                if not last:
                    current(nx)
                low_half(bt, 0, 1)
                if not last:
                    split_q(nx, w, 0)
                    split_q(nx, w, 1)
                    rstd_ctx(nx)
                low_half(bt, 0, 4)
                if not last:
                    split_q(nx, w, 2)
                    split_q(nx, w, 3)
                low_half(bt, 0, 7)
                if not last:
                    split_hi(nx)
                if not first:
                    y_rstd_pow(bt.next(-1))
                low_half(bt, 0, 10)
                if not last:
                    split_lo(nx)
                for n in POOL_TILES:
                    low_half(bt, 1, n)

            b0 = Batch(None, 0)
            w0 = Works(b0, False, False, start=True)
            pool.memset(xh[:, :, :], 1.0).then_inc(init_done, 1)
            for i in range(2):
                pool.memset(cmv[i][:, :, :], 1.0).then_inc(init_done, 1)
            pool.memset(mxp[:, :, :], 0.0).then_inc(init_done, 1)
            current(b0)
            rstd_ctx(b0)
            split_hi(b0)
            split_lo(b0)
            for g in range(4):
                split_q(b0, w0, g)
            over_batches(pool, one_batch)
            y_rstd_pow(Batch(None, B - 1))

        @block.scalar
        def _(act):
            def take_transposes(bt, w, k):
                j = w.flat[k][1][1]
                dst = (xT_hi, xT_lo)[j // 2][bt.par]
                c0, c1 = ((0, 8 * P), (8 * P, T))[j % 2]
                act.wait_ge(work_rdy, w.number(k) + 1)
                act.activation(dst[:, c0:c1], wbank(w, k).bitcast(F16)[:, 0:c1 - c0], ACT.Copy).then_inc(work_act, 1)

            def take_values(bt, u):
                act.wait_ge(pv_done, bt.val(2 * NTILE, NTILE * (u + 1)))
                if bt.off or bt.i is not None:
                    w = Works(bt, False, bt.is_last()) if u else Works(bt.next(-1), False, False)
                    act.wait_ge(work_rdy, w.number(w.find(("Y", u, 2))) + 1)
                for c in range(2):
                    act.activation(uT[u][:, c, :], ps[:, 4 + c, 0:CH], ACT.Copy).then_inc(u_done, 1)

            def one_batch(bt, first, last):
                w = Works(bt, first, last)
                for u in range(2):
                    for n in range(NTILE):
                        t, r = NTILE * u + n, rows_of(n)
                        act.wait_ge(s_rdy, bt.val(2 * NTILE, t + 1))
                        if not first or t >= 3:
                            pb, pt = (bt, t - 3) if t >= 3 else (bt.next(-1), t - 3 + 2 * NTILE)
                            pu, pn = divmod(pt, NTILE)
                            act.wait_ge(lo_pool if pn in POOL_TILES else lo_dve, lo_count(pb, pu, pn))
                        act.activation(e32[t % 3][0:r, :, :], s_banks(t, r), ACT.Exp).then_inc(exp_done, 1)
                        if not first or t >= 4:
                            act.wait_ge(pv_done, bt.val(2 * NTILE, t - 3))
                        act.activation(p_hi[t % 4][0:r, :, :], s_banks(t, r), ACT.Exp).then_inc(exp_done, 1)
                        if n:
                            for k, x in w.at((u, n - 1)):
                                if x[0] == "T":
                                    take_transposes(bt.next(), w, k)
                        elif u:
                            take_values(bt, 0)
                        elif not first:
                            take_values(bt.next(-1), 1)

            w0 = Works(Batch(None, 0), False, False, start=True)
            for k, (_, x) in enumerate(w0.flat):
                if x[0] == "T":
                    take_transposes(Batch(None, 0), w0, k)
            over_batches(act, one_batch)
            take_values(Batch(None, B - 1), 1)

        @block.vector
        def _(dve):
            def stats(bt, part):
                if part == 0:
                    dve.wait_ge(ctx_ld[bt.par], bt.val(16, 32 - 16 * bt.par))
                    if bt.off >= 2:
                        dve.wait_ge(xh_done, bt.val(1, -1))
                        dve.wait_ge(ctx_rstd, bt.val(1, 0))
                tiles = range(6) if part == 0 else range(6, NTILE) if part == 1 else ()
                for n in tiles:
                    r = rows_of(n)
                    ins = dve.bn_stats(cst[0:r, n, :], raw[bt.par][0:r, n, :])
                if part == 1:
                    ins.then_inc(ctx_stat, 1)
                if part == 2:
                    dve.wait_ge(ctx_stat, bt.val(3, 1))
                    dve.sem_inc(dve_waited, 1)
                    for n in range(NTILE):
                        r = rows_of(n)
                        ins = dve.bn_aggr(cmv[bt.par][0:r, n, :], cst[0:r, n, :])
                    ins.then_inc(ctx_stat, 1)
                    dve.wait_ge(ctx_stat, bt.val(3, 2))
                    if bt.off >= 1:
                        dve.wait_ge(ctx_rstd, bt.val(1, 0))
                    dve.tensor_scalar(cve[:, :], cmv[bt.par][:, :, 1], EPS, None, ALU.add).then_inc(ctx_stat, 1)

            def normalise(bt, part):
                if part == 0:
                    dve.wait_ge(ctx_rstd, bt.val(1, 1))
                    if bt.off >= 1:
                        dve.wait_ge(xa_done, bt.val(2, 0))
                for n in (range(6), range(6, NTILE))[part]:
                    r = rows_of(n)
                    ins = dve.tensor_scalar(xh[0:r, n, 1:D], raw[bt.par][0:r, n, 1:D], cmv[bt.par][0:r, n, 0:1],
                                            crs[bt.par][0:r, n:n + 1], ALU.subtract, ALU.mult)
                if part == 1:
                    ins.then_inc(xh_done, 1)

            def low_half(bt, u, n):
                t, r = NTILE * u + n, rows_of(n)
                dve.wait_ge(exp_done, bt.val(4 * NTILE, 2 * t + 2))
                if bt.off or t >= 4:
                    dve.wait_ge(pv_done, bt.val(2 * NTILE, t - 3))
                dve.tensor_tensor(out=p_lo[t % 4][0:r, :, :], in0=e32[t % 3][0:r, :, :], in1=p_hi[t % 4][0:r, :, :],
                                  op=ALU.subtract).then_inc(lo_dve, 1)

            def take(bt, nx, w, k):
                x = w.flat[k][1]
                src = wbank(w, k)
                dve.wait_ge(work_rdy, w.number(k) + 1)
                if x[0] == "q":
                    g = x[1]
                    if nx.off >= 1:
                        dve.wait_ge(q_split, nx.val(8, -8 + 2 * g + 2))
                    for j in range(4):
                        h = 4 * g + j
                        ins = dve.tensor_scalar(q32[:, h * S:(h + 1) * S], src[:, j * S:(j + 1) * S], sc_cur[:, h:h + 1],
                                                kb_cur[:, h:h + 1], ALU.mult, ALU.add)
                    ins.then_inc(work_dve, 1)
                elif x[0] == "M":
                    mt, c = x[1:]
                    r = min(P, HQ - mt * P)
                    ob = nx if mt < 7 else bt
                    if c == 0 and mt in (0, 7) and ob.off >= 1:
                        dve.wait_ge(nm_done, ob.val(2, 0 if mt else -1))
                    dve.tensor_reduce(mxp[0:r, mt, c:c + 1], src[0:r, 0:MCUT[c + 1] - MCUT[c]], AX_X, ALU.max).then_inc(work_dve, 1)
                    if c == 2 and mt in (6, NM - 1):
                        tiles = slice(0, 7) if mt == 6 else slice(7, NM)
                        dve.wait_ge(work_dve, w.taken(k))
                        dve.tensor_reduce(nm[:, tiles], mxp[:, tiles, :], AX_X, ALU.max, negate=True).then_inc(nm_done, 1)
                elif x[0] == "R":
                    c0, c1 = row_cols(x[1])
                    ob = nx if x[1] < 2 else bt
                    dve.tensor_scalar(q_hi[ob.par][0:1, c0:c1], src[0:1, 0:c1 - c0], HEADROOM, None, ALU.add).then_inc(work_dve, 1)
                else:
                    half, g = x[1:]
                    ob = bt.next(-1) if half and not w.tail else bt
                    hs = Y_HEADS[g]
                    yv = src[0:S, 0:len(hs) * (D + 1)].rearrange("s (h n) -> s h n", n=D + 1)
                    base = 8 * half + 3 * g
                    if half == 0 and g == 0 and (ob.off >= 1):
                        dve.wait_ge(y_norm, ob.val(4, 0))
                    h0 = 8 * half + hs[0]
                    dve.reciprocal(ry[:, h0:h0 + len(hs)], yv[:, :, D]).then_inc(y_chain, 1)
                    dve.wait_ge(y_chain, ob.val(16, base + 1))
                    for j, _ in enumerate(hs):
                        if half == 0 and g == 0 and j == 0:
                            add = x1[:, bass.ds(ob.index(), 1), :].rearrange("s a d -> s (a d)")
                        else:
                            add = acc[:, :]
                        ins = dve.scalar_tensor_tensor(out=acc[:, :], in0=yv[:, j, 0:D], scalar=ry[:, h0 + j:h0 + j + 1], in1=add,
                                                       op0=ALU.mult, op1=ALU.add)
                        if j < len(hs) - 1:
                            ins.then_inc(y_chain, 1)
                            dve.wait_ge(y_chain, ob.val(16, base + j + 2))
                        else:
                            ins.then_inc(work_dve, 1)
                    if half == 1 and g == 2:
                        dve.wait_ge(work_dve, w.taken(k))
                        dve.bn_stats(yst[:, :], acc[:, :]).then_inc(y_norm, 1)
                        dve.wait_ge(y_norm, ob.val(4, 1))
                        dve.sem_inc(dve_waited, 1)
                        dve.bn_aggr(ymv[:, :], yst[:, :]).then_inc(y_norm, 1)
                        dve.wait_ge(y_norm, ob.val(4, 2))
                        dve.tensor_scalar(yve[:, :], ymv[:, 1:2], EPS, None, ALU.add).then_inc(y_norm, 1)

            def layer_norm(bt):
                dve.wait_ge(y_rstd, bt.val(1, 1))
                dve.tensor_scalar(x2[:, bass.ds(bt.index(), 1), :].rearrange("s a d -> s (a d)"), acc[:, :], ymv[:, 0:1], yrs[:, 0:1],
                                  ALU.subtract, ALU.mult).then_inc(y_norm, 1)

            def one_batch(bt, first, last):
                w, nx = Works(bt, first, last), bt.next()
                for u in range(2):
                    for n in range(NTILE):
                        before = [] if (u, n) == (0, 0) else w.at((u, n - 1) if n else (u - 1, NTILE - 1))
                        before = [k for k, x in before if x[0] != "T"]
                        for k in before[:1]:
                            take(bt, nx, w, k)
                        if n not in POOL_TILES:
                            low_half(bt, u, n)
                        for k in before[1:]:
                            take(bt, nx, w, k)
                        if u == 0 and n < 3 and not last:
                            stats(nx, n)
                        if u == 0 and n in (4, 5) and not last:
                            normalise(nx, n - 4)
                        if u == 0 and n == 8 and not first:
                            layer_norm(bt.next(-1))
                for k, x in w.at((1, NTILE - 1)):
                    take(bt, nx, w, k)

            b0 = Batch(None, 0)
            w0 = Works(b0, False, False, start=True)
            dve.wait_ge(init_done, 4)
            for part in range(3):
                stats(b0, part)
            for part in range(2):
                normalise(b0, part)
            for k, (_, x) in enumerate(w0.flat):
                if x[0] != "T":
                    if x == ("q", 0):
                        dve.wait_ge(cur_done, 1)
                    take(b0, b0, w0, k)
            over_batches(dve, one_batch)
            bl = Batch(None, B - 1)
            wt = Works(bl.next(), False, False, tail=True)
            for k in range(3):
                take(bl, bl, wt, k)
            layer_norm(bl)

        @block.tensor
        def _(pe):
            def work(bt, nx, w, k):
                x = w.flat[k][1]
                dst = wbank(w, k)
                if k >= 2:
                    pe.wait_ge(work_act if w.is_act(k - 2) else work_dve, w.taken(k - 2))
                elif w.base[1] or w.base[0]:
                    pe.wait_ge(work_dve, bt_val_dve(w, k))
                if x[0] == "q":
                    if x[1] == 0:
                        pe.wait_ge(cur_done, nx.val(1, 1))
                    for j in range(4):
                        last = pe.matmul(dst[:, j * S:(j + 1) * S], qa[:, 4 * x[1] + j, :], ln_cur[:, :], start=True, stop=True)
                elif x[0] == "T":
                    j = x[1]
                    src = (xa_hi, xa_lo)[j // 2][nx.par]
                    pe.wait_ge(xa_done, nx.val(2, 1 + j // 2))
                    n0, n1 = ((0, 8), (8, NTILE))[j % 2]
                    for n in range(n0, n1):
                        r = rows_of(n)
                        c = (n - n0) * P
                        last = pe.transpose(dst.bitcast(F16)[:, c:c + r], src[0:r, n, :], ident16[0:r, 0:r])
                elif x[0] == "M":
                    mt, c = x[1:]
                    ob = nx if mt < 7 else bt
                    r = min(P, HQ - mt * P)
                    if c == 0 and mt in (0, 7):
                        pe.wait_ge(q_split, ob.val(8, 7 if mt else 7))
                        pe.wait_ge(work_act, ob.val(4, 2))
                    last = pe.matmul(dst[0:r, 0:MCUT[c + 1] - MCUT[c]], q_hi[ob.par][:, mt * P:mt * P + r],
                                     xT_hi[ob.par][:, MCUT[c]:MCUT[c + 1]], start=True, stop=True)
                elif x[0] == "R":
                    c0, c1 = row_cols(x[1])
                    ob = nx if x[1] < 2 else bt
                    pe.wait_ge(nm_done, ob.val(2, 1 + x[1] // 2))
                    for c in range(c0, c1, P):
                        r = min(P, c1 - c)
                        last = pe.matmul(dst[0:1, c - c0:c - c0 + r], nm[0:r, c // P:c // P + 1], ident16[0:r, 0:r], start=True, stop=True)
                else:
                    half, g = x[1:]
                    ob = bt.next(-1) if half and not w.tail else bt
                    if g == 0:
                        pe.wait_ge(u_done, ob.val(4, 2 * half + 2))
                    for j, h in enumerate(Y_HEADS[g]):
                        last = pe.matmul(dst[0:S, j * (D + 1):(j + 1) * (D + 1)],
                                         uT[half][:, :, :].rearrange("d c n -> d (c n)")[:, h * S:(h + 1) * S],
                                         w2h[:, half * 8 + h, :], start=True, stop=True)
                last.then_inc(work_rdy, 1)

            def bt_val_dve(w, k):
                return w.bt.val(w.base_dve[0], w.base_dve[1] - 1 + k)

            def scores(bt, u, n, c):
                t, r = NTILE * u + n, rows_of(n)
                if c == 0:
                    if n == 0:
                        if bt.i is None and bt.off == 0:
                            w = Works(bt, u == 1, False, start=u == 0)
                        else:
                            w = Works(bt, False, bt.is_last()) if u else Works(bt.next(-1), False, False)
                        pe.wait_ge(work_dve, w.taken(w.find(("R", 1 if u == 0 else 3))))
                        pe.wait_ge(q_split, bt.val(8, 8))
                        pe.wait_ge(work_act, bt.val(4, 4))
                    if not (bt.i is None and bt.off == 0 and t < 2):
                        pe.wait_ge(exp_done, bt.val(4 * NTILE, 2 * (t - 1)))
                out = ps[0:r, 2 * (t % 2) + c, 0:CH]
                cols = slice(u * HALF + c * CH, u * HALF + (c + 1) * CH)
                hi, lo = xT_hi[bt.par][:, n * P:n * P + r], xT_lo[bt.par][:, n * P:n * P + r]
                pe.matmul(out, hi, q_hi[bt.par][:, cols], start=True, stop=False)
                pe.matmul(out, hi, q_lo[bt.par][:, cols], start=False, stop=False)
                last = pe.matmul(out, lo, q_hi[bt.par][:, cols], start=False, stop=True)
                if c == 1:
                    last.then_inc(s_rdy, 1)

            def values(bt, u, n, c):
                t, r = NTILE * u + n, rows_of(n)
                if c == 0:
                    if n == 0 and not (bt.i is None and bt.off == 0 and u == 0):
                        pe.wait_ge(u_done, bt.val(4, 2 * u))
                    pe.wait_ge(exp_done, bt.val(4 * NTILE, 2 * t + 2))
                out = ps[:, 4 + c, 0:CH]
                hi, lo = xa_hi[bt.par][0:r, n, :], xa_lo[bt.par][0:r, n, :]
                pe.matmul(out, hi, p_hi[t % 4][0:r, c, :], start=n == 0, stop=False)
                pe.matmul(out, lo, p_hi[t % 4][0:r, c, :], start=False, stop=False)
                if c == 0:
                    pe.wait_ge(lo_pool if n in POOL_TILES else lo_dve, lo_count(bt, u, n))
                last = pe.matmul(out, hi, p_lo[t % 4][0:r, c, :], start=False, stop=n == NTILE - 1)
                if c == 1:
                    last.then_inc(pv_done, 1)

            def one_batch(bt, first, last):
                w, nx = Works(bt, first, last), bt.next()
                for u in range(2):
                    for n in range(NTILE):
                        todo = [k for k, _ in w.at((u, n))]
                        t3 = NTILE * u + n + 3
                        sb_, st = (bt, t3) if t3 < 2 * NTILE else (nx, t3 - 2 * NTILE)
                        ahead = not (last and t3 >= 2 * NTILE)
                        for part in range(4):
                            if part < 2:
                                values(bt, u, n, part)
                            elif ahead:
                                scores(sb_, st // NTILE, st % NTILE, part - 2)
                            take_n = -(-len(todo) // (4 - part))
                            for k in todo[:take_n]:
                                work(bt, nx, w, k)
                            todo = todo[take_n:]

            b0 = Batch(None, 0)
            w0 = Works(b0, False, False, start=True)
            for k in range(len(w0.flat)):
                work(b0, b0, w0, k)
            for n in range(3):
                for c in range(2):
                    scores(b0, 0, n, c)
            over_batches(pe, one_batch)
            bl = Batch(None, B - 1)
            wt = Works(bl.next(), False, False, tail=True)
            for k in range(3):
                work(bl, bl, wt, k)


def row_cols(r):
    t0 = (0, 4, 7, 11, NM)
    return t0[r] * P, min(t0[r + 1] * P, HQ)


def ffn(nc, a, m, ps, out):
    with ExitStack() as ctx:
        def sb(name, shape, dt=F32):
            return ctx.enter_context(nc.sbuf_tensor(name, shape, dt))

        def sem(name):
            return ctx.enter_context(nc.semaphore(name))

        ident, nhalf, x2 = m["ident"], m["nhalf"], m["x2"]
        NC = NE // P
        K8 = 8
        HK = FH * K8
        QP = 25

        f_wq, f_wqt = sb("f_wq", [D, NB * KD]), sb("f_wqt", [KD, NB, D])
        f_keys, f_down, f_up = sb("f_keys", [KD, NB, KEYS]), sb("f_down", [D, NE]), sb("f_up", [P, NC, D])
        f_gam, f_bet = sb("f_gam", [KD, NB]), sb("f_bet", [KD, NB])
        x2T, xcT, xct = sb("x2T", [D, NT]), sb("xcT", [D, NT]), sb("xct", [S, B, D])
        msum, mean = sb("msum", [D, 1]), sb("mean", [D, 1])
        cov, cw = sb("cov", [D, D]), sb("cw", [KD, NB, D])
        var, vrs, gain = sb("var", [KD, NB]), sb("vrs", [KD, NB]), sb("gain", [KD, NB])
        kscaled, sim_w, sim_c = sb("kscaled", [KD, NB, KEYS]), sb("sim_w", [D, NB * KEYS]), sb("sim_c", [1, NB * KEYS])
        ones_r = sb("ones_r", [1, S])
        off8 = sb("off8", [P, 1])
        iota8, iota16, iota_i = sb("iota8", [P, K8]), sb("iota16", [P, 2 * NC], F16), sb("iota_i", [P, P], mybir.dt.int32)
        iota_f, iota_w = sb("iota_f", [P, P]), sb("iota_w", [P, P, S], F16)
        xc_cur, x2_cur = sb("xc_cur", [D, 2, S]), sb("x2_cur", [D, 2 * S])
        simb = sb("simb", [S, 2, NB, KEYS])
        top, idx, idxf = sb("top", [S, 2, NB, K8]), sb("idx", [S, 2, NB, K8], U32), sb("idxf", [S, 2, NB, K8])
        comb = sb("comb", [S, 2, FH, K8, K8])
        sc, pk = sb("sc", [S, 2, FH, K8]), sb("pk", [S, 2, FH, K8], U32)
        pij, pijf = sb("pij", [S, 2, 2, HK], U32), sb("pijf", [S, 2, 2, HK])
        eq = sb("eq", [S, 2 * NB, K8, K8])
        ij = sb("ij", [S, 2, NB, K8])
        ef, eu, erc = sb("ef", [S, 2, HK]), sb("eu", [S, 2, HK], U32), sb("erc", [S, 2, 2, HK], U32)
        sel = sb("sel", [S, 3, 2, HK])
        dsc, esc = sb("dsc", [S, 2, FH, K8]), sb("esc", [S, 2, FH, K8])
        ssum, srec = sb("ssum", [S, 2, FH]), sb("srec", [S, 2, FH])
        rT, cT, w_hi, w_lo = sb("rT", [P, S], F16), sb("cT", [P, S], F16), sb("w_hi", [P, S], F16), sb("w_lo", [P, S], F16)
        oneh = sb("oneh", [P, P, S], F16)
        eqc = sb("eqc", [P, S, 2 * NC], F16)
        mv_hi, mv_lo = sb("mv_hi", [P, S, 2 * NC], F16), sb("mv_lo", [P, S, 2 * NC], F16)
        hsq, hth = sb("hsq", [P, 2, 2 * 2 * S]), sb("hth", [P, 2, 2 * 2 * S])
        gel = [sb(f"gel{i}", [P, NC, 2, S]) for i in range(2)]
        wgt = sb("wgt", [P, NC, 2, S])
        zf, ost = sb("zf", [S, 2, D]), sb("ost", [S, 2, D])
        fst, fmv, fve, frs = sb("fst", [S, 2, 6]), sb("fmv", [S, 2, 2]), sb("fve", [S, 2]), sb("frs", [S, 2])

        f_ld, f_waited = sem("f_ld"), sem("f_waited")
        fc_done, x2T_ps, x2T_done, mean_done, xcT_done = (sem(n) for n in ("fc_done", "x2T_ps", "x2T_done", "mean_done", "xcT_done"))
        xct_ps, xct_done, cov_ps, cov_done = (sem(n) for n in ("xct_ps", "xct_done", "cov_ps", "cov_done"))
        cw_ps, cw_done, var_done, vrs_done, gain_done = (sem(n) for n in ("cw_ps", "cw_done", "var_done", "vrs_done", "gain_done"))
        simw_ps, simw_done, wide_done = sem("simw_ps"), sem("simw_done"), sem("wide_done")
        fcur_done, sim_ps, sim_done, top_done, comb_done, best_done = (sem(n) for n in ("fcur_done", "sim_ps", "sim_done", "top_done", "comb_done", "best_done"))
        dsc_done, esc_done, pick, sel_done, selT_ps, selT_done = (sem(n) for n in ("dsc_done", "esc_done", "pick", "sel_done", "selT_ps", "selT_done"))
        wlo_done, oneh_done, g_ps, g_done, y_ps, z_done, z_rstd, o_done, out_done = (
            sem("f" + n) for n in ("wlo_done", "oneh_done", "g_ps", "g_done", "y_ps", "z_done", "z_rstd", "o_done", "out_done"))
        h_ps, hsq_done, hu_done, hth_done, gel_done = (sem(n) for n in ("h_ps", "hsq_done", "hu_done", "hth_done", "gel_done"))

        block = ctx.enter_context(nc.Block())
        NPAIR = B // 2
        BN_C = 0.044715
        TANH_C = (2.0 / 3.141592653589793) ** 0.5

        @block.sync
        def _(sp):
            for dst, src in ((f_wq[:, :], a["L0_ffn_w_q"]),
                             (f_wqt[:, 0:FH, :], a["ffn_wq_t"][0:FH * KD, :].rearrange("(n e) d -> e n d", e=KD)),
                             (f_wqt[:, FH:NB, :], a["ffn_wq_t"][FH * KD:NB * KD, :].rearrange("(n e) d -> e n d", e=KD)),
                             (f_keys[:, :, :], a["ffn_keys_t"].rearrange("e s h k -> e (s h) k")),
                             (f_down[:, :], a["ffn_down_t"]),
                             (f_up[:, :, :], a["L0_ffn_up_embed"].rearrange("(c e) d -> e c d", e=P)),
                             (f_gam[:, :], a["L0_ffn_bn_gamma"]),
                             (f_bet[:, :], a["L0_ffn_bn_beta"])):
                sp.dma_start(dst, src).then_inc(f_ld, 16)
            with sp.Fori(0, NPAIR) as i:
                sp.wait_ge(o_done, i * 1 + 1)
                sp.dma_start(out[bass.ds(i * 2, 2), :, :].rearrange("b s d -> s b d"), ost[:, :, :]).then_inc(out_done, 16)
            sp.wait_ge(out_done, 16 * NPAIR)

        @block.gpsimd
        def _(pool):
            pool.iota(iota_i[:, :], pattern=[[1, P]], base=0, channel_multiplier=0).then_inc(fc_done, 1)
            pool.memset(ones_r[:, :], 1.0).then_inc(fc_done, 1)
            pool.memset(off8[:, :], 0.0).then_inc(fc_done, 1)
            pool.wait_ge(fc_done, 3)
            pool.memset(off8[HK:P, :], float(NC)).then_inc(fc_done, 1)
            pool.wait_ge(fc_done, 4)
            pool.tensor_copy(iota_f[:, :], iota_i[:, :]).then_inc(fc_done, 1)
            pool.tensor_copy(iota8[:, :], iota_i[:, 0:K8]).then_inc(fc_done, 1)
            pool.tensor_copy(iota16[:, :], iota_i[:, 0:2 * NC]).then_inc(fc_done, 1)
            pool.wait_ge(fc_done, 7)
            pool.tensor_copy(iota_w[:, :, :], iota_f[:, :].rearrange("p (e a) -> p e a", a=1).to_broadcast([P, P, S])).then_inc(wide_done, 1)
            pool.wait_ge(var_done, 3)
            pool.tensor_tensor(out=vrs[:, :], in0=var[:, :], in1=nhalf[:, 0:NB], op=ALU.pow).then_inc(vrs_done, 1)

            def one_pair(i, first=False):
                pool.wait_ge(top_done, i * 2 + 1)
                if not first:
                    pool.wait_ge(best_done, i * 2)
                for hf in range(2):
                    ins = pool.tensor_tensor(out=comb[:, hf, :, :, :],
                                             in0=top[:, hf, 0:FH, :].rearrange("s h (i a) -> s h i a", a=1).to_broadcast([S, FH, K8, K8]),
                                             in1=top[:, hf, FH:NB, :].rearrange("s h (a j) -> s h a j", a=1).to_broadcast([S, FH, K8, K8]),
                                             op=ALU.add)
                ins.then_inc(comb_done, 1)

            def finish(i):
                pool.wait_ge(z_done, i * 4 + 4)
                pool.tensor_tensor(out=frs[:, :], in0=fve[:, :], in1=nhalf[0:S, 0:2], op=ALU.pow).then_inc(z_rstd, 1)

            one_pair(0, True)
            one_pair(1)
            finish(0)
            with pool.Fori(2, NPAIR) as i:
                one_pair(i)
                finish(i - 1)
            finish(NPAIR - 1)

        @block.scalar
        def _(act):
            for k in range(NG):
                act.wait_ge(x2T_ps, k + 1)
                act.activation(x2T[:, k * G * S:(k + 1) * G * S], ps[:, k, 0:G * S], ACT.Copy).then_inc(x2T_done, 1)
            for k in range(NG):
                act.wait_ge(xct_ps, k + 1)
                act.activation(xct[:, k * G:(k + 1) * G, :], ps[0:S, 4 + k, :].rearrange("s (b d) -> s b d", b=G), ACT.Copy).then_inc(xct_done, 1)
            act.wait_ge(cov_ps, 1)
            act.activation(cov[:, :], ps[:, 0, 0:D], ACT.Copy, scale=1.0 / NT).then_inc(cov_done, 1)
            act.wait_ge(simw_ps, 1)
            act.activation(sim_w[:, :], ps[:, 5, :], ACT.Copy).then_inc(simw_done, 1)
            act.activation(sim_c[:, :], ps[0:1, 6, :], ACT.Copy).then_inc(simw_done, 1)
            act.wait_ge(fc_done, 7)

            def one_pair(i, first):
                if not first:
                    act.wait_ge(h_ps, i * 2)
                cols = bass.ds(i * (2 * S), 2 * S)
                act.activation(xc_cur[:, :, :].rearrange("d a s -> d (a s)"), xcT[:, cols], ACT.Copy).then_inc(fcur_done, 1)
                act.activation(x2_cur[:, :], x2T[:, cols], ACT.Copy).then_inc(fcur_done, 1)
                act.wait_ge(sim_ps, i * 2 + 2)
                if not first:
                    act.wait_ge(top_done, i * 2)
                act.activation(simb[:, :, :, :].rearrange("s a n k -> s a (n k)"), ps[0:S, 0:2, :], ACT.Copy).then_inc(sim_done, 1)
                for r in range(2):
                    act.wait_ge(h_ps, i * 2 + r + 1)
                    if r or not first:
                        act.wait_ge(gel_done, i * 2 + r)
                    act.activation(hsq[:, :, :], ps[:, 2:4, 0:4 * S], ACT.Square).then_inc(hsq_done, 1)
                    act.wait_ge(hu_done, i * 2 + r + 1)
                    act.activation(hth[:, :, :], hsq[:, :, :], ACT.Tanh, scale=TANH_C * BN_C).then_inc(hth_done, 1)
                act.wait_ge(dsc_done, i * 1 + 1)
                act.activation(esc[:, :, :, :], dsc[:, :, :, :], ACT.Exp).then_inc(esc_done, 1)
                act.wait_ge(selT_ps, i * 1 + 1)
                if not first:
                    act.wait_ge(oneh_done, i * 1)
                act.activation(rT[:, :], ps[:, 4, 0:S], ACT.Copy)
                act.activation(cT[:, :], ps[:, 4, S:2 * S], ACT.Identity, bias=off8[:, 0:1])
                act.activation(w_hi[:, :], ps[:, 4, 2 * S:3 * S], ACT.Copy).then_inc(selT_done, 1)

            one_pair(0, True)
            with act.Fori(1, NPAIR) as i:
                one_pair(i, False)

        @block.vector
        def _(dve):
            dve.wait_ge(x2T_done, NG)
            dve.tensor_reduce(msum[:, :], x2T[:, :], AX_X, ALU.add).then_inc(mean_done, 1)
            dve.wait_ge(mean_done, 1)
            dve.tensor_scalar(mean[:, :], msum[:, :], 1.0 / NT, None, ALU.mult).then_inc(mean_done, 1)
            dve.wait_ge(mean_done, 2)
            dve.tensor_scalar(xcT[:, :], x2T[:, :], mean[:, 0:1], None, ALU.subtract).then_inc(xcT_done, 1)
            dve.wait_ge(f_ld, 16 * 8)
            for k in range(4):
                dve.wait_ge(cw_ps, k + 1)
                dve.tensor_tensor(out=cw[:, 4 * k:4 * k + 4, :], in0=ps[:, 1 + k, :].rearrange("e (n d) -> e n d", n=4),
                                  in1=f_wqt[:, 4 * k:4 * k + 4, :], op=ALU.mult).then_inc(cw_done, 1)
            dve.wait_ge(cw_done, 4)
            dve.tensor_reduce(var[:, :], cw[:, :, :], AX_X, ALU.add).then_inc(var_done, 1)
            dve.wait_ge(var_done, 1)
            dve.tensor_scalar(var[:, :], var[:, :], 0.0, None, ALU.max).then_inc(var_done, 1)
            dve.wait_ge(var_done, 2)
            dve.tensor_scalar(var[:, :], var[:, :], EPS, None, ALU.add).then_inc(var_done, 1)
            dve.wait_ge(vrs_done, 1)
            dve.tensor_tensor(out=gain[:, :], in0=vrs[:, :], in1=f_gam[:, :], op=ALU.mult).then_inc(gain_done, 1)
            dve.wait_ge(gain_done, 1)
            dve.tensor_tensor(out=kscaled[:, :, :], in0=f_keys[:, :, :],
                              in1=gain[:, :].rearrange("e (n a) -> e n a", a=1).to_broadcast([KD, NB, KEYS]), op=ALU.mult).then_inc(gain_done, 1)
            dve.wait_ge(fc_done, 7)
            dve.wait_ge(wide_done, 1)

            def weigh(i, par, n):
                dve.wait_ge(g_ps, i * 4 + n + 1)
                if n == 0:
                    dve.wait_ge(gel_done, i * 2 + 2)
                cols = slice(n * QP, (n + 1) * QP)
                dve.tensor_tensor(out=wgt[:, :, :, cols].rearrange("e c a s -> e a c s"),
                                  in0=ps[:, 5 + n % 2, 0:QP * 2 * NC].rearrange("e (s a c) -> e a c s", a=2, c=NC),
                                  in1=gel[par][:, :, :, cols].rearrange("e c a s -> e a c s"), op=ALU.mult).then_inc(g_done, 1)

            def gelu_part(i, par, r, part):
                hb = ps[:, 2:4, 0:4 * S]
                if part == 0:
                    dve.wait_ge(hsq_done, i * 2 + r + 1)
                    dve.scalar_tensor_tensor(out=hsq[:, :, :], in0=hsq[:, :, :], scalar=1.0 / BN_C, in1=hb,
                                             op0=ALU.add, op1=ALU.mult).then_inc(hu_done, 1)
                else:
                    dve.wait_ge(hth_done, i * 2 + r + 1)
                    dve.scalar_tensor_tensor(out=gel[par][:, 4 * r:4 * r + 4, :, :].rearrange("e (b c) a s -> e b (c a s)", b=2),
                                             in0=hth[:, :, :], scalar=1.0, in1=hb, op0=ALU.add, op1=ALU.mult).then_inc(gel_done, 1)

            def step(i, par, first):
                dve.wait_ge(sim_done, i * 1 + 1)
                if not first:
                    dve.wait_ge(comb_done, i * 1)
                    dve.wait_ge(pick, i * 6)
                dve.sem_inc(f_waited, 1)
                for hf in range(2):
                    for n in range(NB):
                        ins = dve.max(top[:, hf, n, :], simb[:, hf, n, :])
                ins.then_inc(top_done, 1)
                dve.wait_ge(top_done, i * 2 + 1)
                dve.sem_inc(f_waited, 1)
                for hf in range(2):
                    for n in range(NB):
                        ins = dve.max_index(idx[:, hf, n, :], top[:, hf, n, :], simb[:, hf, n, :])
                ins.then_inc(top_done, 1)
                gelu_part(i, par, 0, 0)
                dve.wait_ge(top_done, i * 2 + 2)
                dve.tensor_copy(idxf[:, :, :, :], idx[:, :, :, :]).then_inc(pick, 1)
                gelu_part(i, par, 0, 1)
                if not first:
                    weigh(i - 1, 1 - par, 0)
                    weigh(i - 1, 1 - par, 1)
                gelu_part(i, par, 1, 0)
                dve.wait_ge(comb_done, i * 1 + 1)
                dve.sem_inc(f_waited, 1)
                for hf in range(2):
                    for h in range(FH):
                        ins = dve.max(sc[:, hf, h, :], comb[:, hf, h, :, :].rearrange("s i j -> s (i j)"))
                ins.then_inc(best_done, 1)
                gelu_part(i, par, 1, 1)
                dve.wait_ge(best_done, i * 2 + 1)
                dve.sem_inc(f_waited, 1)
                for hf in range(2):
                    for h in range(FH):
                        ins = dve.max_index(pk[:, hf, h, :], sc[:, hf, h, :], comb[:, hf, h, :, :].rearrange("s i j -> s (i j)"))
                ins.then_inc(best_done, 1)
                if not first:
                    dve.wait_ge(esc_done, i * 1)
                dve.tensor_tensor(out=dsc[:, :, :, :], in0=sc[:, :, :, :], in1=sc[:, :, :, 0:1].to_broadcast([S, 2, FH, K8]),
                                  op=ALU.subtract).then_inc(dsc_done, 1)
                dve.wait_ge(best_done, i * 2 + 2)
                flat = pk[:, :, :, :].rearrange("s a h k -> s a (h k)")
                dve.tensor_scalar(pij[:, :, 0, :], flat, 3, None, ALU.logical_shift_right)
                dve.tensor_scalar(pij[:, :, 1, :], flat, K8 - 1, None, ALU.bitwise_and).then_inc(pick, 1)
                dve.wait_ge(pick, i * 6 + 2)
                dve.tensor_copy(pijf[:, :, :, :], pij[:, :, :, :]).then_inc(pick, 1)
                dve.wait_ge(pick, i * 6 + 3)
                dve.tensor_tensor(out=eq[:, :, :, :],
                                  in0=pijf[:, :, :, :].rearrange("s a b (h k c) -> s (a b h) k c", h=FH, c=1).to_broadcast([S, 2 * NB, K8, K8]),
                                  in1=iota8[0:S, :].rearrange("s (a b j) -> s a b j", a=1, b=1).to_broadcast([S, 2 * NB, K8, K8]),
                                  op=ALU.is_equal).then_inc(pick, 1)
                dve.wait_ge(pick, i * 6 + 4)
                dve.tensor_tensor(out=eq[:, :, :, :], in0=eq[:, :, :, :],
                                  in1=idxf[:, :, :, :].rearrange("s a n (c j) -> s (a n) c j", c=1).to_broadcast([S, 2 * NB, K8, K8]),
                                  op=ALU.mult).then_inc(pick, 1)
                dve.wait_ge(pick, i * 6 + 5)
                dve.tensor_reduce(ij[:, :, :, :].rearrange("s a n k -> s (a n) k"), eq[:, :, :, :], AX_X, ALU.add).then_inc(pick, 1)
                dve.wait_ge(pick, i * 6 + 6)
                dve.scalar_tensor_tensor(out=eu[:, :, :], in0=ij[:, :, 0:FH, :].rearrange("s a h k -> s a (h k)"), scalar=float(KEYS),
                                         in1=ij[:, :, FH:NB, :].rearrange("s a h k -> s a (h k)"), op0=ALU.mult, op1=ALU.add).then_inc(sel_done, 1)
                dve.wait_ge(sel_done, i * 6 + 1)
                dve.tensor_scalar(erc[:, 0, :, :], eu[:, :, :], P - 1, None, ALU.bitwise_and)
                dve.tensor_scalar(erc[:, 1, :, :], eu[:, :, :], 7, None, ALU.logical_shift_right).then_inc(sel_done, 1)
                dve.wait_ge(esc_done, i * 1 + 1)
                dve.tensor_reduce(ssum[:, :, :], esc[:, :, :, :], AX_X, ALU.add).then_inc(sel_done, 1)
                if not first:
                    dve.wait_ge(selT_ps, i * 1)
                dve.wait_ge(sel_done, i * 6 + 2)
                dve.tensor_copy(sel[:, 0:2, :, :], erc[:, :, :, :])
                dve.wait_ge(sel_done, i * 6 + 3)
                dve.reciprocal(srec[:, :, :], ssum[:, :, :]).then_inc(sel_done, 1)
                dve.wait_ge(sel_done, i * 6 + 4)
                dve.tensor_scalar(srec[:, :, :], srec[:, :, :], 0.5, None, ALU.mult).then_inc(sel_done, 1)
                dve.wait_ge(sel_done, i * 6 + 5)
                dve.tensor_tensor(out=sel[:, 2, :, :].rearrange("s a (h k) -> s (a h) k", h=FH),
                                  in0=esc[:, :, :, :].rearrange("s a h k -> s (a h) k"),
                                  in1=srec[:, :, :].rearrange("s a (h c) -> s (a h) c", c=1).to_broadcast([S, 2 * FH, K8]),
                                  op=ALU.mult).then_inc(sel_done, 1)
                if not first:
                    weigh(i - 1, 1 - par, 2)
                    weigh(i - 1, 1 - par, 3)
                dve.wait_ge(selT_done, i * 1 + 1)
                dve.tensor_tensor(out=w_lo[:, :], in0=ps[:, 4, 2 * S:3 * S], in1=w_hi[:, :], op=ALU.subtract).then_inc(wlo_done, 1)
                dve.tensor_tensor(out=oneh[:, :, :], in0=iota_w[:, :, :],
                                  in1=rT[:, :].rearrange("p (a s) -> p a s", a=1).to_broadcast([P, P, S]), op=ALU.is_equal)
                dve.tensor_tensor(out=eqc[:, :, :], in0=cT[:, :].rearrange("p (s a) -> p s a", a=1).to_broadcast([P, S, 2 * NC]),
                                  in1=iota16[:, :].rearrange("p (a j) -> p a j", a=1).to_broadcast([P, S, 2 * NC]), op=ALU.is_equal).then_inc(wlo_done, 1)
                dve.wait_ge(wlo_done, i * 2 + 2)
                for w, dst in ((w_hi, mv_hi), (w_lo, mv_lo)):
                    ins = dve.tensor_tensor(out=dst[:, :, :], in0=eqc[:, :, :],
                                            in1=w[:, :].rearrange("p (s a) -> p s a", a=1).to_broadcast([P, S, 2 * NC]), op=ALU.mult)
                ins.then_inc(oneh_done, 1)

            def add_up(i):
                dve.wait_ge(y_ps, i * 1 + 1)
                dve.tensor_tensor(out=zf[:, :, :], in0=ps[0:S, 7, 0:2 * D].rearrange("s (a d) -> s a d", a=2),
                                  in1=x2[:, bass.ds(i * 2, 2), :], op=ALU.add).then_inc(z_done, 1)
                dve.wait_ge(z_done, i * 4 + 1)
                for hf in range(2):
                    ins = dve.bn_stats(fst[:, hf, :], zf[:, hf, :])
                ins.then_inc(z_done, 1)
                dve.wait_ge(z_done, i * 4 + 2)
                dve.sem_inc(f_waited, 1)
                for hf in range(2):
                    ins = dve.bn_aggr(fmv[:, hf, :], fst[:, hf, :])
                ins.then_inc(z_done, 1)
                dve.wait_ge(z_done, i * 4 + 3)
                dve.tensor_scalar(fve[:, :], fmv[:, :, 1], EPS, None, ALU.add).then_inc(z_done, 1)

            def last_norm(i, first):
                dve.wait_ge(z_rstd, i * 1 + 1)
                if not first:
                    dve.wait_ge(out_done, i * 16)
                for hf in range(2):
                    ins = dve.tensor_scalar(ost[:, hf, :], zf[:, hf, :], fmv[:, hf, 0:1], frs[:, hf:hf + 1], ALU.subtract, ALU.mult)
                ins.then_inc(o_done, 1)

            step(0, 0, True)
            step(1, 1, False)
            add_up(0)
            last_norm(0, True)
            with dve.Fori(0, (NPAIR - 2) // 2) as k:
                for off in range(2):
                    step(k * 2 + 2 + off, off, False)
                    add_up(k * 2 + 1 + off)
                    last_norm(k * 2 + 1 + off, False)
            for n in range(4):
                weigh(NPAIR - 1, (NPAIR - 1) % 2, n)
            add_up(NPAIR - 1)
            last_norm(NPAIR - 1, False)

        @block.tensor
        def _(pe):
            for k in range(NG):
                for j in range(G):
                    last = pe.transpose(ps[:, k, j * S:(j + 1) * S], x2[:, k * G + j, :], ident[0:S, 0:S])
                last.then_inc(x2T_ps, 1)
            pe.wait_ge(xcT_done, 1)
            for k in range(NG):
                for j in range(G):
                    b = k * G + j
                    last = pe.transpose(ps[0:S, 4 + k, j * D:(j + 1) * D], xcT[:, b * S:(b + 1) * S], ident[:, :])
                last.then_inc(xct_ps, 1)
            pe.wait_ge(xct_done, NG)
            for b in range(B):
                last = pe.matmul(ps[:, 0, 0:D], xct[:, b, :], xct[:, b, :], start=b == 0, stop=b == B - 1)
            last.then_inc(cov_ps, 1)
            pe.wait_ge(cov_done, 1)
            pe.wait_ge(f_ld, 16 * 8)
            for n in range(NB):
                last = pe.matmul(ps[:, 1 + n // 4, (n % 4) * D:(n % 4 + 1) * D], f_wq[:, n * KD:(n + 1) * KD], cov[:, :], start=True, stop=True)
                if n % 4 == 3:
                    last.then_inc(cw_ps, 1)
            pe.wait_ge(gain_done, 2)
            pe.wait_ge(fc_done, 2)
            for n in range(NB):
                pe.matmul(ps[:, 5, n * KEYS:(n + 1) * KEYS], f_wqt[:, n, :], kscaled[:, n, :], start=True, stop=True)
                last = pe.matmul(ps[0:1, 6, n * KEYS:(n + 1) * KEYS], f_bet[:, n:n + 1], f_keys[:, n, :], start=True, stop=True)
            last.then_inc(simw_ps, 1)
            pe.wait_ge(simw_done, 2)

            def expert_rows(i, n, first):
                if n == 0:
                    pe.wait_ge(oneh_done, i * 1 + 1)
                if n >= 2 or not first:
                    pe.wait_ge(g_done, i * 4 + n - 1)
                for q in range(QP):
                    s = n * QP + q
                    dst = ps[:, 5 + n % 2, q * 2 * NC:(q + 1) * 2 * NC]
                    pe.matmul(dst, oneh[:, :, s], mv_hi[:, s, :], start=True, stop=False)
                    last = pe.matmul(dst, oneh[:, :, s], mv_lo[:, s, :], start=False, stop=True)
                last.then_inc(g_ps, 1)

            def add_experts(i, first):
                pe.wait_ge(g_done, i * 4 + 4)
                if not first:
                    pe.wait_ge(z_done, i * 4 - 3)
                for hf in range(2):
                    for c in range(NC):
                        last = pe.matmul(ps[0:S, 7, hf * D:(hf + 1) * D], wgt[:, c, hf, :], f_up[:, c, :], start=c == 0, stop=c == NC - 1)
                last.then_inc(y_ps, 1)

            def step(i, first, second):
                pe.wait_ge(fcur_done, i * 2 + 2)
                if not first:
                    pe.wait_ge(sim_done, i * 1)
                for hf in range(2):
                    pe.matmul(ps[0:S, hf, :], xc_cur[:, hf, :], sim_w[:, :], start=True, stop=False)
                    pe.matmul(ps[0:S, hf, :], ones_r[:, :], sim_c[:, :], start=False, stop=True).then_inc(sim_ps, 1)
                for r in range(2):
                    if r or not first:
                        pe.wait_ge(gel_done, i * 2 + r)
                    for c in range(4):
                        last = pe.matmul(ps[:, 2 + c // 2, (c % 2) * 2 * S:(c % 2 + 1) * 2 * S],
                                         f_down[:, (4 * r + c) * P:(4 * r + c + 1) * P], x2_cur[:, :], start=True, stop=True)
                    last.then_inc(h_ps, 1)
                    if not first:
                        for n in (2 * r, 2 * r + 1):
                            expert_rows(i - 1, n, second)
                pe.wait_ge(sel_done, i * 6 + 6)
                if not first:
                    pe.wait_ge(wlo_done, i * 2)
                for n in range(3):
                    last = pe.transpose(ps[:, 4, n * S:(n + 1) * S], sel[:, n, :, :].rearrange("s a k -> s (a k)"), ident[0:S, 0:S])
                last.then_inc(selT_ps, 1)
                if not first:
                    add_experts(i - 1, second)

            step(0, True, False)
            step(1, False, True)
            with pe.Fori(2, NPAIR) as i:
                step(i, False, False)
            for n in range(4):
                expert_rows(NPAIR - 1, n, False)
            add_experts(NPAIR - 1, False)


def decoder(nc, a, out):
    with ExitStack() as whole, ExitStack() as part:
        def sb(name, shape, dt=F32, until=whole):
            return until.enter_context(nc.sbuf_tensor(name, shape, dt))

        ps = whole.enter_context(nc.psum_tensor("ps", [P, 8, 512], F32))
        m = {
            "ident": sb("ident", [P, P]), "nhalf": sb("nhalf", [P, B]),
            "x2": sb("x2", [S, B, D]),
            "ident16": sb("ident16", [P, P], F16, part),
            "qa": sb("qa", [D, H, D], F32, part),
            "w2h": sb("w2h", [D, H, D + 1], F32, part),
            "sc1": sb("sc1", [D, B, H], F32, part),
            "kb": sb("kb", [D, B, H], F32, part),
            "x1": sb("x1", [S, B, D], F32, part),
            "lnT": sb("lnT", [D, NT], F32, part),
        }
        front(nc, a, m, ps)
        cross(nc, a, m, ps)
        part.close()
        ffn(nc, a, m, ps, out)


def kernel(**inputs):
    import numpy as np
    import concourse.bacc as bacc
    from concourse.bass_utils import run_bass_kernel_spmd

    half = D // 2
    angle = np.arange(S)[None, :] / np.power(10000.0, np.arange(half) / half)[:, None]
    cos, sin = np.round(np.cos(angle)).astype(np.float32), np.round(np.sin(angle)).astype(np.float32)
    arrays = {n: np.asarray(v) for n, v in inputs.items()}
    for n in ("L0_attn_g_norm", "L0_attn_b_qkv", "L0_attn_b_proj", "L0_xattn_ln1_w", "L0_xattn_ln1_b",
              "L0_xattn_ln2_w", "L0_xattn_ln2_b"):
        arrays[n] = arrays[n].reshape(-1, 1)
    wkv = arrays.pop("L0_xattn_Wkv")
    arrays["wk_t"], arrays["wv_t"] = wkv[:, :H * DH].T, wkv[:, H * DH:].T
    arrays["wq_t"] = arrays.pop("L0_xattn_Wq").T
    arrays["ffn_wq_t"] = arrays["L0_ffn_w_q"].T
    arrays["ffn_keys_t"] = arrays.pop("L0_ffn_keys").transpose(3, 2, 0, 1)
    arrays["ffn_down_t"] = arrays.pop("L0_ffn_down_embed").T
    arrays["L0_ffn_bn_gamma"] = arrays["L0_ffn_bn_gamma"].reshape(NB, KD).T
    arrays["L0_ffn_bn_beta"] = arrays["L0_ffn_bn_beta"].reshape(NB, KD).T
    arrays["cos_t"] = np.concatenate([cos, cos])
    arrays["sin_t"] = np.concatenate([-sin, sin])

    nc = bacc.Bacc("TRN2", target_bir_lowering=False, num_devices=1)
    feed, aps = {}, {}
    for n, v in arrays.items():
        v = np.ascontiguousarray(v)
        feed[f"in_{n}"] = v
        aps[n] = nc.dram_tensor(f"in_{n}", v.shape, mybir.dt.from_np(v.dtype), kind="ExternalInput").ap()
    out = nc.dram_tensor("out_x", (B, S, D), F32, kind="ExternalOutput").ap()
    decoder(nc, aps, out)
    r = run_bass_kernel_spmd(nc, [feed], core_ids=[0])
    return r.results[0]["out_x"]
```

```python
from contextlib import ExitStack

import concourse.bass as bass
from concourse import mybir

F32 = mybir.dt.float32
F16 = mybir.dt.float16
BF16 = mybir.dt.bfloat16
U32 = mybir.dt.uint32
ALU = mybir.AluOpType
ACT = mybir.ActivationFunctionType
AX_X = mybir.AxisListType.X

P = 128
B, S, D = 16, 100, 128
NT = B * S
G = 4
NG = B // G
T = 1444
TF = T // P
TR = T - TF * P
NTILE = TF + 1
H, DH = 16, 64
HQ = H * S
HALF = HQ // 2
CH = HALF // 2
NM = (HQ + P - 1) // P
LN3 = 1.0986122886681098
ATT_SCALE = LN3 / float(D) ** 0.5
EPS_RMS, EPS = 1e-6, 1e-5
HEADROOM = 6.0
FH, KEYS, KD, NE = 8, 32, 128, 1024
NB = 2 * FH


def front(nc, a, m, ps):
    with ExitStack() as ctx:
        def sb(name, shape, dt=F32):
            return ctx.enter_context(nc.sbuf_tensor(name, shape, dt))

        def sem(name):
            return ctx.enter_context(nc.semaphore(name))

        x_tok = sb("x_tok", [S, B, D])
        w_qkv = sb("w_qkv", [D, 3 * D])
        w_swap = sb("w_swap", [D, 2 * D])
        b_qkv = sb("b_qkv", [D, 3])
        b_swap = sb("b_swap", [D, 2])
        g_col = sb("g_col", [D, 1])
        w_proj = sb("w_proj", [D, D])
        bp_row = sb("bp_row", [S, D])
        cos_t = sb("cos_t", [D, S])
        sin_t = sb("sin_t", [D, S])
        w2_col = sb("w2_col", [D, 1])
        b2_col = sb("b2_col", [D, 1])
        sq = sb("sq", [S, B, D])
        ms = sb("ms", [S, B])
        rr = sb("rr", [S, B])
        xr = sb("xr", [S, B, D])
        x2b = sb("x2b", [S, B, D])
        hT = sb("hT", [D, NT])
        rot_a = sb("rot_a", [D, G, S])
        rot_b = sb("rot_b", [D, G, S])
        qT = sb("qT", [D, NT])
        kT = sb("kT", [D, NT])
        v_sb = sb("v_sb", [S, B, D])
        mx = sb("mx", [S, B])
        nb = sb("nb", [S, B])
        rs = sb("rs", [S, B])
        rc = sb("rc", [S, B])
        prob = sb("prob", [S, B, S])
        probT = sb("probT", [S, B, S])
        oT = sb("oT", [D, NT])
        z = sb("z", [S, B, D])
        bst = sb("bst", [S, B, 6])
        mv = sb("mv", [S, B, 2])
        ve = sb("ve", [S, B])
        rstd = sb("rstd", [S, B])
        wq_t = sb("wq_t", [DH, H, D])
        wk_t = sb("wk_t", [DH, H, D])
        wv_t = sb("wv_t", [DH, H, D])
        wout = sb("wout", [DH, H, D])
        wk_f = sb("wk_f", [DH, H, D])
        wv_f = sb("wv_f", [DH, H, D])
        wtmp = sb("wtmp", [DH, H, D])
        vb = sb("vb", [DH, H])
        w1_row = sb("w1_row", [DH, D])
        b1_row = sb("b1_row", [DH, D])
        ones_c = sb("ones_c", [DH, 1])
        side = sb("side", [D, B, H])
        kbar = sb("kbar", [D, H])

        ident, ident16, nhalf = m["ident"], m["ident16"], m["nhalf"]
        qa, w2h, sc1, kb, x1, lnT = m["qa"], m["w2h"], m["sc1"], m["kb"], m["x1"], m["lnT"]

        ld_x, ld_att, ld_fold, ld_side = sem("ld_x"), sem("ld_att"), sem("ld_fold"), sem("ld_side")
        ident_done, const_done = sem("ident_done"), sem("const_done")
        sq_done, ms_done, rr_done, xr_done = sem("sq_done"), sem("ms_done"), sem("rr_done"), sem("xr_done")
        x2b_done = sem("x2b_done")
        hT_ps, hT_done = sem("hT_ps"), sem("hT_done")
        qk_ps, rot_done, qk_done = sem("qk_ps"), sem("rot_done"), sem("qk_done")
        v_ps, v_done = sem("v_ps"), sem("v_done")
        sc_ps, mx_done, nb_done, exp_done = sem("sc_ps"), sem("mx_done"), sem("nb_done"), sem("exp_done")
        rc_done, prob_done, pT_ps, pT_done = sem("rc_done"), sem("prob_done"), sem("pT_ps"), sem("pT_done")
        o_ps, o_done, y_ps, z_done = sem("o_ps"), sem("o_done"), sem("y_ps"), sem("z_done")
        st_done, ag_done, ve_done = sem("st_done"), sem("ag_done"), sem("ve_done")
        rstd_done, norm_done = sem("rstd_done"), sem("norm_done")
        ln_ps, ln_done = sem("ln_ps"), sem("ln_done")
        kmul_done, kfold_done, vmul_done, vfold_done = sem("kmul_done"), sem("kfold_done"), sem("vmul_done"), sem("vfold_done")
        qa_ps, qa_done, kb_ps, kbar_done, w2_ps, w2_done = (sem(n) for n in ("qa_ps", "qa_done", "kb_ps", "kbar_done", "w2_ps", "w2_done"))
        side_done = sem("side_done")

        block = ctx.enter_context(nc.Block())

        def bank(k, parts, shape):
            names = " ".join("abc"[: len(shape)])
            n = 1
            for s in shape:
                n *= s
            v = ps[0:parts, k, 0:n]
            if len(shape) == 1:
                return v
            return v.rearrange(f"p ({names}) -> p {names}", **dict(zip("abc", shape)))

        @block.sync
        def _(sp):
            sp.dma_start(x_tok[:, :, :], a["x"].rearrange("b s d -> s b d")).then_inc(ld_x, 16)
            sp.dma_start(w_qkv[:, :], a["L0_attn_w_qkv"]).then_inc(ld_att, 16)
            for n in range(2):
                for half in range(2):
                    src = n * D + (1 - half) * (D // 2)
                    dst = n * D + half * (D // 2)
                    sp.dma_start(w_swap[:, dst:dst + D // 2],
                                 a["L0_attn_w_qkv"][:, src:src + D // 2]).then_inc(ld_att, 16)
                    sp.dma_start(b_swap[half * (D // 2):(half + 1) * (D // 2), n:n + 1],
                                 a["L0_attn_b_qkv"][src:src + D // 2, :]).then_inc(ld_att, 16)
            for n in range(3):
                sp.dma_start(b_qkv[:, n:n + 1], a["L0_attn_b_qkv"][n * D:(n + 1) * D, :]).then_inc(ld_att, 16)
            sp.dma_start(g_col[:, :], a["L0_attn_g_norm"]).then_inc(ld_att, 16)
            sp.dma_start(cos_t[:, :], a["cos_t"]).then_inc(ld_att, 16)
            sp.dma_start(sin_t[:, :], a["sin_t"]).then_inc(ld_att, 16)
            sp.dma_start(w_proj[:, :], a["L0_attn_w_proj"]).then_inc(ld_att, 16)
            sp.dma_start(bp_row[:, :], a["L0_attn_b_proj"].rearrange("d a -> a d").to_broadcast([S, D])).then_inc(ld_att, 16)
            sp.dma_start(w2_col[:, :], a["L0_xattn_ln2_w"]).then_inc(ld_att, 16)
            sp.dma_start(b2_col[:, :], a["L0_xattn_ln2_b"]).then_inc(ld_att, 16)
            ld = [(wk_t, a["wk_t"].rearrange("(h c) d -> c h d", c=DH)),
                  (wq_t, a["wq_t"].rearrange("(h c) d -> c h d", c=DH)),
                  (wv_t, a["wv_t"].rearrange("(h c) d -> c h d", c=DH)),
                  (wout, a["L0_xattn_Wout"].rearrange("(h c) n -> c h n", c=DH))]
            sp.dma_start(w1_row[:, :], a["L0_xattn_ln1_w"].rearrange("d a -> a d").to_broadcast([DH, D])).then_inc(ld_fold, 16)
            sp.dma_start(b1_row[:, :], a["L0_xattn_ln1_b"].rearrange("d a -> a d").to_broadcast([DH, D])).then_inc(ld_fold, 16)
            for dst, src in ld:
                sp.dma_start(dst[:, :, :], src).then_inc(ld_fold, 16)
            sp.dma_start(side[:, :, :].rearrange("p b h -> p (b h)"),
                         a["fside_Bx16_0"].rearrange("b h -> (b h)").rearrange("(a n) -> a n", a=1).to_broadcast([D, B * H])).then_inc(ld_side, 16)

        LD_ATT, LD_FOLD = 16 * 19, 16 * 6

        @block.gpsimd
        def _(pool):
            pool.memset(ident[:, :], 0.0).then_inc(ident_done, 1)
            pool.memset(ident16[:, :], 0.0).then_inc(ident_done, 1)
            pool.memset(nhalf[:, :], -0.5).then_inc(ident_done, 1)
            pool.memset(ones_c[:, :], 1.0).then_inc(ident_done, 1)
            pool.wait_ge(ident_done, 4)
            for t in (ident, ident16):
                pool.affine_select(out=t[:, :], in_=t[:, :], compare_op=ALU.not_equal, fill=1.0, base=0,
                                   pattern=[[-1, P]], channel_multiplier=1).then_inc(const_done, 1)
            pool.wait_ge(ms_done, 1)
            pool.tensor_tensor(out=rr[:, :], in0=ms[:, :], in1=nhalf[0:S, 0:B], op=ALU.pow).then_inc(rr_done, 1)
            pool.wait_ge(ld_fold, LD_FOLD)
            pool.tensor_tensor(out=wtmp[:, :, :], in0=wk_t[:, :, :],
                               in1=w1_row[:, :].rearrange("c (a d) -> c a d", a=1).to_broadcast([DH, H, D]), op=ALU.mult).then_inc(kmul_done, 1)
            pool.wait_ge(kmul_done, 1)
            pool.memset(wk_f[:, :, 0:1], 0.0).then_inc(kfold_done, 1)
            pool.tensor_tensor(out=wk_f[:, :, 1:D], in0=wtmp[:, :, 1:D],
                               in1=wtmp[:, :, 0:1].to_broadcast([DH, H, D - 1]), op=ALU.subtract).then_inc(kfold_done, 1)
            for c in range(NG):
                for k in range(2):
                    pool.wait_ge(ve_done, 2 * c + k + 1)
                    pool.tensor_tensor(out=rstd[:, c * G:(c + 1) * G], in0=ve[:, c * G:(c + 1) * G],
                                       in1=nhalf[0:S, 0:G], op=ALU.pow).then_inc(rstd_done, 1)

        @block.scalar
        def _(act):
            for k in range(NG):
                act.wait_ge(qa_ps, k + 1)
                act.activation(qa[:, 4 * k:4 * k + 4, :], bank(4 + k, D, (4, D)), ACT.Copy, scale=DH ** -0.5).then_inc(qa_done, 1)
            act.wait_ge(kb_ps, 1)
            act.activation(kbar[:, :], bank(3, D, (H,)), ACT.Copy, scale=DH ** -0.5).then_inc(kbar_done, 1)
            for c in range(NG):
                act.wait_ge(v_ps, c + 1)
                act.activation(v_sb[:, c * G:(c + 1) * G, :], bank(c, S, (G, D)), ACT.Copy).then_inc(v_done, 1)
            for c in range(NG):
                act.wait_ge(nb_done, c + 1)
                for j in range(G):
                    b = c * G + j
                    act.activation(prob[:, b, :], bank(c, S, (G, S))[:, j, :], ACT.Exp, bias=nb[:, b:b + 1],
                                   scale=ATT_SCALE, accum_out=rs[:, b:b + 1]).then_inc(exp_done, 1)
            for c in range(NG):
                act.wait_ge(pT_ps, c + 1)
                act.activation(probT[:, c * G:(c + 1) * G, :], bank(4 + c, S, (G, S)), ACT.Copy).then_inc(pT_done, 1)
                act.wait_ge(o_ps, c + 1)
                act.activation(oT[:, c * G * S:(c + 1) * G * S], bank(c, D, (G * S,)), ACT.Identity,
                               bias=b_qkv[:, 2:3]).then_inc(o_done, 1)
            for k in range(NG):
                act.wait_ge(w2_ps, k + 1)
                act.activation(w2h[:, 4 * k:4 * k + 4, 0:D], bank(k, D, (4, D)), ACT.Copy).then_inc(w2_done, 1)

        @block.vector
        def _(dve):
            dve.wait_ge(ld_x, 16)
            dve.tensor_tensor(out=sq[:, :, :], in0=x_tok[:, :, :], in1=x_tok[:, :, :], op=ALU.mult).then_inc(sq_done, 1)
            dve.wait_ge(sq_done, 1)
            dve.tensor_reduce(ms[:, :], sq[:, :, :], AX_X, ALU.add).then_inc(sq_done, 1)
            dve.wait_ge(sq_done, 2)
            dve.tensor_scalar(ms[:, :], ms[:, :], 1.0 / D, EPS_RMS, ALU.mult, ALU.add).then_inc(ms_done, 1)
            dve.wait_ge(ld_att, LD_ATT)
            dve.scalar_tensor_tensor(out=x2b[:, :, :], in0=x_tok[:, :, :], scalar=2.0,
                                     in1=bp_row[:, :].rearrange("s (a d) -> s a d", a=1).to_broadcast([S, B, D]),
                                     op0=ALU.mult, op1=ALU.add).then_inc(x2b_done, 1)
            dve.wait_ge(rr_done, 1)
            dve.tensor_tensor(out=xr[:, :, :], in0=x_tok[:, :, :],
                              in1=rr[:, :].rearrange("s (b a) -> s b a", a=1).to_broadcast([S, B, D]), op=ALU.mult).then_inc(xr_done, 1)
            for c in range(NG):
                dve.wait_ge(hT_ps, c + 1)
                dve.tensor_scalar(hT[:, c * G * S:(c + 1) * G * S], bank(c, D, (G * S,)), g_col[:, 0:1], None, ALU.mult).then_inc(hT_done, 1)
            dve.wait_ge(ld_fold, LD_FOLD)
            dve.tensor_tensor(out=wv_f[:, :, :], in0=wv_t[:, :, :],
                              in1=b1_row[:, :].rearrange("c (a d) -> c a d", a=1).to_broadcast([DH, H, D]), op=ALU.mult).then_inc(vmul_done, 1)
            dve.wait_ge(vmul_done, 1)
            dve.tensor_reduce(vb[:, :], wv_f[:, :, :], AX_X, ALU.add).then_inc(vmul_done, 1)
            dve.tensor_tensor(out=wv_t[:, :, :], in0=wv_t[:, :, :],
                              in1=w1_row[:, :].rearrange("c (a d) -> c a d", a=1).to_broadcast([DH, H, D]), op=ALU.mult).then_inc(vmul_done, 1)
            dve.wait_ge(vmul_done, 3)
            dve.tensor_tensor(out=wv_f[:, :, 1:D], in0=wv_t[:, :, 1:D],
                              in1=wv_t[:, :, 0:1].to_broadcast([DH, H, D - 1]), op=ALU.subtract).then_inc(vfold_done, 1)
            dve.tensor_copy(wv_f[:, :, 0:1], vb[:, :].rearrange("c (h a) -> c h a", a=1)).then_inc(vfold_done, 1)
            dve.memset(w2h[:, :, D:D + 1], 0.0).then_inc(vfold_done, 1)
            dve.wait_ge(vfold_done, 3)
            dve.memset(w2h[0:1, :, D:D + 1], 1.0).then_inc(vfold_done, 1)
            for c in range(NG):
                for n, dst in enumerate((qT, kT)):
                    dve.wait_ge(qk_ps, 2 * c + n + 1)
                    if c or n:
                        dve.wait_ge(qk_done, 2 * c + n)
                    dve.scalar_tensor_tensor(out=rot_a[:, :, :], in0=bank(4 + 2 * n, D, (G, S)), scalar=b_qkv[:, n:n + 1],
                                             in1=cos_t[:, :].rearrange("d (a s) -> d a s", a=1).to_broadcast([D, G, S]),
                                             op0=ALU.add, op1=ALU.mult).then_inc(rot_done, 1)
                    dve.scalar_tensor_tensor(out=rot_b[:, :, :], in0=bank(5 + 2 * n, D, (G, S)), scalar=b_swap[:, n:n + 1],
                                             in1=sin_t[:, :].rearrange("d (a s) -> d a s", a=1).to_broadcast([D, G, S]),
                                             op0=ALU.add, op1=ALU.mult).then_inc(rot_done, 1)
                    dve.wait_ge(rot_done, 4 * c + 2 * n + 2)
                    dve.tensor_tensor(out=dst[:, c * G * S:(c + 1) * G * S].rearrange("d (a s) -> d a s", a=G),
                                      in0=rot_a[:, :, :], in1=rot_b[:, :, :], op=ALU.add).then_inc(qk_done, 1)
            for c in range(NG):
                cs = slice(c * G, (c + 1) * G)
                dve.wait_ge(sc_ps, c + 1)
                dve.tensor_reduce(mx[:, cs], bank(c, S, (G, S)), AX_X, ALU.max).then_inc(mx_done, 1)
                dve.wait_ge(mx_done, c + 1)
                dve.tensor_scalar(nb[:, cs], mx[:, cs], -ATT_SCALE, None, ALU.mult).then_inc(nb_done, 1)
            for c in range(NG):
                cs = slice(c * G, (c + 1) * G)
                dve.wait_ge(exp_done, (c + 1) * G)
                dve.reciprocal(rc[:, cs], rs[:, cs]).then_inc(rc_done, 1)
                dve.wait_ge(rc_done, c + 1)
                dve.tensor_tensor(out=prob[:, cs, :], in0=prob[:, cs, :],
                                  in1=rc[:, cs].rearrange("s (b a) -> s b a", a=1).to_broadcast([S, G, S]),
                                  op=ALU.mult).then_inc(prob_done, 1)
            for c in range(NG):
                cs = slice(c * G, (c + 1) * G)
                dve.wait_ge(y_ps, c + 1)
                dve.tensor_tensor(out=z[:, cs, :], in0=bank(4 + c, S, (G, D)), in1=x2b[:, cs, :], op=ALU.add).then_inc(z_done, 1)
                dve.wait_ge(z_done, c + 1)
                for k, (src, dst) in enumerate(((z, x1), (x1, sq))):
                    n = 2 * c + k
                    if n:
                        dve.wait_ge(norm_done, G * n)
                    for j in range(G):
                        dve.bn_stats(bst[:, c * G + j, :], src[:, c * G + j, :]).then_inc(st_done, 1)
                    dve.wait_ge(st_done, G * (n + 1))
                    for j in range(G):
                        dve.bn_aggr(mv[:, c * G + j, :], bst[:, c * G + j, :]).then_inc(ag_done, 1)
                    dve.wait_ge(ag_done, G * (n + 1))
                    dve.tensor_scalar(ve[:, cs], mv[:, cs, 1], EPS, None, ALU.add).then_inc(ve_done, 1)
                    dve.wait_ge(rstd_done, n + 1)
                    for j in range(G):
                        b = c * G + j
                        dve.tensor_scalar(dst[:, b, :], src[:, b, :], mv[:, b, 0:1], rstd[:, b:b + 1],
                                          ALU.subtract, ALU.mult).then_inc(norm_done, 1)
                dve.wait_ge(ln_ps, c + 1)
                dve.tensor_scalar(lnT[:, c * G * S:(c + 1) * G * S], bank(c, D, (G * S,)), w2_col[:, 0:1], b2_col[:, 0:1],
                                  ALU.mult, ALU.add).then_inc(ln_done, 1)
            dve.wait_ge(ld_side, 16)
            dve.tensor_scalar(sc1[:, :, :], side[:, :, :], 1.0, None, ALU.add).then_inc(side_done, 1)
            dve.wait_ge(kbar_done, 1)
            dve.tensor_tensor(out=kb[:, :, :], in0=side[:, :, :],
                              in1=kbar[:, :].rearrange("d (a h) -> d a h", a=1).to_broadcast([D, B, H]), op=ALU.mult).then_inc(side_done, 1)

        @block.tensor
        def _(pe):
            pe.wait_ge(const_done, 2)
            pe.wait_ge(xr_done, 1)
            for c in range(NG):
                for j in range(G):
                    last = pe.transpose(bank(c, D, (G, S))[:, j, :], xr[:, c * G + j, :], ident[0:S, 0:S])
                last.then_inc(hT_ps, 1)
            pe.wait_ge(kfold_done, 2)
            for k in range(NG):
                for j in range(4):
                    last = pe.matmul(bank(4 + k, D, (4, D))[:, j, :], wq_t[:, 4 * k + j, :], wk_f[:, 4 * k + j, :], start=True, stop=True)
                last.then_inc(qa_ps, 1)
            pe.wait_ge(hT_done, NG)
            for h in range(H):
                last = pe.matmul(bank(3, D, (H,))[:, h:h + 1], wk_f[:, h, :], ones_c[:, 0:1], start=True, stop=True)
            last.then_inc(kb_ps, 1)
            for c in range(NG):
                if c == NG - 1:
                    pe.wait_ge(kbar_done, 1)
                for j in range(G):
                    b = c * G + j
                    last = pe.matmul(bank(c, S, (G, D))[:, j, :], hT[:, b * S:(b + 1) * S], w_qkv[:, 2 * D:3 * D], start=True, stop=True)
                last.then_inc(v_ps, 1)
            pe.wait_ge(qa_done, NG)
            for c in range(NG):
                for n in range(2):
                    if c:
                        pe.wait_ge(qk_done, 2 * (c - 1) + n + 1)
                    cols = slice(c * G * S, (c + 1) * G * S)
                    pe.matmul(bank(4 + 2 * n, D, (G * S,)), w_qkv[:, n * D:(n + 1) * D], hT[:, cols], start=True, stop=True)
                    pe.matmul(bank(5 + 2 * n, D, (G * S,)), w_swap[:, n * D:(n + 1) * D], hT[:, cols], start=True, stop=True).then_inc(qk_ps, 1)
            for c in range(NG):
                pe.wait_ge(qk_done, 2 * (c + 1))
                pe.wait_ge(v_done, c + 1)
                for j in range(G):
                    bs = slice((c * G + j) * S, (c * G + j + 1) * S)
                    last = pe.matmul(bank(c, S, (G, S))[:, j, :], qT[:, bs], kT[:, bs], start=True, stop=True)
                last.then_inc(sc_ps, 1)
            for c in range(NG):
                pe.wait_ge(prob_done, c + 1)
                for j in range(G):
                    last = pe.transpose(bank(4 + c, S, (G, S))[:, j, :], prob[:, c * G + j, :], ident[0:S, 0:S])
                last.then_inc(pT_ps, 1)
                pe.wait_ge(pT_done, c + 1)
                for j in range(G):
                    b = c * G + j
                    last = pe.matmul(bank(c, D, (G, S))[:, j, :], v_sb[:, b, :], probT[:, b, :], start=True, stop=True)
                last.then_inc(o_ps, 1)
                pe.wait_ge(o_done, c + 1)
                for j in range(G):
                    b = c * G + j
                    last = pe.matmul(bank(4 + c, S, (G, D))[:, j, :], oT[:, b * S:(b + 1) * S], w_proj[:, :], start=True, stop=True)
                last.then_inc(y_ps, 1)
            for c in range(NG):
                pe.wait_ge(norm_done, G * (2 * c + 2))
                for j in range(G):
                    last = pe.transpose(bank(c, D, (G, S))[:, j, :], sq[:, c * G + j, :], ident[0:S, 0:S])
                last.then_inc(ln_ps, 1)
            pe.wait_ge(vfold_done, 4)
            for k in range(NG):
                pe.wait_ge(ln_done, k + 1)
                for j in range(4):
                    last = pe.matmul(bank(k, D, (4, D))[:, j, :], wv_f[:, 4 * k + j, :], wout[:, 4 * k + j, :], start=True, stop=True)
                last.then_inc(w2_ps, 1)


class Batch:

    def __init__(self, i, off):
        self.i, self.off = i, off

    def val(self, coef, const):
        v = coef * self.off + const
        return v if self.i is None else self.i * (2 * coef) + v

    def next(self, n=1):
        return Batch(self.i, self.off + n)

    def is_last(self):
        return self.i is None and self.off == B - 1

    @property
    def par(self):
        return self.off % 2

    def index(self):
        return self.val(1, 0)


def over_batches(eng, body):
    body(Batch(None, 0), True, False)
    with eng.Fori(0, (B - 2) // 2) as i:
        body(Batch(i, 1), False, False)
        body(Batch(i, 2), False, False)
    body(Batch(None, B - 1), False, True)


AHEAD = 9


def side_work(first, last):
    own = [("M", m, c) for m in range(AHEAD, NM) for c in range(3)]
    nxt = [("M", m, c) for m in range(AHEAD) for c in range(3)]
    w = {(u, n): [] for u in range(2) for n in range(NTILE)}

    def put(u, counts, works):
        for n, k in counts:
            w[u, n] += [works.pop(0) for _ in range(k)]

    if not last:
        put(0, ((1, 1), (2, 1), (3, 1), (4, 1)), [("q", g) for g in range(4)])
        put(0, ((10, 1), (11, 1)), [("T", 0), ("T", 1)])
        put(1, ((0, 1), (1, 1)), [("T", 2), ("T", 3)])
        put(1, ((1, 3), (2, 4), (3, 4), (4, 4), (5, 3), (6, 3), (7, 2)), nxt)
        w[1, 7] += [("R", 0), ("R", 1)]
        put(1, ((8, 1), (9, 1), (10, 1), (11, 1)), nxt)
    if not first:
        put(0, ((8, 1), (9, 1), (10, 1)), [("Y", 1, g) for g in range(3)])
    put(0, ((0, 2), (1, 2), (2, 2), (3, 1), (4, 1), (5, 2), (6, 2)), own)
    w[0, 7] += [("R", 2), ("R", 3)]
    put(1, ((9, 1), (10, 1), (11, 1)), [("Y", 0, g) for g in range(3)])
    return w


START_WORK = ([("q", g) for g in range(4)] + [("T", j) for j in range(4)]
              + [("M", m, c) for m in range(AHEAD) for c in range(3)] + [("R", 0), ("R", 1)])
WORKS, ACTS = 57, 8
TAIL_WORK = [("Y", 1, g) for g in range(3)]


class Works:

    def __init__(self, bt, first, last, start=False, tail=False):
        self.bt, self.tail = bt, tail
        if start:
            self.base, self.base_dve, self.base_act = (0, 0), (0, 0), (0, 0)
            flat = [(None, w) for w in START_WORK]
        else:
            n = len(START_WORK)
            if first:
                self.base, self.base_dve = (0, n), (0, n - ACTS)
            else:
                self.base, self.base_dve = (WORKS, n - 3), (WORKS - ACTS, n - 3 - ACTS)
            self.base_act = (ACTS, ACTS)
            if tail:
                lost = ACTS + 3 * AHEAD + 2
                self.base = (WORKS, n - 3 - lost)
                self.base_dve = (WORKS - ACTS, n - 3 - ACTS - (lost - ACTS))
                self.base_act = (ACTS, 0)
                flat = [(None, w) for w in TAIL_WORK]
            else:
                plan = side_work(first, last)
                flat = [(k, w) for k in sorted(plan) for w in plan[k]]
        self.flat = flat

    def number(self, k):
        return self.bt.val(self.base[0], self.base[1] + k)

    def bank(self, k):
        c, n = self.base
        return (c * self.bt.off + n + k) % 2

    def is_act(self, k):
        return self.flat[k][1][0] in ("q", "T")

    def taken(self, k):
        acts = sum(self.is_act(j) for j in range(k + 1)) if k >= 0 else 0
        if k >= 0 and self.is_act(k):
            return self.bt.val(self.base_act[0], self.base_act[1] + acts)
        return self.bt.val(self.base_dve[0], self.base_dve[1] + k + 1 - acts)

    def at(self, key):
        return [(k, w) for k, (s, w) in enumerate(self.flat) if s == key]

    def find(self, work):
        return next(k for k, (_, w) in enumerate(self.flat) if w == work)


LEAD = 4
E_SLOTS, P_SLOTS = 4, 6
POOL_TILES = ((0, 2, 5, 8, 10), (0, 2, 4, 6, 8, 10))
MCUT = (0, 482, 963, T)
Y_HEADS = ((0, 1, 2), (3, 4, 5), (6, 7))


def lo_count(bt, u, n):
    both = len(POOL_TILES[0]) + len(POOL_TILES[1])
    pool = (len(POOL_TILES[0]) if u else 0) + sum(k <= n for k in POOL_TILES[u])
    if n in POOL_TILES[u]:
        return bt.val(both, pool)
    return bt.val(2 * NTILE - both, NTILE * u + n + 1 - pool)


def tile_number(bt, u, n):
    return bt.val(2 * NTILE, NTILE * u + n)


def rows_of(n):
    return P if n < TF else TR


def cross(nc, a, m, ps):
    with ExitStack() as ctx:
        def sb(name, shape, dt=F32):
            return ctx.enter_context(nc.sbuf_tensor(name, shape, dt))

        def sem(name):
            return ctx.enter_context(nc.semaphore(name))

        ident16, nhalf = m["ident16"], m["nhalf"]
        qa, w2h, sc1, kb, x1, lnT, x2 = m["qa"], m["w2h"], m["sc1"], m["kb"], m["x1"], m["lnT"], m["x2"]
        raw = [sb(f"raw{i}", [P, NTILE, D]) for i in range(2)]
        cst = sb("cst", [P, NTILE, 6])
        cmv = [sb(f"cmv{i}", [P, NTILE, 2]) for i in range(2)]
        cve = sb("cve", [P, NTILE])
        crs = [sb(f"crs{i}", [P, NTILE]) for i in range(2)]
        xh = sb("xh", [P, NTILE, D])
        xa_hi = [sb(f"xa_hi{i}", [P, NTILE, D], F16) for i in range(2)]
        xa_lo = [sb(f"xa_lo{i}", [P, NTILE, D], F16) for i in range(2)]
        xT_hi = [sb(f"xT_hi{i}", [D, NTILE * P], F16) for i in range(2)]
        xT_lo = [sb(f"xT_lo{i}", [D, NTILE * P], F16) for i in range(2)]
        ln_cur, sc_cur, kb_cur = sb("ln_cur", [D, S]), sb("sc_cur", [D, H]), sb("kb_cur", [D, H])
        q32 = sb("q32", [D, HQ])
        q_hi = [sb(f"q_hi{i}", [D, HQ], F16) for i in range(2)]
        q_lo = [sb(f"q_lo{i}", [D, HQ], F16) for i in range(2)]
        mxp = sb("mxp", [P, NM, 3])
        nm = sb("nm", [P, NM], F16)
        e32 = [sb(f"e32_{i}", [P, 2, CH]) for i in range(E_SLOTS)]
        p_hi = [sb(f"p_hi{i}", [P, 2, CH], F16) for i in range(P_SLOTS)]
        p_lo = [sb(f"p_lo{i}", [P, 2, CH], F16) for i in range(P_SLOTS)]
        uT = [sb(f"uT{i}", [D, 2, CH]) for i in range(2)]
        ry = sb("ry", [S, H])
        acc = sb("acc", [S, D])
        yst, ymv, yve, yrs = sb("yst", [S, 6]), sb("ymv", [S, 2]), sb("yve", [S, 1]), sb("yrs", [S, 1])

        ctx_ld = [sem(f"ctx_ld{i}") for i in range(2)]
        init_done, ctx_stat, ctx_rstd, xh_done = sem("init_done"), sem("ctx_stat"), sem("ctx_rstd"), sem("xh_done")
        xa_hi_done, xa_lo_done, cur_done = sem("xa_hi_done"), sem("xa_lo_done"), sem("cur_done")
        q_hi_done, q_lo_done = sem("q_hi_done"), sem("q_lo_done")
        work_rdy, work_dve, work_act, nm_done = sem("work_rdy"), sem("work_dve"), sem("work_act"), sem("nm_done")
        s_rdy, exp_done, lo_dve, lo_pool = sem("s_rdy"), sem("exp_done"), sem("lo_dve"), sem("lo_pool")
        pv_done, u_done, y_chain, y_norm, y_rstd = (sem(n) for n in ("pv_done", "u_done", "y_chain", "y_norm", "y_rstd"))

        pool_waited, dve_waited = sem("pool_waited"), sem("dve_waited")

        block = ctx.enter_context(nc.Block())

        def s_banks(n, rows):
            return ps[0:rows, 2 * (n % 2):2 * (n % 2) + 2, 0:CH]

        def wbank(w, k):
            return ps[:, 6 + w.bank(k), :]

        @block.sync
        def _(sp):
            def load(bt):
                src = a["ctx_1024"][bass.ds(bt.index(), 1), :, :].rearrange("a t d -> (a t) d")
                sp.dma_start(raw[bt.par][:, 0:TF, :],
                             src[0:TF * P, :].rearrange("(p j) d -> p j d", j=TF)).then_inc(ctx_ld[bt.par], 16)
                sp.dma_start(raw[bt.par][0:TR, TF, :], src[TF * P:T, :]).then_inc(ctx_ld[bt.par], 16)

            load(Batch(None, 0))
            load(Batch(None, 1))
            with sp.Fori(1, B // 2) as i:
                for off in range(2):
                    bt = Batch(i, off)
                    sp.wait_ge(xh_done, bt.val(1, -1))
                    load(bt)

        @block.gpsimd
        def _(pool):
            def current(bt):
                x = bt.index()
                pool.tensor_copy(ln_cur[:, :], lnT[:, bass.ds(bt.val(S, 0), S)])
                pool.tensor_copy(sc_cur[:, :], sc1[:, bass.ds(x, 1), :].rearrange("d a h -> d (a h)"))
                pool.tensor_copy(kb_cur[:, :], kb[:, bass.ds(x, 1), :].rearrange("d a h -> d (a h)")).then_inc(cur_done, 1)

            def rstd_ctx(bt):
                pool.wait_ge(ctx_stat, bt.val(3, 3))
                if bt.off >= 2:
                    pool.wait_ge(xh_done, bt.val(1, -1))
                pool.tensor_tensor(out=crs[bt.par][:, :], in0=cve[:, :], in1=nhalf[:, 0:NTILE], op=ALU.pow).then_inc(ctx_rstd, 1)

            def queries_lo(bt, g):
                cols = slice(g * CH, (g + 1) * CH)
                pool.wait_ge(q_hi_done, bt.val(4, g + 1))
                if bt.off >= 2:
                    pool.wait_ge(s_rdy, bt.val(2 * NTILE, -2 * NTILE))
                pool.tensor_tensor(out=q_lo[bt.par][:, cols], in0=q32[:, cols], in1=q_hi[bt.par][:, cols],
                                   op=ALU.subtract).then_inc(q_lo_done, 1)

            def context_lo(bt):
                pool.wait_ge(xa_hi_done, bt.val(1, 1))
                if bt.off >= 2:
                    pool.wait_ge(pv_done, bt.val(2 * NTILE, -2 * NTILE))
                pool.tensor_tensor(out=xa_lo[bt.par][:, :, :], in0=xh[:, :, :], in1=xa_hi[bt.par][:, :, :],
                                   op=ALU.subtract).then_inc(xa_lo_done, 1)

            def low_half(bt, u, n):
                t, r = NTILE * u + n, rows_of(n)
                pool.wait_ge(exp_done, bt.val(4 * NTILE, 2 * t + 2))
                if bt.off or t >= P_SLOTS:
                    pool.wait_ge(pv_done, bt.val(2 * NTILE, t - P_SLOTS + 1))
                pool.tensor_tensor(out=p_lo[t % P_SLOTS][0:r, :, :], in0=e32[t % E_SLOTS][0:r, :, :], in1=p_hi[t % P_SLOTS][0:r, :, :],
                                   op=ALU.subtract).then_inc(lo_pool, 1)

            def y_rstd_pow(bt):
                pool.wait_ge(y_norm, bt.val(4, 3))
                pool.tensor_tensor(out=yrs[:, :], in0=yve[:, :], in1=nhalf[0:S, 0:1], op=ALU.pow).then_inc(y_rstd, 1)

            def one_batch(bt, first, last):
                nx = bt.next()
                if not last:
                    current(nx)
                for n in POOL_TILES[0]:
                    low_half(bt, 0, n)
                    if n == 2 and not last:
                        queries_lo(nx, 0)
                        queries_lo(nx, 1)
                    if n == 5 and not last:
                        rstd_ctx(nx)
                        queries_lo(nx, 2)
                        queries_lo(nx, 3)
                if not last:
                    context_lo(nx)
                for n in POOL_TILES[1]:
                    low_half(bt, 1, n)
                    if n == 0 and not first:
                        y_rstd_pow(bt.next(-1))

            b0 = Batch(None, 0)
            pool.memset(xh[:, :, :], 1.0).then_inc(init_done, 1)
            for i in range(2):
                pool.memset(cmv[i][:, :, :], 1.0).then_inc(init_done, 1)
            pool.memset(mxp[:, :, :], 0.0).then_inc(init_done, 1)
            current(b0)
            rstd_ctx(b0)
            context_lo(b0)
            for g in range(4):
                queries_lo(b0, g)
            over_batches(pool, one_batch)
            y_rstd_pow(Batch(None, B - 1))

        @block.scalar
        def _(act):
            def take_transposes(bt, w, k):
                j = w.flat[k][1][1]
                dst = (xT_hi, xT_lo)[j // 2][bt.par]
                c0, c1 = ((0, 8 * P), (8 * P, T))[j % 2]
                act.wait_ge(work_rdy, w.number(k) + 1)
                act.activation(dst[:, c0:c1], wbank(w, k).bitcast(F16)[:, 0:c1 - c0], ACT.Copy).then_inc(work_act, 1)

            def take_queries(bt, w, k):
                g = w.flat[k][1][1]
                act.wait_ge(cur_done, bt.val(1, 1))
                if bt.off >= 1:
                    act.wait_ge(q_lo_done, bt.val(4, -4 + g + 1))
                act.wait_ge(work_rdy, w.number(k) + 1)
                for j in range(4):
                    h = 4 * g + j
                    ins = act.activation(q32[:, h * S:(h + 1) * S], wbank(w, k)[:, j * S:(j + 1) * S], ACT.Identity,
                                         bias=kb_cur[:, h:h + 1], scale=sc_cur[:, h:h + 1])
                ins.then_inc(work_act, 1)
                if bt.off >= 2:
                    act.wait_ge(s_rdy, bt.val(2 * NTILE, -2 * NTILE))
                act.wait_ge(work_act, w.taken(k))
                cols = slice(g * CH, (g + 1) * CH)
                act.activation(q_hi[bt.par][:, cols], q32[:, cols], ACT.Copy).then_inc(q_hi_done, 1)

            def context_hi(bt):
                act.wait_ge(xh_done, bt.val(1, 1))
                if bt.off >= 2:
                    act.wait_ge(pv_done, bt.val(2 * NTILE, -2 * NTILE))
                act.activation(xa_hi[bt.par][:, :, :], xh[:, :, :], ACT.Copy).then_inc(xa_hi_done, 1)

            def take_values(bt, u):
                act.wait_ge(pv_done, bt.val(2 * NTILE, NTILE * (u + 1)))
                if bt.off or bt.i is not None:
                    w = Works(bt, False, bt.is_last()) if u else Works(bt.next(-1), False, False)
                    act.wait_ge(work_rdy, w.number(w.find(("Y", u, 2))) + 1)
                for c in range(2):
                    act.activation(uT[u][:, c, :], ps[:, 4 + c, 0:CH], ACT.Copy).then_inc(u_done, 1)

            def one_batch(bt, first, last):
                w = Works(bt, first, last)
                for u in range(2):
                    for n in range(NTILE):
                        t, r = NTILE * u + n, rows_of(n)
                        act.wait_ge(s_rdy, bt.val(2 * NTILE, t + 1))
                        if not first or t >= E_SLOTS:
                            pb, pt = (bt, t - E_SLOTS) if t >= E_SLOTS else (bt.next(-1), t - E_SLOTS + 2 * NTILE)
                            pu, pn = divmod(pt, NTILE)
                            act.wait_ge(lo_pool if pn in POOL_TILES[pu] else lo_dve, lo_count(pb, pu, pn))
                        act.activation(e32[t % E_SLOTS][0:r, :, :], s_banks(t, r), ACT.Exp).then_inc(exp_done, 1)
                        if not first or t >= P_SLOTS:
                            act.wait_ge(pv_done, bt.val(2 * NTILE, t - P_SLOTS + 1))
                        act.activation(p_hi[t % P_SLOTS][0:r, :, :], s_banks(t, r), ACT.Exp).then_inc(exp_done, 1)
                        if t >= LEAD - 2:
                            for k, x in w.at(divmod(t - LEAD + 2, NTILE)):
                                if x[0] == "T":
                                    take_transposes(bt.next(), w, k)
                                elif x[0] == "q":
                                    take_queries(bt.next(), w, k)
                        if t == 9 and not last:
                            context_hi(bt.next())
                        if n == LEAD - 3:
                            if u:
                                take_values(bt, 0)
                            elif not first:
                                take_values(bt.next(-1), 1)

            w0 = Works(Batch(None, 0), False, False, start=True)
            context_hi(Batch(None, 0))
            for k, (_, x) in enumerate(w0.flat):
                if x[0] == "T":
                    take_transposes(Batch(None, 0), w0, k)
                elif x[0] == "q":
                    take_queries(Batch(None, 0), w0, k)
            over_batches(act, one_batch)
            take_values(Batch(None, B - 1), 1)

        @block.vector
        def _(dve):
            def stats(bt, part):
                if part == 0:
                    dve.wait_ge(ctx_ld[bt.par], bt.val(16, 32 - 16 * bt.par))
                    if bt.off >= 2:
                        dve.wait_ge(xh_done, bt.val(1, -1))
                        dve.wait_ge(ctx_rstd, bt.val(1, 0))
                if part < 3:
                    for n in range(4 * part, 4 * part + 4):
                        r = rows_of(n)
                        ins = dve.bn_stats(cst[0:r, n, :], raw[bt.par][0:r, n, :])
                    if part == 2:
                        ins.then_inc(ctx_stat, 1)
                else:
                    dve.wait_ge(ctx_stat, bt.val(3, 1))
                    dve.sem_inc(dve_waited, 1)
                    for n in range(NTILE):
                        r = rows_of(n)
                        ins = dve.bn_aggr(cmv[bt.par][0:r, n, :], cst[0:r, n, :])
                    ins.then_inc(ctx_stat, 1)
                    dve.wait_ge(ctx_stat, bt.val(3, 2))
                    if bt.off >= 1:
                        dve.wait_ge(ctx_rstd, bt.val(1, 0))
                    dve.tensor_scalar(cve[:, :], cmv[bt.par][:, :, 1], EPS, None, ALU.add).then_inc(ctx_stat, 1)

            def normalise(bt, part):
                if part == 0:
                    dve.wait_ge(ctx_rstd, bt.val(1, 1))
                    if bt.off >= 1:
                        dve.wait_ge(xa_lo_done, bt.val(1, 0))
                for n in range(4 * part, 4 * part + 4):
                    r = rows_of(n)
                    ins = dve.tensor_scalar(xh[0:r, n, 1:D], raw[bt.par][0:r, n, 1:D], cmv[bt.par][0:r, n, 0:1],
                                            crs[bt.par][0:r, n:n + 1], ALU.subtract, ALU.mult)
                if part == 2:
                    ins.then_inc(xh_done, 1)

            def low_half(bt, u, n):
                t, r = NTILE * u + n, rows_of(n)
                dve.wait_ge(exp_done, bt.val(4 * NTILE, 2 * t + 2))
                if bt.off or t >= P_SLOTS:
                    dve.wait_ge(pv_done, bt.val(2 * NTILE, t - P_SLOTS + 1))
                dve.tensor_tensor(out=p_lo[t % P_SLOTS][0:r, :, :], in0=e32[t % E_SLOTS][0:r, :, :], in1=p_hi[t % P_SLOTS][0:r, :, :],
                                  op=ALU.subtract).then_inc(lo_dve, 1)

            def take(bt, nx, w, k):
                x = w.flat[k][1]
                src = wbank(w, k)
                dve.wait_ge(work_rdy, w.number(k) + 1)
                if x[0] == "M":
                    mt, c = x[1:]
                    r = min(P, HQ - mt * P)
                    ob = nx if mt < AHEAD else bt
                    if c == 0 and mt in (0, 7) and ob.off >= 1:
                        dve.wait_ge(nm_done, ob.val(2, 0 if mt else -1))
                    dve.tensor_reduce(mxp[0:r, mt, c:c + 1], src[0:r, 0:MCUT[c + 1] - MCUT[c]], AX_X, ALU.max).then_inc(work_dve, 1)
                    if c == 2 and mt in (6, NM - 1):
                        tiles = slice(0, 7) if mt == 6 else slice(7, NM)
                        dve.wait_ge(work_dve, w.taken(k))
                        dve.tensor_reduce(nm[:, tiles], mxp[:, tiles, :], AX_X, ALU.max, negate=True).then_inc(nm_done, 1)
                elif x[0] == "R":
                    c0, c1 = row_cols(x[1])
                    ob = nx if x[1] < 2 else bt
                    if x[1] == 0:
                        dve.wait_ge(q_lo_done, ob.val(4, 4))
                    dve.tensor_scalar(q_hi[ob.par][0:1, c0:c1], src[0:1, 0:c1 - c0], HEADROOM, None, ALU.add).then_inc(work_dve, 1)
                else:
                    half, g = x[1:]
                    ob = bt.next(-1) if half and not w.tail else bt
                    hs = Y_HEADS[g]
                    yv = src[0:S, 0:len(hs) * (D + 1)].rearrange("s (h n) -> s h n", n=D + 1)
                    base = 8 * half + 3 * g
                    if half == 0 and g == 0 and (ob.off >= 1):
                        dve.wait_ge(y_norm, ob.val(4, 0))
                    h0 = 8 * half + hs[0]
                    dve.reciprocal(ry[:, h0:h0 + len(hs)], yv[:, :, D]).then_inc(y_chain, 1)
                    dve.wait_ge(y_chain, ob.val(16, base + 1))
                    for j, _ in enumerate(hs):
                        if half == 0 and g == 0 and j == 0:
                            add = x1[:, bass.ds(ob.index(), 1), :].rearrange("s a d -> s (a d)")
                        else:
                            add = acc[:, :]
                        ins = dve.scalar_tensor_tensor(out=acc[:, :], in0=yv[:, j, 0:D], scalar=ry[:, h0 + j:h0 + j + 1], in1=add,
                                                       op0=ALU.mult, op1=ALU.add)
                        if j < len(hs) - 1:
                            ins.then_inc(y_chain, 1)
                            dve.wait_ge(y_chain, ob.val(16, base + j + 2))
                        else:
                            ins.then_inc(work_dve, 1)
                    if half == 1 and g == 2:
                        dve.wait_ge(work_dve, w.taken(k))
                        dve.bn_stats(yst[:, :], acc[:, :]).then_inc(y_norm, 1)
                        dve.wait_ge(y_norm, ob.val(4, 1))
                        dve.sem_inc(dve_waited, 1)
                        dve.bn_aggr(ymv[:, :], yst[:, :]).then_inc(y_norm, 1)
                        dve.wait_ge(y_norm, ob.val(4, 2))
                        dve.tensor_scalar(yve[:, :], ymv[:, 1:2], EPS, None, ALU.add).then_inc(y_norm, 1)

            def layer_norm(bt):
                dve.wait_ge(y_rstd, bt.val(1, 1))
                dve.tensor_scalar(x2[:, bass.ds(bt.index(), 1), :].rearrange("s a d -> s (a d)"), acc[:, :], ymv[:, 0:1], yrs[:, 0:1],
                                  ALU.subtract, ALU.mult).then_inc(y_norm, 1)

            def one_batch(bt, first, last):
                w, nx = Works(bt, first, last), bt.next()
                for u in range(2):
                    for n in range(NTILE):
                        before = [] if (u, n) == (0, 0) else w.at((u, n - 1) if n else (u - 1, NTILE - 1))
                        before = [k for k, x in before if x[0] not in ("q", "T")]
                        for k in before[:1]:
                            take(bt, nx, w, k)
                        t = NTILE * u + n + 1
                        if n == 0 and u == 0 and 0 not in POOL_TILES[0]:
                            low_half(bt, 0, 0)
                        if t < 2 * NTILE and t % NTILE not in POOL_TILES[t // NTILE]:
                            low_half(bt, *divmod(t, NTILE))
                        for k in before[1:]:
                            take(bt, nx, w, k)
                        if u == 0 and n < 4 and not last:
                            stats(nx, n)
                        if u == 0 and n in (5, 6, 7) and not last:
                            normalise(nx, n - 5)
                        if u == 1 and n == 2 and not first:
                            layer_norm(bt.next(-1))
                for k, x in w.at((1, NTILE - 1)):
                    take(bt, nx, w, k)

            b0 = Batch(None, 0)
            w0 = Works(b0, False, False, start=True)
            dve.wait_ge(init_done, 4)
            for part in range(4):
                stats(b0, part)
            for part in range(3):
                normalise(b0, part)
            for k, (_, x) in enumerate(w0.flat):
                if x[0] not in ("q", "T"):
                    take(b0, b0, w0, k)
            over_batches(dve, one_batch)
            bl = Batch(None, B - 1)
            wt = Works(bl.next(), False, False, tail=True)
            for k in range(3):
                take(bl, bl, wt, k)
            layer_norm(bl)

        @block.tensor
        def _(pe):
            def work(bt, nx, w, k):
                x = w.flat[k][1]
                dst = wbank(w, k)
                if k >= 2:
                    pe.wait_ge(work_act if w.is_act(k - 2) else work_dve, w.taken(k - 2))
                elif w.base[1] or w.base[0]:
                    pe.wait_ge(work_dve, bt_val_dve(w, k))
                if x[0] == "q":
                    if x[1] == 0:
                        pe.wait_ge(cur_done, nx.val(1, 1))
                    for j in range(4):
                        last = pe.matmul(dst[:, j * S:(j + 1) * S], qa[:, 4 * x[1] + j, :], ln_cur[:, :], start=True, stop=True)
                elif x[0] == "T":
                    j = x[1]
                    src = (xa_hi, xa_lo)[j // 2][nx.par]
                    pe.wait_ge((xa_hi_done, xa_lo_done)[j // 2], nx.val(1, 1))
                    n0, n1 = ((0, 8), (8, NTILE))[j % 2]
                    for n in range(n0, n1):
                        r = rows_of(n)
                        c = (n - n0) * P
                        last = pe.transpose(dst.bitcast(F16)[:, c:c + r], src[0:r, n, :], ident16[0:r, 0:r])
                elif x[0] == "M":
                    mt, c = x[1:]
                    ob = nx if mt < AHEAD else bt
                    r = min(P, HQ - mt * P)
                    if c == 0 and mt in (0, 7):
                        pe.wait_ge(q_hi_done, ob.val(4, 4))
                        pe.wait_ge(work_act, ob.val(ACTS, 6))
                    last = pe.matmul(dst[0:r, 0:MCUT[c + 1] - MCUT[c]], q_hi[ob.par][:, mt * P:mt * P + r],
                                     xT_hi[ob.par][:, MCUT[c]:MCUT[c + 1]], start=True, stop=True)
                elif x[0] == "R":
                    c0, c1 = row_cols(x[1])
                    ob = nx if x[1] < 2 else bt
                    pe.wait_ge(nm_done, ob.val(2, 1 + x[1] // 2))
                    for c in range(c0, c1, P):
                        r = min(P, c1 - c)
                        last = pe.matmul(dst[0:1, c - c0:c - c0 + r], nm[0:r, c // P:c // P + 1], ident16[0:r, 0:r], start=True, stop=True)
                else:
                    half, g = x[1:]
                    ob = bt.next(-1) if half and not w.tail else bt
                    if g == 0:
                        pe.wait_ge(u_done, ob.val(4, 2 * half + 2))
                    for j, h in enumerate(Y_HEADS[g]):
                        last = pe.matmul(dst[0:S, j * (D + 1):(j + 1) * (D + 1)],
                                         uT[half][:, :, :].rearrange("d c n -> d (c n)")[:, h * S:(h + 1) * S],
                                         w2h[:, half * 8 + h, :], start=True, stop=True)
                last.then_inc(work_rdy, 1)

            def bt_val_dve(w, k):
                return w.bt.val(w.base_dve[0], w.base_dve[1] - 1 + k)

            def scores(bt, u, n, c):
                t, r = NTILE * u + n, rows_of(n)
                if c == 0:
                    if n == 0:
                        if bt.i is None and bt.off == 0:
                            w = Works(bt, u == 1, False, start=u == 0)
                        else:
                            w = Works(bt, False, bt.is_last()) if u else Works(bt.next(-1), False, False)
                        pe.wait_ge(work_dve, w.taken(w.find(("R", 1 if u == 0 else 3))))
                        pe.wait_ge(q_lo_done, bt.val(4, 4))
                        pe.wait_ge(work_act, bt.val(ACTS, ACTS))
                    if not (bt.i is None and bt.off == 0 and t < 2):
                        pe.wait_ge(exp_done, bt.val(4 * NTILE, 2 * (t - 1)))
                out = ps[0:r, 2 * (t % 2) + c, 0:CH]
                cols = slice(u * HALF + c * CH, u * HALF + (c + 1) * CH)
                hi, lo = xT_hi[bt.par][:, n * P:n * P + r], xT_lo[bt.par][:, n * P:n * P + r]
                pe.matmul(out, hi, q_hi[bt.par][:, cols], start=True, stop=False)
                pe.matmul(out, hi, q_lo[bt.par][:, cols], start=False, stop=False)
                last = pe.matmul(out, lo, q_hi[bt.par][:, cols], start=False, stop=True)
                if c == 1:
                    last.then_inc(s_rdy, 1)

            def values(bt, u, n, c):
                t, r = NTILE * u + n, rows_of(n)
                if c == 0:
                    if n == 0 and not (bt.i is None and bt.off == 0 and u == 0):
                        pe.wait_ge(u_done, bt.val(4, 2 * u))
                    pe.wait_ge(exp_done, bt.val(4 * NTILE, 2 * t + 2))
                out = ps[:, 4 + c, 0:CH]
                hi, lo = xa_hi[bt.par][0:r, n, :], xa_lo[bt.par][0:r, n, :]
                pe.matmul(out, hi, p_hi[t % P_SLOTS][0:r, c, :], start=n == 0, stop=False)
                pe.matmul(out, lo, p_hi[t % P_SLOTS][0:r, c, :], start=False, stop=False)
                if c == 0:
                    pe.wait_ge(lo_pool if n in POOL_TILES[u] else lo_dve, lo_count(bt, u, n))
                last = pe.matmul(out, hi, p_lo[t % P_SLOTS][0:r, c, :], start=False, stop=n == NTILE - 1)
                if c == 1:
                    last.then_inc(pv_done, 1)

            def one_batch(bt, first, last):
                w, nx = Works(bt, first, last), bt.next()
                for u in range(2):
                    for n in range(NTILE):
                        todo = [k for k, _ in w.at((u, n))]
                        t3 = NTILE * u + n + LEAD
                        sb_, st = (bt, t3) if t3 < 2 * NTILE else (nx, t3 - 2 * NTILE)
                        ahead = not (last and t3 >= 2 * NTILE)
                        for part in range(4):
                            if part < 2:
                                values(bt, u, n, part)
                            elif ahead:
                                scores(sb_, st // NTILE, st % NTILE, part - 2)
                            take_n = -(-len(todo) // (4 - part))
                            for k in todo[:take_n]:
                                work(bt, nx, w, k)
                            todo = todo[take_n:]

            b0 = Batch(None, 0)
            w0 = Works(b0, False, False, start=True)
            for k in range(len(w0.flat)):
                work(b0, b0, w0, k)
            for n in range(LEAD):
                for c in range(2):
                    scores(b0, 0, n, c)
            over_batches(pe, one_batch)
            bl = Batch(None, B - 1)
            wt = Works(bl.next(), False, False, tail=True)
            for k in range(3):
                work(bl, bl, wt, k)


def row_cols(r):
    t0 = (0, 4, 7, 11, NM)
    return t0[r] * P, min(t0[r + 1] * P, HQ)


def ffn(nc, a, m, ps, out):
    with ExitStack() as ctx:
        def sb(name, shape, dt=F32):
            return ctx.enter_context(nc.sbuf_tensor(name, shape, dt))

        def sem(name):
            return ctx.enter_context(nc.semaphore(name))

        ident, nhalf, x2 = m["ident"], m["nhalf"], m["x2"]
        NC = NE // P
        K8 = 8
        HK = FH * K8
        QP = 25

        f_wq, f_wqt = sb("f_wq", [D, NB * KD]), sb("f_wqt", [KD, NB, D])
        f_keys, f_down, f_up = sb("f_keys", [KD, NB, KEYS]), sb("f_down", [D, NE]), sb("f_up", [P, NC, D])
        f_gam, f_bet = sb("f_gam", [KD, NB]), sb("f_bet", [KD, NB])
        x2T, xcT, xct = sb("x2T", [D, NT]), sb("xcT", [D, NT]), sb("xct", [S, B, D])
        msum, mean = sb("msum", [D, 1]), sb("mean", [D, 1])
        cov, cw = sb("cov", [D, D]), sb("cw", [KD, NB, D])
        var, vrs, gain = sb("var", [KD, NB]), sb("vrs", [KD, NB]), sb("gain", [KD, NB])
        kscaled, sim_w, sim_c = sb("kscaled", [KD, NB, KEYS]), sb("sim_w", [D, NB * KEYS]), sb("sim_c", [1, NB * KEYS])
        ones_r = sb("ones_r", [1, S])
        off8 = sb("off8", [P, 1])
        iota_i = sb("iota_i", [P, P], mybir.dt.int32)
        iota_f, iota_w = sb("iota_f", [P, P]), sb("iota_w", [P, P, S], F16)
        iota_c, iota_j = sb("iota_c", [P, 2 * NC, S], F16), sb("iota_j", [P, K8, K8], F16)
        ones_col = sb("ones_col", [P, 1])
        xc_cur = sb("xc_cur", [D, 2, S])
        simb = sb("simb", [S, 2, NB, KEYS])
        top, idx, idxf = sb("top", [S, 2, NB, K8]), sb("idx", [S, 2, NB, K8], U32), sb("idxf", [S, 2, NB, K8], F16)
        comb = sb("comb", [S, 2, FH, K8, K8])
        sc, pk = sb("sc", [S, 2, FH, K8]), sb("pk", [S, 2, FH, K8], U32)
        pij, pijf = sb("pij", [S, 2, 2, HK], U32), sb("pijf", [S, 2, 2, HK], F16)
        idxw, eq = sb("idxw", [S, 2 * NB, K8, K8], F16), sb("eq", [S, 2 * NB, K8, K8], F16)
        half4, half2 = sb("half4", [S, 2 * NB, 4, K8], F16), sb("half2", [S, 2 * NB, 2, K8], F16)
        ij = sb("ij", [S, 2, NB, K8], F16)
        ef, eu, erc = sb("ef", [S, 2, HK]), sb("eu", [S, 2, HK], U32), sb("erc", [S, 2, 2, HK], U32)
        sel = sb("sel", [S, 3, 2, HK])
        dsc, esc = sb("dsc", [S, 2, FH, K8]), sb("esc", [S, 2, FH, K8])
        ssum, srec = sb("ssum", [S, 2, FH]), sb("srec", [S, 2, FH])
        rT, cT, w_hi, w_lo = sb("rT", [P, S], F16), sb("cT", [P, S], F16), sb("w_hi", [P, S], F16), sb("w_lo", [P, S], F16)
        oneh = sb("oneh", [P, P, S], F16)
        eqc = sb("eqc", [P, 2 * NC, S], F16)
        mv_hi, mv_lo = sb("mv_hi", [P, 2 * NC, S], F16), sb("mv_lo", [P, 2 * NC, S], F16)
        hid, hfac = ([sb(f"{n}{i}", [P, 2, 2 * 2 * S]) for i in range(2)] for n in ("hid", "hfac"))
        gel = [sb(f"gel{i}", [P, NC, 2, S]) for i in range(2)]
        wgt = sb("wgt", [P, NC, 2, S])
        zf, ost = sb("zf", [S, 2, D]), sb("ost", [S, 2, D])
        fst, fmv, fve, frs = sb("fst", [S, 2, 6]), sb("fmv", [S, 2, 2]), sb("fve", [S, 2]), sb("frs", [S, 2])

        f_ld, f_waited = sem("f_ld"), sem("f_waited")
        fc_done, x2T_ps, x2T_done, mean_done, xcT_done = (sem(n) for n in ("fc_done", "x2T_ps", "x2T_done", "mean_done", "xcT_done"))
        xct_ps, xct_done, cov_ps, cov_done = (sem(n) for n in ("xct_ps", "xct_done", "cov_ps", "cov_done"))
        cw_ps, cw_done, var_done, vrs_done, gain_done = (sem(n) for n in ("cw_ps", "cw_done", "var_done", "vrs_done", "gain_done"))
        simw_ps, simw_done, wide_done = sem("simw_ps"), sem("simw_done"), sem("wide_done")
        fcur_done, sim_ps, sim_done, top_done, comb_done, best_done = (sem(n) for n in ("fcur_done", "sim_ps", "sim_done", "top_done", "comb_done", "best_done"))
        dsc_done, esc_done, pick, sel_done, selT_ps, selT_done = (sem(n) for n in ("dsc_done", "esc_done", "pick", "sel_done", "selT_ps", "selT_done"))
        wlo_done, oneh_done, g_ps, g_done, y_ps, z_done, z_rstd, o_done, out_done = (
            sem("f" + n) for n in ("wlo_done", "oneh_done", "g_ps", "g_done", "y_ps", "z_done", "z_rstd", "o_done", "out_done"))
        h_ps, hid_done, hadd_done, hu_done, hth_done, gel_done = (
            sem(n) for n in ("h_ps", "hid_done", "hadd_done", "hu_done", "hth_done", "gel_done"))
        wide_idx, th_done = sem("wide_idx"), sem("th_done")

        block = ctx.enter_context(nc.Block())
        NPAIR = B // 2
        BN_C = 0.044715
        TANH_C = (2.0 / 3.141592653589793) ** 0.5

        @block.sync
        def _(sp):
            for dst, src in ((f_wq[:, :], a["L0_ffn_w_q"]),
                             (f_wqt[:, 0:FH, :], a["ffn_wq_t"][0:FH * KD, :].rearrange("(n e) d -> e n d", e=KD)),
                             (f_wqt[:, FH:NB, :], a["ffn_wq_t"][FH * KD:NB * KD, :].rearrange("(n e) d -> e n d", e=KD)),
                             (f_keys[:, :, :], a["ffn_keys_t"].rearrange("e s h k -> e (s h) k")),
                             (f_down[:, :], a["ffn_down_t"]),
                             (f_up[:, :, :], a["L0_ffn_up_embed"].rearrange("(c e) d -> e c d", e=P)),
                             (f_gam[:, :], a["L0_ffn_bn_gamma"]),
                             (f_bet[:, :], a["L0_ffn_bn_beta"])):
                sp.dma_start(dst, src).then_inc(f_ld, 16)
            with sp.Fori(0, NPAIR) as i:
                sp.wait_ge(o_done, i * 1 + 1)
                sp.dma_start(out[bass.ds(i * 2, 2), :, :].rearrange("b s d -> s b d"), ost[:, :, :]).then_inc(out_done, 16)
            sp.wait_ge(out_done, 16 * NPAIR)

        @block.gpsimd
        def _(pool):
            pool.iota(iota_i[:, :], pattern=[[1, P]], base=0, channel_multiplier=0).then_inc(fc_done, 1)
            pool.memset(ones_r[:, :], 1.0).then_inc(fc_done, 1)
            pool.memset(ones_col[:, :], 1.0).then_inc(fc_done, 1)
            pool.memset(off8[:, :], 0.0).then_inc(fc_done, 1)
            pool.wait_ge(fc_done, 4)
            pool.memset(off8[HK:P, :], float(NC)).then_inc(fc_done, 1)
            pool.wait_ge(fc_done, 5)
            pool.tensor_copy(iota_f[:, :], iota_i[:, :]).then_inc(fc_done, 1)
            pool.wait_ge(var_done, 3)
            pool.tensor_tensor(out=vrs[:, :], in0=var[:, :], in1=nhalf[:, 0:NB], op=ALU.pow).then_inc(vrs_done, 1)

            def step(i, par, first, second=False):
                pool.wait_ge(top_done, i * 2 + 1)
                if not first:
                    pool.wait_ge(best_done, i * 2)
                for hf in range(2):
                    ins = pool.tensor_tensor(out=comb[:, hf, :, :, :],
                                             in0=top[:, hf, 0:FH, :].rearrange("s h (i a) -> s h i a", a=1).to_broadcast([S, FH, K8, K8]),
                                             in1=top[:, hf, FH:NB, :].rearrange("s h (a j) -> s h a j", a=1).to_broadcast([S, FH, K8, K8]),
                                             op=ALU.add)
                ins.then_inc(comb_done, 1)
                for r in range(2):
                    pool.wait_ge(hadd_done, i * 2 + r + 1)
                    pool.tensor_tensor(out=hfac[r][:, :, :], in0=hfac[r][:, :, :], in1=hid[r][:, :, :], op=ALU.mult).then_inc(hu_done, 1)
                if not (first or second):
                    pool.wait_ge(g_done, i * 4 - 4)
                for r in range(2):
                    pool.wait_ge(hth_done, i * 2 + r + 1)
                    pool.tensor_tensor(out=gel[par][:, 4 * r:4 * r + 4, :, :].rearrange("e (b c) a s -> e b (c a s)", b=2),
                                       in0=hfac[r][:, :, :], in1=hid[r][:, :, :], op=ALU.mult).then_inc(gel_done, 1)

            def finish(i):
                pool.wait_ge(z_done, i * 4 + 4)
                pool.tensor_tensor(out=frs[:, :], in0=fve[:, :], in1=nhalf[0:S, 0:2], op=ALU.pow).then_inc(z_rstd, 1)

            step(0, 0, True)
            step(1, 1, False, True)
            finish(0)
            with pool.Fori(0, (NPAIR - 2) // 2) as k:
                for off in range(2):
                    step(k * 2 + 2 + off, off, False)
                    finish(k * 2 + 1 + off)
            finish(NPAIR - 1)

        @block.scalar
        def _(act):
            for k in range(NG):
                act.wait_ge(x2T_ps, k + 1)
                act.activation(x2T[:, k * G * S:(k + 1) * G * S], ps[:, k, 0:G * S], ACT.Copy).then_inc(x2T_done, 1)
            for k in range(NG):
                act.wait_ge(xct_ps, k + 1)
                act.activation(xct[:, k * G:(k + 1) * G, :], ps[0:S, 4 + k, :].rearrange("s (b d) -> s b d", b=G), ACT.Copy).then_inc(xct_done, 1)
            act.wait_ge(cov_ps, 1)
            act.activation(cov[:, :], ps[:, 0, 0:D], ACT.Copy, scale=1.0 / NT).then_inc(cov_done, 1)
            act.wait_ge(fc_done, 6)
            act.activation(iota_w[:, :, :], iota_f[:, :].rearrange("p (e a) -> p e a", a=1).to_broadcast([P, P, S]), ACT.Copy)
            act.activation(iota_c[:, :, :], iota_f[:, 0:2 * NC].rearrange("p (e a) -> p e a", a=1).to_broadcast([P, 2 * NC, S]), ACT.Copy)
            act.activation(iota_j[:, :, :], iota_f[:, 0:K8].rearrange("p (j a) -> p j a", a=1).to_broadcast([P, K8, K8]),
                           ACT.Copy).then_inc(wide_done, 1)
            act.wait_ge(simw_ps, 1)
            act.activation(sim_w[:, :], ps[:, 5, :], ACT.Copy).then_inc(simw_done, 1)
            act.activation(sim_c[:, :], ps[0:1, 6, :], ACT.Copy).then_inc(simw_done, 1)
            def step(i, first):
                if not first:
                    act.wait_ge(sim_ps, i * 2)
                act.activation(xc_cur[:, :, :].rearrange("d a s -> d (a s)"), xcT[:, bass.ds(i * (2 * S), 2 * S)],
                               ACT.Copy).then_inc(fcur_done, 1)
                act.wait_ge(sim_ps, i * 2 + 2)
                if not first:
                    act.wait_ge(top_done, i * 2)
                act.activation(simb[:, :, :, :].rearrange("s a n k -> s a (n k)"), ps[0:S, 0:2, :], ACT.Copy).then_inc(sim_done, 1)
                for r in range(2):
                    act.wait_ge(h_ps, i * 2 + r + 1)
                    if not first:
                        act.wait_ge(gel_done, i * 2 + r - 1)
                    act.activation(hid[r][:, :, :], ps[:, 2:4, 0:4 * S], ACT.Copy)
                    act.activation(hfac[r][:, :, :], ps[:, 2:4, 0:4 * S], ACT.Square, scale=BN_C ** 0.5).then_inc(hid_done, 1)
                    act.wait_ge(hid_done, i * 2 + r + 1)
                    act.activation(hfac[r][:, :, :], hfac[r][:, :, :], ACT.Identity, bias=ones_col[:, 0:1]).then_inc(hadd_done, 1)
                act.wait_ge(pick, i * 7 + 1)
                act.activation(idxw[:, :, :, :], idxf[:, :, :, :].rearrange("s a n (j c) -> s (a n) j c", c=1).to_broadcast([S, 2 * NB, K8, K8]),
                               ACT.Copy).then_inc(wide_idx, 1)
                for r in range(2):
                    act.wait_ge(hu_done, i * 2 + r + 1)
                    act.activation(hfac[r][:, :, :], hfac[r][:, :, :], ACT.Tanh, scale=TANH_C).then_inc(th_done, 1)
                    act.wait_ge(th_done, i * 2 + r + 1)
                    act.activation(hfac[r][:, :, :], hfac[r][:, :, :], ACT.Identity, bias=ones_col[:, 0:1]).then_inc(hth_done, 1)
                act.wait_ge(dsc_done, i * 1 + 1)
                act.activation(esc[:, :, :, :], dsc[:, :, :, :], ACT.Exp).then_inc(esc_done, 1)
                act.wait_ge(selT_ps, i * 1 + 1)
                if not first:
                    act.wait_ge(oneh_done, i * 1)
                act.activation(rT[:, :], ps[:, 4, 0:S], ACT.Copy)
                act.activation(cT[:, :], ps[:, 4, S:2 * S], ACT.Identity, bias=off8[:, 0:1])
                act.activation(w_hi[:, :], ps[:, 4, 2 * S:3 * S], ACT.Copy).then_inc(selT_done, 1)

            step(0, True)
            with act.Fori(1, NPAIR) as i:
                step(i, False)

        @block.vector
        def _(dve):
            dve.wait_ge(x2T_done, NG)
            dve.tensor_reduce(msum[:, :], x2T[:, :], AX_X, ALU.add).then_inc(mean_done, 1)
            dve.wait_ge(mean_done, 1)
            dve.tensor_scalar(mean[:, :], msum[:, :], 1.0 / NT, None, ALU.mult).then_inc(mean_done, 1)
            dve.wait_ge(mean_done, 2)
            dve.tensor_scalar(xcT[:, :], x2T[:, :], mean[:, 0:1], None, ALU.subtract).then_inc(xcT_done, 1)
            dve.wait_ge(f_ld, 16 * 8)
            for k in range(4):
                dve.wait_ge(cw_ps, k + 1)
                dve.tensor_tensor(out=cw[:, 4 * k:4 * k + 4, :], in0=ps[:, 1 + k, :].rearrange("e (n d) -> e n d", n=4),
                                  in1=f_wqt[:, 4 * k:4 * k + 4, :], op=ALU.mult).then_inc(cw_done, 1)
            dve.wait_ge(cw_done, 4)
            dve.tensor_reduce(var[:, :], cw[:, :, :], AX_X, ALU.add).then_inc(var_done, 1)
            dve.wait_ge(var_done, 1)
            dve.tensor_scalar(var[:, :], var[:, :], 0.0, None, ALU.max).then_inc(var_done, 1)
            dve.wait_ge(var_done, 2)
            dve.tensor_scalar(var[:, :], var[:, :], EPS, None, ALU.add).then_inc(var_done, 1)
            dve.wait_ge(vrs_done, 1)
            dve.tensor_tensor(out=gain[:, :], in0=vrs[:, :], in1=f_gam[:, :], op=ALU.mult).then_inc(gain_done, 1)
            dve.wait_ge(gain_done, 1)
            dve.tensor_tensor(out=kscaled[:, :, :], in0=f_keys[:, :, :],
                              in1=gain[:, :].rearrange("e (n a) -> e n a", a=1).to_broadcast([KD, NB, KEYS]), op=ALU.mult).then_inc(gain_done, 1)
            dve.wait_ge(wide_done, 1)

            def weigh(i, par, n):
                dve.wait_ge(g_ps, i * 4 + n + 1)
                if n == 0:
                    dve.wait_ge(gel_done, i * 2 + 2)
                cols = slice(n * QP, (n + 1) * QP)
                dve.tensor_tensor(out=wgt[:, :, :, cols].rearrange("e c a s -> e a c s"),
                                  in0=ps[:, 5 + n % 2, 0:QP * 2 * NC].rearrange("e (s a c) -> e a c s", a=2, c=NC),
                                  in1=gel[par][:, :, :, cols].rearrange("e c a s -> e a c s"), op=ALU.mult).then_inc(g_done, 1)

            def step(i, par, first, second=False, third=False):
                dve.wait_ge(sim_done, i * 1 + 1)
                if not first:
                    dve.wait_ge(comb_done, i * 1)
                    dve.wait_ge(pick, i * 7)
                dve.sem_inc(f_waited, 1)
                for hf in range(2):
                    for n in range(NB):
                        ins = dve.max(top[:, hf, n, :], simb[:, hf, n, :])
                ins.then_inc(top_done, 1)
                if not (first or second):
                    last_norm(i - 2, third)
                dve.wait_ge(top_done, i * 2 + 1)
                dve.sem_inc(f_waited, 1)
                for hf in range(2):
                    for n in range(NB):
                        ins = dve.max_index(idx[:, hf, n, :], top[:, hf, n, :], simb[:, hf, n, :])
                ins.then_inc(top_done, 1)
                dve.wait_ge(top_done, i * 2 + 2)
                dve.tensor_copy(idxf[:, :, :, :], idx[:, :, :, :]).then_inc(pick, 1)
                if not first:
                    weigh(i - 1, 1 - par, 0)
                    weigh(i - 1, 1 - par, 1)
                dve.wait_ge(comb_done, i * 1 + 1)
                dve.sem_inc(f_waited, 1)
                for hf in range(2):
                    for h in range(FH):
                        ins = dve.max(sc[:, hf, h, :], comb[:, hf, h, :, :].rearrange("s i j -> s (i j)"))
                ins.then_inc(best_done, 1)
                dve.wait_ge(best_done, i * 2 + 1)
                dve.sem_inc(f_waited, 1)
                for hf in range(2):
                    for h in range(FH):
                        ins = dve.max_index(pk[:, hf, h, :], sc[:, hf, h, :], comb[:, hf, h, :, :].rearrange("s i j -> s (i j)"))
                ins.then_inc(best_done, 1)
                if not first:
                    dve.wait_ge(esc_done, i * 1)
                dve.tensor_tensor(out=dsc[:, :, :, :], in0=sc[:, :, :, :], in1=sc[:, :, :, 0:1].to_broadcast([S, 2, FH, K8]),
                                  op=ALU.subtract).then_inc(dsc_done, 1)
                dve.wait_ge(best_done, i * 2 + 2)
                flat = pk[:, :, :, :].rearrange("s a h k -> s a (h k)")
                dve.tensor_scalar(pij[:, :, 0, :], flat, 3, None, ALU.logical_shift_right)
                dve.tensor_scalar(pij[:, :, 1, :], flat, K8 - 1, None, ALU.bitwise_and).then_inc(pick, 1)
                dve.wait_ge(pick, i * 7 + 2)
                dve.tensor_copy(pijf[:, :, :, :], pij[:, :, :, :]).then_inc(pick, 1)
                dve.wait_ge(pick, i * 7 + 3)
                dve.tensor_tensor(out=eq[:, :, :, :],
                                  in0=pijf[:, :, :, :].rearrange("s a b (h c k) -> s (a b h) c k", h=FH, c=1).to_broadcast([S, 2 * NB, K8, K8]),
                                  in1=iota_j[0:S, :, :].rearrange("s (a j) k -> s a j k", a=1).to_broadcast([S, 2 * NB, K8, K8]),
                                  op=ALU.is_equal).then_inc(pick, 1)
                dve.wait_ge(wide_idx, i * 1 + 1)
                dve.wait_ge(pick, i * 7 + 4)
                dve.tensor_tensor(out=eq[:, :, :, :], in0=eq[:, :, :, :], in1=idxw[:, :, :, :], op=ALU.mult).then_inc(pick, 1)
                dve.wait_ge(pick, i * 7 + 5)
                dve.tensor_tensor(out=half4[:, :, :, :], in0=eq[:, :, 0:4, :], in1=eq[:, :, 4:8, :], op=ALU.add).then_inc(pick, 1)
                dve.wait_ge(pick, i * 7 + 6)
                dve.tensor_tensor(out=half2[:, :, :, :], in0=half4[:, :, 0:2, :], in1=half4[:, :, 2:4, :], op=ALU.add).then_inc(pick, 1)
                dve.wait_ge(pick, i * 7 + 7)
                dve.tensor_tensor(out=ij[:, :, :, :].rearrange("s a n k -> s (a n) k"), in0=half2[:, :, 0, :], in1=half2[:, :, 1, :],
                                  op=ALU.add).then_inc(sel_done, 1)
                dve.wait_ge(sel_done, i * 7 + 1)
                dve.scalar_tensor_tensor(out=eu[:, :, :], in0=ij[:, :, 0:FH, :].rearrange("s a h k -> s a (h k)"), scalar=float(KEYS),
                                         in1=ij[:, :, FH:NB, :].rearrange("s a h k -> s a (h k)"), op0=ALU.mult, op1=ALU.add).then_inc(sel_done, 1)
                dve.wait_ge(sel_done, i * 7 + 2)
                dve.tensor_scalar(erc[:, 0, :, :], eu[:, :, :], P - 1, None, ALU.bitwise_and)
                dve.tensor_scalar(erc[:, 1, :, :], eu[:, :, :], 7, None, ALU.logical_shift_right).then_inc(sel_done, 1)
                dve.wait_ge(esc_done, i * 1 + 1)
                dve.tensor_reduce(ssum[:, :, :], esc[:, :, :, :], AX_X, ALU.add).then_inc(sel_done, 1)
                if not first:
                    dve.wait_ge(selT_ps, i * 1)
                dve.wait_ge(sel_done, i * 7 + 3)
                dve.tensor_copy(sel[:, 0:2, :, :], erc[:, :, :, :])
                dve.wait_ge(sel_done, i * 7 + 4)
                dve.reciprocal(srec[:, :, :], ssum[:, :, :]).then_inc(sel_done, 1)
                dve.wait_ge(sel_done, i * 7 + 5)
                dve.tensor_scalar(srec[:, :, :], srec[:, :, :], 0.5, None, ALU.mult).then_inc(sel_done, 1)
                dve.wait_ge(sel_done, i * 7 + 6)
                dve.tensor_tensor(out=sel[:, 2, :, :].rearrange("s a (h k) -> s (a h) k", h=FH),
                                  in0=esc[:, :, :, :].rearrange("s a h k -> s (a h) k"),
                                  in1=srec[:, :, :].rearrange("s a (h c) -> s (a h) c", c=1).to_broadcast([S, 2 * FH, K8]),
                                  op=ALU.mult).then_inc(sel_done, 1)
                if not first:
                    weigh(i - 1, 1 - par, 2)
                    weigh(i - 1, 1 - par, 3)
                dve.wait_ge(selT_done, i * 1 + 1)
                dve.tensor_tensor(out=w_lo[:, :], in0=ps[:, 4, 2 * S:3 * S], in1=w_hi[:, :], op=ALU.subtract).then_inc(wlo_done, 1)
                dve.tensor_tensor(out=oneh[:, :, :], in0=iota_w[:, :, :],
                                  in1=rT[:, :].rearrange("p (a s) -> p a s", a=1).to_broadcast([P, P, S]), op=ALU.is_equal)
                dve.tensor_tensor(out=eqc[:, :, :], in0=iota_c[:, :, :],
                                  in1=cT[:, :].rearrange("p (a s) -> p a s", a=1).to_broadcast([P, 2 * NC, S]), op=ALU.is_equal).then_inc(wlo_done, 1)
                dve.wait_ge(wlo_done, i * 2 + 2)
                for w, dst in ((w_hi, mv_hi), (w_lo, mv_lo)):
                    ins = dve.tensor_tensor(out=dst[:, :, :], in0=eqc[:, :, :],
                                            in1=w[:, :].rearrange("p (a s) -> p a s", a=1).to_broadcast([P, 2 * NC, S]), op=ALU.mult)
                ins.then_inc(oneh_done, 1)

            def add_up(i):
                dve.wait_ge(y_ps, i * 1 + 1)
                dve.tensor_tensor(out=zf[:, :, :], in0=ps[0:S, 7, 0:2 * D].rearrange("s (a d) -> s a d", a=2),
                                  in1=x2[:, bass.ds(i * 2, 2), :], op=ALU.add).then_inc(z_done, 1)
                dve.wait_ge(z_done, i * 4 + 1)
                for hf in range(2):
                    ins = dve.bn_stats(fst[:, hf, :], zf[:, hf, :])
                ins.then_inc(z_done, 1)
                dve.wait_ge(z_done, i * 4 + 2)
                dve.sem_inc(f_waited, 1)
                for hf in range(2):
                    ins = dve.bn_aggr(fmv[:, hf, :], fst[:, hf, :])
                ins.then_inc(z_done, 1)
                dve.wait_ge(z_done, i * 4 + 3)
                dve.tensor_scalar(fve[:, :], fmv[:, :, 1], EPS, None, ALU.add).then_inc(z_done, 1)

            def last_norm(i, first):
                dve.wait_ge(z_rstd, i * 1 + 1)
                if not first:
                    dve.wait_ge(out_done, i * 16)
                for hf in range(2):
                    ins = dve.tensor_scalar(ost[:, hf, :], zf[:, hf, :], fmv[:, hf, 0:1], frs[:, hf:hf + 1], ALU.subtract, ALU.mult)
                ins.then_inc(o_done, 1)

            step(0, 0, True)
            step(1, 1, False, second=True)
            add_up(0)
            step(2, 0, False, third=True)
            add_up(1)
            step(3, 1, False)
            add_up(2)
            with dve.Fori(0, (NPAIR - 4) // 2) as k:
                for off in range(2):
                    step(k * 2 + 4 + off, off, False)
                    add_up(k * 2 + 3 + off)
            last_norm(NPAIR - 2, False)
            for n in range(4):
                weigh(NPAIR - 1, (NPAIR - 1) % 2, n)
            add_up(NPAIR - 1)
            last_norm(NPAIR - 1, False)

        @block.tensor
        def _(pe):
            for k in range(NG):
                for j in range(G):
                    last = pe.transpose(ps[:, k, j * S:(j + 1) * S], x2[:, k * G + j, :], ident[0:S, 0:S])
                last.then_inc(x2T_ps, 1)
            pe.wait_ge(xcT_done, 1)
            for k in range(NG):
                for j in range(G):
                    b = k * G + j
                    last = pe.transpose(ps[0:S, 4 + k, j * D:(j + 1) * D], xcT[:, b * S:(b + 1) * S], ident[:, :])
                last.then_inc(xct_ps, 1)
            pe.wait_ge(xct_done, NG)
            for b in range(B):
                last = pe.matmul(ps[:, 0, 0:D], xct[:, b, :], xct[:, b, :], start=b == 0, stop=b == B - 1)
            last.then_inc(cov_ps, 1)
            pe.wait_ge(cov_done, 1)
            pe.wait_ge(f_ld, 16 * 8)
            for n in range(NB):
                last = pe.matmul(ps[:, 1 + n // 4, (n % 4) * D:(n % 4 + 1) * D], f_wq[:, n * KD:(n + 1) * KD], cov[:, :], start=True, stop=True)
                if n % 4 == 3:
                    last.then_inc(cw_ps, 1)
            pe.wait_ge(fc_done, 6)
            for n in range(NB):
                last = pe.matmul(ps[0:1, 6, n * KEYS:(n + 1) * KEYS], f_bet[:, n:n + 1], f_keys[:, n, :], start=True, stop=True)
            pe.wait_ge(gain_done, 2)
            for n in range(NB):
                last = pe.matmul(ps[:, 5, n * KEYS:(n + 1) * KEYS], f_wqt[:, n, :], kscaled[:, n, :], start=True, stop=True)
            last.then_inc(simw_ps, 1)
            pe.wait_ge(simw_done, 2)

            def expert_rows(i, n, first):
                if n == 0:
                    pe.wait_ge(oneh_done, i * 1 + 1)
                if n >= 2 or not first:
                    pe.wait_ge(g_done, i * 4 + n - 1)
                for q in range(QP):
                    s = n * QP + q
                    dst = ps[:, 5 + n % 2, q * 2 * NC:(q + 1) * 2 * NC]
                    pe.matmul(dst, oneh[:, :, s], mv_hi[:, :, s], start=True, stop=False)
                    last = pe.matmul(dst, oneh[:, :, s], mv_lo[:, :, s], start=False, stop=True)
                last.then_inc(g_ps, 1)

            def add_experts(i, first):
                pe.wait_ge(g_done, i * 4 + 4)
                if not first:
                    pe.wait_ge(z_done, i * 4 - 3)
                for hf in range(2):
                    for c in range(NC):
                        last = pe.matmul(ps[0:S, 7, hf * D:(hf + 1) * D], wgt[:, c, hf, :], f_up[:, c, :], start=c == 0, stop=c == NC - 1)
                last.then_inc(y_ps, 1)

            def step(i, first, second):
                pe.wait_ge(fcur_done, i * 1 + 1)
                if not first:
                    pe.wait_ge(sim_done, i * 1)
                for hf in range(2):
                    pe.matmul(ps[0:S, hf, :], xc_cur[:, hf, :], sim_w[:, :], start=True, stop=False)
                    pe.matmul(ps[0:S, hf, :], ones_r[:, :], sim_c[:, :], start=False, stop=True).then_inc(sim_ps, 1)
                for r in range(2):
                    if r or not first:
                        pe.wait_ge(hid_done, i * 2 + r)
                    for c in range(4):
                        last = pe.matmul(ps[:, 2 + c // 2, (c % 2) * 2 * S:(c % 2 + 1) * 2 * S],
                                         f_down[:, (4 * r + c) * P:(4 * r + c + 1) * P], x2T[:, bass.ds(i * (2 * S), 2 * S)],
                                         start=True, stop=True)
                    last.then_inc(h_ps, 1)
                    if not first:
                        for n in (2 * r, 2 * r + 1):
                            expert_rows(i - 1, n, second)
                pe.wait_ge(sel_done, i * 7 + 7)
                if not first:
                    pe.wait_ge(wlo_done, i * 2)
                for n in range(3):
                    last = pe.transpose(ps[:, 4, n * S:(n + 1) * S], sel[:, n, :, :].rearrange("s a k -> s (a k)"), ident[0:S, 0:S])
                last.then_inc(selT_ps, 1)
                if not first:
                    add_experts(i - 1, second)

            step(0, True, False)
            step(1, False, True)
            with pe.Fori(2, NPAIR) as i:
                step(i, False, False)
            for n in range(4):
                expert_rows(NPAIR - 1, n, False)
            add_experts(NPAIR - 1, False)


def decoder(nc, a, out):
    with ExitStack() as whole, ExitStack() as part:
        def sb(name, shape, dt=F32, until=whole):
            return until.enter_context(nc.sbuf_tensor(name, shape, dt))

        ps = whole.enter_context(nc.psum_tensor("ps", [P, 8, 512], F32))
        m = {
            "ident": sb("ident", [P, P]), "nhalf": sb("nhalf", [P, B]),
            "x2": sb("x2", [S, B, D]),
            "ident16": sb("ident16", [P, P], F16, part),
            "qa": sb("qa", [D, H, D], F32, part),
            "w2h": sb("w2h", [D, H, D + 1], F32, part),
            "sc1": sb("sc1", [D, B, H], F32, part),
            "kb": sb("kb", [D, B, H], F32, part),
            "x1": sb("x1", [S, B, D], F32, part),
            "lnT": sb("lnT", [D, NT], F32, part),
        }
        front(nc, a, m, ps)
        cross(nc, a, m, ps)
        part.close()
        ffn(nc, a, m, ps, out)


def kernel(**inputs):
    import numpy as np
    import concourse.bacc as bacc
    from concourse.bass_utils import run_bass_kernel_spmd

    half = D // 2
    angle = np.arange(S)[None, :] / np.power(10000.0, np.arange(half) / half)[:, None]
    cos, sin = np.round(np.cos(angle)).astype(np.float32), np.round(np.sin(angle)).astype(np.float32)
    arrays = {n: np.asarray(v) for n, v in inputs.items()}
    for n in ("L0_attn_g_norm", "L0_attn_b_qkv", "L0_attn_b_proj", "L0_xattn_ln1_w", "L0_xattn_ln1_b",
              "L0_xattn_ln2_w", "L0_xattn_ln2_b"):
        arrays[n] = arrays[n].reshape(-1, 1)
    wkv = arrays.pop("L0_xattn_Wkv")
    arrays["wk_t"], arrays["wv_t"] = wkv[:, :H * DH].T, wkv[:, H * DH:].T
    arrays["wq_t"] = arrays.pop("L0_xattn_Wq").T
    arrays["ffn_wq_t"] = arrays["L0_ffn_w_q"].T
    arrays["ffn_keys_t"] = arrays.pop("L0_ffn_keys").transpose(3, 2, 0, 1)
    arrays["ffn_down_t"] = arrays.pop("L0_ffn_down_embed").T
    arrays["L0_ffn_bn_gamma"] = arrays["L0_ffn_bn_gamma"].reshape(NB, KD).T
    arrays["L0_ffn_bn_beta"] = arrays["L0_ffn_bn_beta"].reshape(NB, KD).T
    arrays["cos_t"] = np.concatenate([cos, cos])
    arrays["sin_t"] = np.concatenate([-sin, sin])

    nc = bacc.Bacc("TRN2", target_bir_lowering=False, num_devices=1)
    feed, aps = {}, {}
    for n, v in arrays.items():
        v = np.ascontiguousarray(v)
        feed[f"in_{n}"] = v
        aps[n] = nc.dram_tensor(f"in_{n}", v.shape, mybir.dt.from_np(v.dtype), kind="ExternalInput").ap()
    out = nc.dram_tensor("out_x", (B, S, D), F32, kind="ExternalOutput").ap()
    decoder(nc, aps, out)
    r = run_bass_kernel_spmd(nc, [feed], core_ids=[0])
    return r.results[0]["out_x"]
```

```python
from contextlib import ExitStack

import concourse.bass as bass
from concourse import mybir

F32 = mybir.dt.float32
F16 = mybir.dt.float16
BF16 = mybir.dt.bfloat16
U32 = mybir.dt.uint32
ALU = mybir.AluOpType
ACT = mybir.ActivationFunctionType
AX_X = mybir.AxisListType.X

P = 128
B, S, D = 16, 100, 128
NT = B * S
G = 4
NG = B // G
T = 1444
TF = T // P
TR = T - TF * P
NTILE = TF + 1
H, DH = 16, 64
HQ = H * S
HALF = HQ // 2
CH = HALF // 2
NM = (HQ + P - 1) // P
LN3 = 1.0986122886681098
ATT_SCALE = LN3 / float(D) ** 0.5
EPS_RMS, EPS = 1e-6, 1e-5
QA_SCALE = 64.0
HEADROOM = 6.0
FH, KEYS, KD, NE = 8, 32, 128, 1024
NB = 2 * FH


def front(nc, a, m, ps):
    with ExitStack() as ctx:
        def sb(name, shape, dt=F32):
            return ctx.enter_context(nc.sbuf_tensor(name, shape, dt))

        def sem(name):
            return ctx.enter_context(nc.semaphore(name))

        x_tok = sb("x_tok", [S, B, D])
        w_qkv = sb("w_qkv", [D, 3 * D])
        w_swap = sb("w_swap", [D, 2 * D])
        b_qkv = sb("b_qkv", [D, 3])
        b_swap = sb("b_swap", [D, 2])
        g_col = sb("g_col", [D, 1])
        w_proj = sb("w_proj", [D, D])
        bp_row = sb("bp_row", [S, D])
        cos_t = sb("cos_t", [D, S])
        sin_t = sb("sin_t", [D, S])
        w2_col = sb("w2_col", [D, 1])
        b2_col = sb("b2_col", [D, 1])
        sq_all = sb("sq", [P, B, D])
        sq = sq_all[0:S]
        qa = sq_all
        ms = sb("ms", [S, B])
        rr = sb("rr", [S, B])
        xr = sb("xr", [S, B, D])
        x2b = sb("x2b", [S, B, D])
        hT = sb("hT", [D, NT])
        rot_a = sb("rot_a", [D, G, S])
        rot_b = sb("rot_b", [D, G, S])
        qT = sb("qT", [D, NT])
        kT = sb("kT", [D, NT])
        v_sb = sb("v_sb", [S, B, D])
        mx = sb("mx", [S, B])
        nb = sb("nb", [S, B])
        rs = sb("rs", [S, B])
        rc = sb("rc", [S, B])
        prob = sb("prob", [S, B, S])
        probT = sb("probT", [S, B, S])
        oT = hT
        z = xr
        bst = sb("bst", [S, B, 6])
        mv = sb("mv", [S, B, 2])
        ve = sb("ve", [S, B])
        rstd = sb("rstd", [S, B])
        ve2 = sb("ve2", [S, B])
        rstd2 = sb("rstd2", [S, B])
        eps_t = sb("eps_t", [S, G])
        wq_t = sb("wq_t", [DH, H, D])
        wk_t = sb("wk_t", [DH, H, D])
        wv_t = sb("wv_t", [DH, H, D])
        wout = sb("wout", [DH, H, D])
        wk_f = sb("wk_f", [DH, H, D])
        wv_f = sb("wv_f", [DH, H, D])
        vb = sb("vb", [DH, H])
        w1_row = sb("w1_row", [DH, D])
        b1_row = sb("b1_row", [DH, D])
        ones_c = sb("ones_c", [DH, 1])
        side = sb("side", [D, B, H])
        kbar = sb("kbar", [D, H])

        ident, ident16, nhalf = m["ident"], m["ident16"], m["nhalf"]
        cx = m["context"]
        w2h, sc1, kb, x1 = m["w2h"], m["sc1"], m["kb"], m["x1"]
        qa_hi, qa_lo, ln_hi, ln_lo = m["qa_hi"], m["qa_lo"], m["ln_hi"], m["ln_lo"]
        lnT = kT

        ld_x, ld_att, ld_fold, ld_side = sem("ld_x"), sem("ld_att"), sem("ld_fold"), sem("ld_side")
        ident_done, const_done = sem("ident_done"), sem("const_done")
        sq_done, ms_done, rr_done, xr_done = sem("sq_done"), sem("ms_done"), sem("rr_done"), sem("xr_done")
        x2b_done = sem("x2b_done")
        hT_ps, hT_done = sem("hT_ps"), sem("hT_done")
        qk_ps, rot_done, qk_done = sem("qk_ps"), sem("rot_done"), sem("qk_done")
        v_ps, v_done = sem("v_ps"), sem("v_done")
        sc_ps, mx_done, nb_done, exp_done = sem("sc_ps"), sem("mx_done"), sem("nb_done"), sem("exp_done")
        rc_done, prob_done, pT_ps, pT_done = sem("rc_done"), sem("prob_done"), sem("pT_ps"), sem("pT_done")
        o_ps, o_done, y_ps, z_done = sem("o_ps"), sem("o_done"), sem("y_ps"), sem("z_done")
        st_done, ag_done, ve_done = sem("st_done"), sem("ag_done"), sem("ve_done")
        rstd_done, norm_done = sem("rstd_done"), sem("norm_done")
        ln_ps, ln_done = sem("ln_ps"), sem("ln_done")
        qa_split, ln_split = sem("qa_split"), sem("ln_split")
        again_chain, rstd2_done, again_done = sem("again_chain"), sem("rstd2_done"), sem("again_done")
        kmul_done, kfold_done, vmul_done, vfold_done = sem("kmul_done"), sem("kfold_done"), sem("vmul_done"), sem("vfold_done")
        qa_ps, qa_done, kb_ps, kbar_done, w2_ps, w2_done = (sem(n) for n in ("qa_ps", "qa_done", "kb_ps", "kbar_done", "w2_ps", "w2_done"))
        side_done = sem("side_done")

        block = ctx.enter_context(nc.Block())

        def bank(k, parts, shape):
            names = " ".join("abc"[: len(shape)])
            n = 1
            for s in shape:
                n *= s
            v = ps[0:parts, k, 0:n]
            if len(shape) == 1:
                return v
            return v.rearrange(f"p ({names}) -> p {names}", **dict(zip("abc", shape)))

        first = Batch(None, 0)

        @block.sync
        def _(sp):
            sp.dma_start(x_tok[:, :, :], a["x"].rearrange("b s d -> s b d")).then_inc(ld_x, 16)
            sp.dma_start(w_qkv[:, :], a["L0_attn_w_qkv"]).then_inc(ld_att, 16)
            context_load(sp, cx, a, first)
            for n in range(2):
                for half in range(2):
                    src = n * D + (1 - half) * (D // 2)
                    dst = n * D + half * (D // 2)
                    sp.dma_start(w_swap[:, dst:dst + D // 2],
                                 a["L0_attn_w_qkv"][:, src:src + D // 2]).then_inc(ld_att, 16)
                    sp.dma_start(b_swap[half * (D // 2):(half + 1) * (D // 2), n:n + 1],
                                 a["L0_attn_b_qkv"][src:src + D // 2, :]).then_inc(ld_att, 16)
            for n in range(3):
                sp.dma_start(b_qkv[:, n:n + 1], a["L0_attn_b_qkv"][n * D:(n + 1) * D, :]).then_inc(ld_att, 16)
            sp.dma_start(g_col[:, :], a["L0_attn_g_norm"]).then_inc(ld_att, 16)
            sp.dma_start(cos_t[:, :], a["cos_t"]).then_inc(ld_att, 16)
            sp.dma_start(sin_t[:, :], a["sin_t"]).then_inc(ld_att, 16)
            sp.dma_start(w_proj[:, :], a["L0_attn_w_proj"]).then_inc(ld_att, 16)
            sp.dma_start(bp_row[:, :], a["L0_attn_b_proj"].rearrange("d a -> a d").to_broadcast([S, D])).then_inc(ld_att, 16)
            sp.dma_start(w2_col[:, :], a["L0_xattn_ln2_w"]).then_inc(ld_att, 16)
            sp.dma_start(b2_col[:, :], a["L0_xattn_ln2_b"]).then_inc(ld_att, 16)
            ld = [(wk_t, a["wk_t"].rearrange("(h c) d -> c h d", c=DH)),
                  (wq_t, a["wq_t"].rearrange("(h c) d -> c h d", c=DH)),
                  (wv_t, a["wv_t"].rearrange("(h c) d -> c h d", c=DH)),
                  (wout, a["L0_xattn_Wout"].rearrange("(h c) n -> c h n", c=DH))]
            sp.dma_start(w1_row[:, :], a["L0_xattn_ln1_w"].rearrange("d a -> a d").to_broadcast([DH, D])).then_inc(ld_fold, 16)
            sp.dma_start(b1_row[:, :], a["L0_xattn_ln1_b"].rearrange("d a -> a d").to_broadcast([DH, D])).then_inc(ld_fold, 16)
            for dst, src in ld:
                sp.dma_start(dst[:, :, :], src).then_inc(ld_fold, 16)
            sp.dma_start(side[:, :, :].rearrange("p b h -> p (b h)"),
                         a["fside_Bx16_0"].rearrange("b h -> (b h)").rearrange("(a n) -> a n", a=1).to_broadcast([D, B * H])).then_inc(ld_side, 16)
            context_load(sp, cx, a, first.next())

        LD_ATT, LD_FOLD = 16 * 19, 16 * 6

        @block.gpsimd
        def _(pool):
            pool.memset(ident[:, :], 0.0).then_inc(ident_done, 1)
            pool.memset(ident16[:, :], 0.0).then_inc(ident_done, 1)
            pool.memset(nhalf[:, :], -0.5).then_inc(ident_done, 1)
            pool.memset(ones_c[:, :], 1.0).then_inc(ident_done, 1)
            pool.memset(eps_t[:, :], EPS).then_inc(ident_done, 1)
            pool.wait_ge(ident_done, 5)
            for t in (ident, ident16):
                pool.affine_select(out=t[:, :], in_=t[:, :], compare_op=ALU.not_equal, fill=1.0, base=0,
                                   pattern=[[-1, P]], channel_multiplier=1).then_inc(const_done, 1)
            context_init(pool, cx)
            pool.wait_ge(ms_done, 1)
            pool.tensor_tensor(out=rr[:, :], in0=ms[:, :], in1=nhalf[0:S, 0:B], op=ALU.pow).then_inc(rr_done, 1)
            pool.wait_ge(ld_fold, LD_FOLD)
            pool.tensor_tensor(out=wk_t[:, :, :], in0=wk_t[:, :, :],
                               in1=w1_row[:, :].rearrange("c (a d) -> c a d", a=1).to_broadcast([DH, H, D]), op=ALU.mult).then_inc(kmul_done, 1)
            context_rstd(pool, cx, nhalf, first)
            pool.wait_ge(kmul_done, 1)
            pool.memset(wk_f[:, :, 0:1], 0.0).then_inc(kfold_done, 1)
            pool.tensor_tensor(out=wk_f[:, :, 1:D], in0=wk_t[:, :, 1:D],
                               in1=wk_t[:, :, 0:1].to_broadcast([DH, H, D - 1]), op=ALU.subtract).then_inc(kfold_done, 1)
            context_lo(pool, cx, first)
            pool.wait_ge(qa_split, 1)
            pool.tensor_tensor(out=qa_lo[:, :, :], in0=qa[:, :, :], in1=qa_hi[:, :, :], op=ALU.subtract).then_inc(qa_split, 1)
            for c in range(NG):
                cs = slice(c * G, (c + 1) * G)
                pool.wait_ge(ve_done, c + 1)
                pool.tensor_tensor(out=rstd[:, cs], in0=ve[:, cs], in1=nhalf[0:S, 0:G], op=ALU.pow).then_inc(rstd_done, 1)
                pool.wait_ge(rstd_done, c + 1)
                pool.tensor_tensor(out=ve2[:, cs], in0=mv[:, cs, 1], in1=rstd[:, cs], op=ALU.mult).then_inc(again_chain, 1)
                pool.wait_ge(again_chain, 3 * c + 1)
                pool.tensor_tensor(out=ve2[:, cs], in0=ve2[:, cs], in1=rstd[:, cs], op=ALU.mult).then_inc(again_chain, 1)
                pool.wait_ge(again_chain, 3 * c + 2)
                pool.tensor_tensor(out=ve2[:, cs], in0=ve2[:, cs], in1=eps_t[:, :], op=ALU.add).then_inc(again_chain, 1)
                pool.wait_ge(again_chain, 3 * c + 3)
                pool.tensor_tensor(out=rstd2[:, cs], in0=ve2[:, cs], in1=nhalf[0:S, 0:G], op=ALU.pow).then_inc(rstd2_done, 1)

        @block.scalar
        def _(act):
            def probT_out(c):
                act.wait_ge(pT_ps, c + 1)
                act.activation(probT[:, c * G:(c + 1) * G, :], bank(4 + c, S, (G, S)), ACT.Copy).then_inc(pT_done, 1)

            def oT_out(c):
                act.wait_ge(o_ps, c + 1)
                act.activation(oT[:, c * G * S:(c + 1) * G * S], bank(c, D, (G * S,)), ACT.Identity,
                               bias=b_qkv[:, 2:3]).then_inc(o_done, 1)

            for c in range(NG):
                act.wait_ge(v_ps, c + 1)
                act.activation(v_sb[:, c * G:(c + 1) * G, :], bank(c, S, (G, D)), ACT.Copy).then_inc(v_done, 1)
            context_hi(act, cx, first)
            for c in range(NG):
                act.wait_ge(nb_done, c + 1)
                for j in range(G):
                    b = c * G + j
                    act.activation(prob[:, b, :], bank(c, S, (G, S))[:, j, :], ACT.Exp, bias=nb[:, b:b + 1],
                                   scale=ATT_SCALE, accum_out=rs[:, b:b + 1]).then_inc(exp_done, 1)
            for k in range(NG):
                act.wait_ge(qa_ps, k + 1)
                act.activation(qa[:, 4 * k:4 * k + 4, :], bank(4 + k, D, (4, D)), ACT.Copy,
                               scale=QA_SCALE * DH ** -0.5).then_inc(qa_done, 1)
            probT_out(0)
            act.wait_ge(qa_done, NG)
            act.activation(qa_hi[:, :, :], qa[:, :, :], ACT.Copy).then_inc(qa_split, 1)
            for c in range(NG):
                if c + 1 < NG:
                    probT_out(c + 1)
                oT_out(c)
            for k in range(NG):
                act.wait_ge(w2_ps, k + 1)
                act.activation(w2h[:, 4 * k:4 * k + 4, 0:D], bank(k, D, (4, D)), ACT.Copy).then_inc(w2_done, 1)
            act.wait_ge(kb_ps, 1)
            act.activation(kbar[:, :], bank(0, D, (H,)), ACT.Copy, scale=DH ** -0.5).then_inc(kbar_done, 1)
            for c in range(NG):
                act.wait_ge(rstd2_done, c + 1)
                act.wait_ge(qa_split, 2)
                act.wait_ge(norm_done, c + 1)
                for j in range(G):
                    b = c * G + j
                    ins = act.activation(sq[:, b, :], x1[:, b, :], ACT.Identity, scale=rstd2[:, b:b + 1])
                ins.then_inc(again_done, 1)
            for c in range(NG):
                cs = slice(c * G * S, (c + 1) * G * S)
                act.wait_ge(ln_done, c + 1)
                act.activation(ln_hi[:, cs], lnT[:, cs], ACT.Copy).then_inc(ln_split, 1)

        @block.vector
        def _(dve):
            dve.wait_ge(ld_x, 16)
            dve.tensor_tensor(out=sq[:, :, :], in0=x_tok[:, :, :], in1=x_tok[:, :, :], op=ALU.mult).then_inc(sq_done, 1)
            dve.wait_ge(sq_done, 1)
            dve.tensor_reduce(ms[:, :], sq[:, :, :], AX_X, ALU.add).then_inc(sq_done, 1)
            dve.wait_ge(sq_done, 2)
            dve.tensor_scalar(ms[:, :], ms[:, :], 1.0 / D, EPS_RMS, ALU.mult, ALU.add).then_inc(ms_done, 1)
            dve.wait_ge(ld_att, LD_ATT)
            dve.scalar_tensor_tensor(out=x2b[:, :, :], in0=x_tok[:, :, :], scalar=2.0,
                                     in1=bp_row[:, :].rearrange("s (a d) -> s a d", a=1).to_broadcast([S, B, D]),
                                     op0=ALU.mult, op1=ALU.add).then_inc(x2b_done, 1)
            dve.wait_ge(rr_done, 1)
            dve.tensor_tensor(out=xr[:, :, :], in0=x_tok[:, :, :],
                              in1=rr[:, :].rearrange("s (b a) -> s b a", a=1).to_broadcast([S, B, D]), op=ALU.mult).then_inc(xr_done, 1)
            dve.wait_ge(cx.init_done, 3)
            for part in range(2):
                context_stats(dve, cx, first, part)
            for c in range(NG):
                dve.wait_ge(hT_ps, c + 1)
                dve.tensor_scalar(hT[:, c * G * S:(c + 1) * G * S], bank(c, D, (G * S,)), g_col[:, 0:1], None, ALU.mult).then_inc(hT_done, 1)
            for part in (2, 3):
                context_stats(dve, cx, first, part)
            for c in range(NG):
                for n, dst in enumerate((qT, kT)):
                    dve.wait_ge(qk_ps, 2 * c + n + 1)
                    if c or n:
                        dve.wait_ge(qk_done, 2 * c + n)
                    dve.scalar_tensor_tensor(out=rot_a[:, :, :], in0=bank(4 + 2 * n, D, (G, S)), scalar=b_qkv[:, n:n + 1],
                                             in1=cos_t[:, :].rearrange("d (a s) -> d a s", a=1).to_broadcast([D, G, S]),
                                             op0=ALU.add, op1=ALU.mult).then_inc(rot_done, 1)
                    dve.scalar_tensor_tensor(out=rot_b[:, :, :], in0=bank(5 + 2 * n, D, (G, S)), scalar=b_swap[:, n:n + 1],
                                             in1=sin_t[:, :].rearrange("d (a s) -> d a s", a=1).to_broadcast([D, G, S]),
                                             op0=ALU.add, op1=ALU.mult).then_inc(rot_done, 1)
                    dve.wait_ge(rot_done, 4 * c + 2 * n + 2)
                    dve.tensor_tensor(out=dst[:, c * G * S:(c + 1) * G * S].rearrange("d (a s) -> d a s", a=G),
                                      in0=rot_a[:, :, :], in1=rot_b[:, :, :], op=ALU.add).then_inc(qk_done, 1)
                if c == 0:
                    for part in range(3):
                        context_norm(dve, cx, first, part)
            for c in range(NG):
                cs = slice(c * G, (c + 1) * G)
                dve.wait_ge(sc_ps, c + 1)
                dve.tensor_reduce(mx[:, cs], bank(c, S, (G, S)), AX_X, ALU.max).then_inc(mx_done, 1)
                dve.wait_ge(mx_done, c + 1)
                dve.tensor_scalar(nb[:, cs], mx[:, cs], -ATT_SCALE, None, ALU.mult).then_inc(nb_done, 1)
            dve.wait_ge(ld_fold, LD_FOLD)
            dve.tensor_tensor(out=wv_f[:, :, :], in0=wv_t[:, :, :],
                              in1=b1_row[:, :].rearrange("c (a d) -> c a d", a=1).to_broadcast([DH, H, D]), op=ALU.mult).then_inc(vmul_done, 1)
            for c in range(NG):
                cs = slice(c * G, (c + 1) * G)
                dve.wait_ge(exp_done, (c + 1) * G)
                dve.reciprocal(rc[:, cs], rs[:, cs]).then_inc(rc_done, 1)
                dve.wait_ge(rc_done, c + 1)
                dve.tensor_tensor(out=prob[:, cs, :], in0=prob[:, cs, :],
                                  in1=rc[:, cs].rearrange("s (b a) -> s b a", a=1).to_broadcast([S, G, S]),
                                  op=ALU.mult).then_inc(prob_done, 1)
            dve.wait_ge(vmul_done, 1)
            dve.tensor_reduce(vb[:, :], wv_f[:, :, :], AX_X, ALU.add).then_inc(vmul_done, 1)
            dve.tensor_tensor(out=wv_t[:, :, :], in0=wv_t[:, :, :],
                              in1=w1_row[:, :].rearrange("c (a d) -> c a d", a=1).to_broadcast([DH, H, D]), op=ALU.mult).then_inc(vmul_done, 1)
            dve.wait_ge(vmul_done, 3)
            dve.tensor_tensor(out=wv_f[:, :, 1:D], in0=wv_t[:, :, 1:D],
                              in1=wv_t[:, :, 0:1].to_broadcast([DH, H, D - 1]), op=ALU.subtract).then_inc(vfold_done, 1)
            dve.tensor_copy(wv_f[:, :, 0:1], vb[:, :].rearrange("c (h a) -> c h a", a=1)).then_inc(vfold_done, 1)
            dve.memset(w2h[:, :, D:D + 1], 0.0).then_inc(vfold_done, 1)
            dve.wait_ge(vfold_done, 3)
            dve.memset(w2h[0:1, :, D:D + 1], 1.0).then_inc(vfold_done, 1)

            def normed(c):
                dve.wait_ge(rstd_done, c + 1)
                for j in range(G):
                    b = c * G + j
                    ins = dve.tensor_scalar(x1[:, b, :], z[:, b, :], mv[:, b, 0:1], rstd[:, b:b + 1], ALU.subtract, ALU.mult)
                ins.then_inc(norm_done, 1)

            def queries_out(c):
                dve.wait_ge(ln_ps, c + 1)
                dve.tensor_scalar(lnT[:, c * G * S:(c + 1) * G * S], bank(4 + c, D, (G * S,)), w2_col[:, 0:1], b2_col[:, 0:1],
                                  ALU.mult, ALU.add).then_inc(ln_done, 1)

            for c in range(NG):
                cs = slice(c * G, (c + 1) * G)
                dve.wait_ge(y_ps, c + 1)
                dve.tensor_tensor(out=z[:, cs, :], in0=bank(4 + c, S, (G, D)), in1=x2b[:, cs, :], op=ALU.add).then_inc(z_done, 1)
                dve.wait_ge(z_done, c + 1)
                for j in range(G):
                    ins = dve.bn_stats(bst[:, c * G + j, :], z[:, c * G + j, :])
                ins.then_inc(st_done, 1)
                dve.wait_ge(st_done, c + 1)
                for j in range(G):
                    ins = dve.bn_aggr(mv[:, c * G + j, :], bst[:, c * G + j, :])
                ins.then_inc(ag_done, 1)
                dve.wait_ge(ag_done, c + 1)
                dve.tensor_scalar(ve[:, cs], mv[:, cs, 1], EPS, None, ALU.add).then_inc(ve_done, 1)
                if c:
                    normed(c - 1)
            normed(NG - 1)
            dve.wait_ge(ld_side, 16)
            dve.tensor_scalar(sc1[:, :, :], side[:, :, :], 1.0, 1.0 / QA_SCALE, ALU.add, ALU.mult).then_inc(side_done, 1)
            dve.wait_ge(kbar_done, 1)
            dve.tensor_tensor(out=kb[:, :, :], in0=side[:, :, :],
                              in1=kbar[:, :].rearrange("d (a h) -> d a h", a=1).to_broadcast([D, B, H]), op=ALU.mult).then_inc(side_done, 1)
            for c in range(NG + 1):
                if c < NG:
                    queries_out(c)
                if c:
                    cs = slice((c - 1) * G * S, c * G * S)
                    dve.wait_ge(ln_split, c)
                    dve.tensor_tensor(out=ln_lo[:, cs], in0=lnT[:, cs], in1=ln_hi[:, cs], op=ALU.subtract)

        @block.tensor
        def _(pe):
            def prob_turned(c):
                pe.wait_ge(prob_done, c + 1)
                pe.wait_ge(qa_done, c + 1)
                for j in range(G):
                    last = pe.transpose(bank(4 + c, S, (G, S))[:, j, :], prob[:, c * G + j, :], ident[0:S, 0:S])
                last.then_inc(pT_ps, 1)

            def weighted(c):
                pe.wait_ge(pT_done, c + 1)
                for j in range(G):
                    b = c * G + j
                    last = pe.matmul(bank(c, D, (G, S))[:, j, :], v_sb[:, b, :], probT[:, b, :], start=True, stop=True)
                last.then_inc(o_ps, 1)

            def projected(c):
                pe.wait_ge(o_done, c + 1)
                for j in range(G):
                    b = c * G + j
                    last = pe.matmul(bank(4 + c, S, (G, D))[:, j, :], oT[:, b * S:(b + 1) * S], w_proj[:, :], start=True, stop=True)
                last.then_inc(y_ps, 1)

            pe.wait_ge(const_done, 2)
            pe.wait_ge(xr_done, 1)
            for c in range(NG):
                for j in range(G):
                    last = pe.transpose(bank(c, D, (G, S))[:, j, :], xr[:, c * G + j, :], ident[0:S, 0:S])
                last.then_inc(hT_ps, 1)
            for c in range(NG):
                for n in range(2):
                    if n == 0:
                        pe.wait_ge(hT_done, c + 1)
                    if c:
                        pe.wait_ge(qk_done, 2 * (c - 1) + n + 1)
                    cols = slice(c * G * S, (c + 1) * G * S)
                    pe.matmul(bank(4 + 2 * n, D, (G * S,)), w_qkv[:, n * D:(n + 1) * D], hT[:, cols], start=True, stop=True)
                    pe.matmul(bank(5 + 2 * n, D, (G * S,)), w_swap[:, n * D:(n + 1) * D], hT[:, cols], start=True, stop=True).then_inc(qk_ps, 1)
                for j in range(G):
                    b = c * G + j
                    last = pe.matmul(bank(c, S, (G, D))[:, j, :], hT[:, b * S:(b + 1) * S], w_qkv[:, 2 * D:3 * D], start=True, stop=True)
                last.then_inc(v_ps, 1)
            for c in range(NG):
                pe.wait_ge(qk_done, 2 * (c + 1))
                pe.wait_ge(v_done, c + 1)
                for j in range(G):
                    bs = slice((c * G + j) * S, (c * G + j + 1) * S)
                    last = pe.matmul(bank(c, S, (G, S))[:, j, :], qT[:, bs], kT[:, bs], start=True, stop=True)
                last.then_inc(sc_ps, 1)
            pe.wait_ge(kfold_done, 2)
            for k in range(NG):
                for j in range(4):
                    last = pe.matmul(bank(4 + k, D, (4, D))[:, j, :], wq_t[:, 4 * k + j, :], wk_f[:, 4 * k + j, :], start=True, stop=True)
                last.then_inc(qa_ps, 1)
            prob_turned(0)
            for c in range(NG + 1):
                if c + 1 < NG:
                    prob_turned(c + 1)
                if c < NG:
                    weighted(c)
                if c:
                    projected(c - 1)
            pe.wait_ge(vfold_done, 4)
            for k in range(NG):
                for j in range(4):
                    last = pe.matmul(bank(k, D, (4, D))[:, j, :], wv_f[:, 4 * k + j, :], wout[:, 4 * k + j, :], start=True, stop=True)
                last.then_inc(w2_ps, 1)
            pe.wait_ge(w2_done, 1)
            for h in range(H):
                last = pe.matmul(bank(0, D, (H,))[:, h:h + 1], wk_f[:, h, :], ones_c[:, 0:1], start=True, stop=True)
            last.then_inc(kb_ps, 1)
            for c in range(NG):
                pe.wait_ge(again_done, c + 1)
                for j in range(G):
                    last = pe.transpose(bank(4 + c, D, (G, S))[:, j, :], sq[:, c * G + j, :], ident[0:S, 0:S])
                last.then_inc(ln_ps, 1)


class Batch:

    def __init__(self, i, off):
        self.i, self.off = i, off

    def val(self, coef, const):
        v = coef * self.off + const
        return v if self.i is None else self.i * (2 * coef) + v

    def next(self, n=1):
        return Batch(self.i, self.off + n)

    def is_last(self):
        return self.i is None and self.off == B - 1

    @property
    def par(self):
        return self.off % 2

    def index(self):
        return self.val(1, 0)


def over_batches(eng, body):
    body(Batch(None, 0), True, False)
    with eng.Fori(0, (B - 2) // 2) as i:
        body(Batch(i, 1), False, False)
        body(Batch(i, 2), False, False)
    body(Batch(None, B - 1), False, True)


class Context:

    def __init__(self, sb, sem):
        self.raw = [sb(f"raw{i}", [P, NTILE, D]) for i in range(2)]
        self.cst = sb("cst", [P, NTILE, 6])
        self.cmv = [sb(f"cmv{i}", [P, NTILE, 2]) for i in range(2)]
        self.cve = sb("cve", [P, NTILE])
        self.crs = [sb(f"crs{i}", [P, NTILE]) for i in range(2)]
        self.xh = sb("xh", [P, NTILE, D])
        self.xa_hi = [sb(f"xa_hi{i}", [P, NTILE, D], F16) for i in range(2)]
        self.xa_lo = [sb(f"xa_lo{i}", [P, NTILE, D], F16) for i in range(2)]
        self.ctx_ld = [sem(f"ctx_ld{i}") for i in range(2)]
        self.init_done, self.ctx_stat, self.ctx_rstd, self.xh_done = (sem(n) for n in ("init_done", "ctx_stat", "ctx_rstd", "xh_done"))
        self.xa_hi_done, self.xa_lo_done = sem("xa_hi_done"), sem("xa_lo_done")
        self.pv_done = sem("pv_done")
        self.dve_waited = sem("dve_waited")


def context_init(pool, c):
    pool.memset(c.xh[:, :, :], 1.0).then_inc(c.init_done, 1)
    for i in range(2):
        pool.memset(c.cmv[i][:, :, :], 1.0).then_inc(c.init_done, 1)


def context_load(sp, c, a, bt):
    src = a["ctx_1024"][bass.ds(bt.index(), 1), :, :].rearrange("a t d -> (a t) d")
    sp.dma_start(c.raw[bt.par][:, 0:TF, :],
                 src[0:TF * P, :].rearrange("(p j) d -> p j d", j=TF)).then_inc(c.ctx_ld[bt.par], 16)
    sp.dma_start(c.raw[bt.par][0:TR, TF, :], src[TF * P:T, :]).then_inc(c.ctx_ld[bt.par], 16)


def context_stats(dve, c, bt, part):
    if part == 0:
        dve.wait_ge(c.ctx_ld[bt.par], bt.val(16, 32 - 16 * bt.par))
        if bt.off >= 2:
            dve.wait_ge(c.xh_done, bt.val(1, -1))
            dve.wait_ge(c.ctx_rstd, bt.val(1, 0))
    if part < 3:
        for n in range(4 * part, 4 * part + 4):
            r = rows_of(n)
            ins = dve.bn_stats(c.cst[0:r, n, :], c.raw[bt.par][0:r, n, :])
        if part == 2:
            ins.then_inc(c.ctx_stat, 1)
    else:
        dve.wait_ge(c.ctx_stat, bt.val(3, 1))
        dve.sem_inc(c.dve_waited, 1)
        for n in range(NTILE):
            r = rows_of(n)
            ins = dve.bn_aggr(c.cmv[bt.par][0:r, n, :], c.cst[0:r, n, :])
        ins.then_inc(c.ctx_stat, 1)
        dve.wait_ge(c.ctx_stat, bt.val(3, 2))
        if bt.off >= 1:
            dve.wait_ge(c.ctx_rstd, bt.val(1, 0))
        dve.tensor_scalar(c.cve[:, :], c.cmv[bt.par][:, :, 1], EPS, None, ALU.add).then_inc(c.ctx_stat, 1)


def context_rstd(pool, c, nhalf, bt):
    pool.wait_ge(c.ctx_stat, bt.val(3, 3))
    if bt.off >= 2:
        pool.wait_ge(c.xh_done, bt.val(1, -1))
    pool.tensor_tensor(out=c.crs[bt.par][:, :], in0=c.cve[:, :], in1=nhalf[:, 0:NTILE], op=ALU.pow).then_inc(c.ctx_rstd, 1)


def context_norm(dve, c, bt, part):
    if part == 0:
        dve.wait_ge(c.ctx_rstd, bt.val(1, 1))
        if bt.off >= 1:
            dve.wait_ge(c.xa_lo_done, bt.val(1, 0))
    for n in range(4 * part, 4 * part + 4):
        r = rows_of(n)
        ins = dve.tensor_scalar(c.xh[0:r, n, 1:D], c.raw[bt.par][0:r, n, 1:D], c.cmv[bt.par][0:r, n, 0:1],
                                c.crs[bt.par][0:r, n:n + 1], ALU.subtract, ALU.mult)
    if part == 2:
        ins.then_inc(c.xh_done, 1)


def context_hi(act, c, bt):
    act.wait_ge(c.xh_done, bt.val(1, 1))
    if bt.off >= 2:
        act.wait_ge(c.pv_done, bt.val(2 * NTILE, -2 * NTILE))
    act.activation(c.xa_hi[bt.par][:, :, :], c.xh[:, :, :], ACT.Copy).then_inc(c.xa_hi_done, 1)


def context_lo(pool, c, bt):
    pool.wait_ge(c.xa_hi_done, bt.val(1, 1))
    if bt.off >= 2:
        pool.wait_ge(c.pv_done, bt.val(2 * NTILE, -2 * NTILE))
    pool.tensor_tensor(out=c.xa_lo[bt.par][:, :, :], in0=c.xh[:, :, :], in1=c.xa_hi[bt.par][:, :, :],
                       op=ALU.subtract).then_inc(c.xa_lo_done, 1)


AHEAD = 9


def side_work(first, last):
    own = [("M", m, c) for m in range(AHEAD, NM) for c in range(3)]
    nxt = [("M", m, c) for m in range(AHEAD) for c in range(3)]
    w = {(u, n): [] for u in range(2) for n in range(NTILE)}

    def put(u, counts, works):
        for n, k in counts:
            w[u, n] += [works.pop(0) for _ in range(k)]

    if not last:
        put(0, ((10, 1), (11, 1)), [("T", 0), ("T", 1)])
        put(1, ((0, 1), (1, 1)), [("T", 2), ("T", 3)])
        put(1, ((1, 3), (2, 4), (3, 4), (4, 4), (5, 3), (6, 3), (7, 2)), nxt)
        w[1, 7] += [("R", 0), ("R", 1)]
        put(1, ((8, 1), (9, 1), (10, 1), (11, 1)), nxt)
    if not first:
        put(0, ((8, 1), (9, 1), (10, 1)), [("Y", 1, g) for g in range(3)])
    put(0, ((0, 2), (1, 1), (2, 3), (3, 1), (4, 3), (5, 1), (6, 1)), own)
    w[0, 7] += [("R", 2), ("R", 3)]
    if not last:
        for g, n in enumerate((1, 3, 5, 6)):
            w[0, n].insert(0, ("q", g))
    put(1, ((9, 1), (10, 1), (11, 1)), [("Y", 0, g) for g in range(3)])
    return w


START_WORK = ([("T", 0), ("T", 1)] + [("q", g) for g in range(4)] + [("M", m, c) for m in range(5) for c in range(3)]
              + [("T", 2), ("T", 3)] + [("M", m, c) for m in range(5, AHEAD) for c in range(3)] + [("R", 0), ("R", 1)])
WORKS, ACTS = 57, 8
TAIL_WORK = [("Y", 1, g) for g in range(3)]


class Works:

    def __init__(self, bt, first, last, start=False, tail=False):
        self.bt, self.tail = bt, tail
        if start:
            self.base, self.base_dve, self.base_act = (0, 0), (0, 0), (0, 0)
            flat = [(None, w) for w in START_WORK]
        else:
            n = len(START_WORK)
            if first:
                self.base, self.base_dve = (0, n), (0, n - ACTS)
            else:
                self.base, self.base_dve = (WORKS, n - 3), (WORKS - ACTS, n - 3 - ACTS)
            self.base_act = (ACTS, ACTS)
            if tail:
                lost = ACTS + 3 * AHEAD + 2
                self.base = (WORKS, n - 3 - lost)
                self.base_dve = (WORKS - ACTS, n - 3 - ACTS - (lost - ACTS))
                self.base_act = (ACTS, 0)
                flat = [(None, w) for w in TAIL_WORK]
            else:
                plan = side_work(first, last)
                flat = [(k, w) for k in sorted(plan) for w in plan[k]]
        self.flat = flat

    def number(self, k):
        return self.bt.val(self.base[0], self.base[1] + k)

    def bank(self, k):
        c, n = self.base
        return (c * self.bt.off + n + k) % 2

    def is_act(self, k):
        return self.flat[k][1][0] in ("q", "T")

    def taken(self, k):
        acts = sum(self.is_act(j) for j in range(k + 1)) if k >= 0 else 0
        if k >= 0 and self.is_act(k):
            return self.bt.val(self.base_act[0], self.base_act[1] + acts)
        return self.bt.val(self.base_dve[0], self.base_dve[1] + k + 1 - acts)

    def at(self, key):
        return [(k, w) for k, (s, w) in enumerate(self.flat) if s == key]

    def find(self, work):
        return next(k for k, (_, w) in enumerate(self.flat) if w == work)


LEAD = 4
E_SLOTS, P_SLOTS = 4, 6
POOL_TILES = ((0, 2, 5, 8, 10), (0, 2, 3, 4, 5, 6, 8, 10))
MCUT = (0, 482, 963, T)
Y_HEADS = ((0, 1, 2), (3, 4, 5), (6, 7))


def lo_count(bt, u, n):
    both = len(POOL_TILES[0]) + len(POOL_TILES[1])
    pool = (len(POOL_TILES[0]) if u else 0) + sum(k <= n for k in POOL_TILES[u])
    if n in POOL_TILES[u]:
        return bt.val(both, pool)
    return bt.val(2 * NTILE - both, NTILE * u + n + 1 - pool)


def tile_number(bt, u, n):
    return bt.val(2 * NTILE, NTILE * u + n)


def rows_of(n):
    return P if n < TF else TR


def cross(nc, a, m, ps):
    with ExitStack() as ctx:
        def sb(name, shape, dt=F32):
            return ctx.enter_context(nc.sbuf_tensor(name, shape, dt))

        def sem(name):
            return ctx.enter_context(nc.semaphore(name))

        ident16, nhalf = m["ident16"], m["nhalf"]
        w2h, sc1, kb, x1, x2 = m["w2h"], m["sc1"], m["kb"], m["x1"], m["x2"]
        qa_hi, qa_lo, ln_hi, ln_lo = m["qa_hi"], m["qa_lo"], m["ln_hi"], m["ln_lo"]
        xT_hi = [sb(f"xT_hi{i}", [D, NTILE * P], F16) for i in range(2)]
        xT_lo = [sb(f"xT_lo{i}", [D, NTILE * P], F16) for i in range(2)]
        sc_cur, kb_cur = sb("sc_cur", [D, H]), sb("kb_cur", [D, H])
        q32 = sb("q32", [D, HQ])
        q_hi = [sb(f"q_hi{i}", [D, HQ], F16) for i in range(2)]
        q_lo = [sb(f"q_lo{i}", [D, HQ], F16) for i in range(2)]
        mxp = sb("mxp", [P, NM, 3])
        nm = sb("nm", [P, NM], F16)
        e32 = [sb(f"e32_{i}", [P, 2, CH]) for i in range(E_SLOTS)]
        p_hi = [sb(f"p_hi{i}", [P, 2, CH], F16) for i in range(P_SLOTS)]
        p_lo = [sb(f"p_lo{i}", [P, 2, CH], F16) for i in range(P_SLOTS)]
        uT = [sb(f"uT{i}", [D, 2, CH]) for i in range(2)]
        ry = sb("ry", [S, H])
        acc = sb("acc", [S, D])
        yst, ymv, yve, yrs = sb("yst", [S, 6]), sb("ymv", [S, 2]), sb("yve", [S, 1]), sb("yrs", [S, 1])

        cx = m["context"]
        xa_hi, xa_lo, xh_done, xa_hi_done, xa_lo_done, pv_done, dve_waited = (
            cx.xa_hi, cx.xa_lo, cx.xh_done, cx.xa_hi_done, cx.xa_lo_done, cx.pv_done, cx.dve_waited)
        init_done, cur_done = sem("maxima_init"), sem("cur_done")
        q_hi_done, q_lo_done = sem("q_hi_done"), sem("q_lo_done")
        work_rdy, work_dve, work_act, nm_done = sem("work_rdy"), sem("work_dve"), sem("work_act"), sem("nm_done")
        s_rdy, exp_done, lo_dve, lo_pool = sem("s_rdy"), sem("exp_done"), sem("lo_dve"), sem("lo_pool")
        u_done, y_chain, y_norm, y_rstd = (sem(n) for n in ("u_done", "y_chain", "y_norm", "y_rstd"))


        block = ctx.enter_context(nc.Block())

        def s_banks(n, rows):
            return ps[0:rows, 2 * (n % 2):2 * (n % 2) + 2, 0:CH]

        def wbank(w, k):
            return ps[:, 6 + w.bank(k), :]

        @block.sync
        def _(sp):
            with sp.Fori(1, B // 2) as i:
                for off in range(2):
                    bt = Batch(i, off)
                    sp.wait_ge(xh_done, bt.val(1, -1))
                    context_load(sp, cx, a, bt)

        @block.gpsimd
        def _(pool):
            def current(bt):
                x = bt.index()
                pool.tensor_copy(sc_cur[:, :], sc1[:, bass.ds(x, 1), :].rearrange("d a h -> d (a h)"))
                pool.tensor_copy(kb_cur[:, :], kb[:, bass.ds(x, 1), :].rearrange("d a h -> d (a h)")).then_inc(cur_done, 1)

            def queries_lo(bt, g):
                cols = slice(g * CH, (g + 1) * CH)
                pool.wait_ge(q_hi_done, bt.val(4, g + 1))
                if bt.off >= 2:
                    pool.wait_ge(s_rdy, bt.val(2 * NTILE, -2 * NTILE))
                pool.tensor_tensor(out=q_lo[bt.par][:, cols], in0=q32[:, cols], in1=q_hi[bt.par][:, cols],
                                   op=ALU.subtract).then_inc(q_lo_done, 1)

            def low_half(bt, u, n):
                t, r = NTILE * u + n, rows_of(n)
                pool.wait_ge(exp_done, bt.val(4 * NTILE, 2 * t + 2))
                if bt.off or t >= P_SLOTS:
                    pool.wait_ge(pv_done, bt.val(2 * NTILE, t - P_SLOTS + 1))
                pool.tensor_tensor(out=p_lo[t % P_SLOTS][0:r, :, :], in0=e32[t % E_SLOTS][0:r, :, :], in1=p_hi[t % P_SLOTS][0:r, :, :],
                                   op=ALU.subtract).then_inc(lo_pool, 1)

            def y_rstd_pow(bt):
                pool.wait_ge(y_norm, bt.val(4, 3))
                pool.tensor_tensor(out=yrs[:, :], in0=yve[:, :], in1=nhalf[0:S, 0:1], op=ALU.pow).then_inc(y_rstd, 1)

            def one_batch(bt, first, last):
                nx = bt.next()
                if not last:
                    current(nx)
                for n in POOL_TILES[0]:
                    low_half(bt, 0, n)
                    if n == 2 and not last:
                        queries_lo(nx, 0)
                    if n == 5 and not last:
                        context_rstd(pool, cx, nhalf, nx)
                        queries_lo(nx, 1)
                    if n in (8, 10) and not last:
                        queries_lo(nx, n // 2 - 2 if n == 8 else 3)
                if not last:
                    context_lo(pool, cx, nx)
                for n in POOL_TILES[1]:
                    low_half(bt, 1, n)
                    if n == 0 and not first:
                        y_rstd_pow(bt.next(-1))

            b0 = Batch(None, 0)
            pool.memset(mxp[:, :, :], 0.0).then_inc(init_done, 1)
            current(b0)
            for g in range(4):
                queries_lo(b0, g)
            over_batches(pool, one_batch)
            y_rstd_pow(Batch(None, B - 1))

        @block.scalar
        def _(act):
            def take_transposes(bt, w, k):
                j = w.flat[k][1][1]
                dst = (xT_hi, xT_lo)[j // 2][bt.par]
                c0, c1 = ((0, 8 * P), (8 * P, T))[j % 2]
                act.wait_ge(work_rdy, w.number(k) + 1)
                act.activation(dst[:, c0:c1], wbank(w, k).bitcast(F16)[:, 0:c1 - c0], ACT.Copy).then_inc(work_act, 1)

            def take_queries(bt, w, k):
                g = w.flat[k][1][1]
                act.wait_ge(cur_done, bt.val(1, 1))
                if bt.off >= 1:
                    act.wait_ge(q_lo_done, bt.val(4, -4 + g + 1))
                act.wait_ge(work_rdy, w.number(k) + 1)
                for j in range(4):
                    h = 4 * g + j
                    ins = act.activation(q32[:, h * S:(h + 1) * S], wbank(w, k)[:, j * S:(j + 1) * S], ACT.Identity,
                                         bias=kb_cur[:, h:h + 1], scale=sc_cur[:, h:h + 1])
                ins.then_inc(work_act, 1)

            def queries_hi(bt, w, k):
                g = w.flat[k][1][1]
                if bt.off >= 2:
                    act.wait_ge(s_rdy, bt.val(2 * NTILE, -2 * NTILE))
                act.wait_ge(work_act, w.taken(k))
                cols = slice(g * CH, (g + 1) * CH)
                act.activation(q_hi[bt.par][:, cols], q32[:, cols], ACT.Copy).then_inc(q_hi_done, 1)

            def take_values(bt, u):
                act.wait_ge(pv_done, bt.val(2 * NTILE, NTILE * (u + 1)))
                if bt.off or bt.i is not None:
                    w = Works(bt, False, bt.is_last()) if u else Works(bt.next(-1), False, False)
                    act.wait_ge(work_rdy, w.number(w.find(("Y", u, 2))) + 1)
                for c in range(2):
                    act.activation(uT[u][:, c, :], ps[:, 4 + c, 0:CH], ACT.Copy).then_inc(u_done, 1)

            def one_batch(bt, first, last):
                w = Works(bt, first, last)
                for u in range(2):
                    for n in range(NTILE):
                        t, r = NTILE * u + n, rows_of(n)
                        act.wait_ge(s_rdy, bt.val(2 * NTILE, t + 1))
                        if not first or t >= E_SLOTS:
                            pb, pt = (bt, t - E_SLOTS) if t >= E_SLOTS else (bt.next(-1), t - E_SLOTS + 2 * NTILE)
                            pu, pn = divmod(pt, NTILE)
                            act.wait_ge(lo_pool if pn in POOL_TILES[pu] else lo_dve, lo_count(pb, pu, pn))
                        act.activation(e32[t % E_SLOTS][0:r, :, :], s_banks(t, r), ACT.Exp).then_inc(exp_done, 1)
                        if not first or t >= P_SLOTS:
                            act.wait_ge(pv_done, bt.val(2 * NTILE, t - P_SLOTS + 1))
                        act.activation(p_hi[t % P_SLOTS][0:r, :, :], s_banks(t, r), ACT.Exp).then_inc(exp_done, 1)
                        if t >= LEAD - 2:
                            for k, x in w.at(divmod(t - LEAD + 2, NTILE)):
                                if x[0] == "T":
                                    take_transposes(bt.next(), w, k)
                                elif x[0] == "q":
                                    take_queries(bt.next(), w, k)
                            if t > LEAD - 2:
                                for k, x in w.at(divmod(t - LEAD + 1, NTILE)):
                                    if x[0] == "q":
                                        queries_hi(bt.next(), w, k)
                        if t == 10 and not last:
                            context_hi(act, cx, bt.next())
                        if n == LEAD - 3:
                            if u:
                                take_values(bt, 0)
                            elif not first:
                                take_values(bt.next(-1), 1)

            w0 = Works(Batch(None, 0), False, False, start=True)
            for k, (_, x) in enumerate(w0.flat):
                if x[0] == "T":
                    take_transposes(Batch(None, 0), w0, k)
                elif x[0] == "q":
                    take_queries(Batch(None, 0), w0, k)
                    queries_hi(Batch(None, 0), w0, k)
            over_batches(act, one_batch)
            take_values(Batch(None, B - 1), 1)

        @block.vector
        def _(dve):
            def low_half(bt, u, n):
                t, r = NTILE * u + n, rows_of(n)
                dve.wait_ge(exp_done, bt.val(4 * NTILE, 2 * t + 2))
                if bt.off or t >= P_SLOTS:
                    dve.wait_ge(pv_done, bt.val(2 * NTILE, t - P_SLOTS + 1))
                dve.tensor_tensor(out=p_lo[t % P_SLOTS][0:r, :, :], in0=e32[t % E_SLOTS][0:r, :, :], in1=p_hi[t % P_SLOTS][0:r, :, :],
                                  op=ALU.subtract).then_inc(lo_dve, 1)

            def take(bt, nx, w, k):
                x = w.flat[k][1]
                src = wbank(w, k)
                dve.wait_ge(work_rdy, w.number(k) + 1)
                if x[0] == "M":
                    mt, c = x[1:]
                    r = min(P, HQ - mt * P)
                    ob = nx if mt < AHEAD else bt
                    if c == 0 and mt in (0, 7) and ob.off >= 1:
                        dve.wait_ge(nm_done, ob.val(2, 0 if mt else -1))
                    dve.tensor_reduce(mxp[0:r, mt, c:c + 1], src[0:r, 0:MCUT[c + 1] - MCUT[c]], AX_X, ALU.max).then_inc(work_dve, 1)
                    if c == 2 and mt in (6, NM - 1):
                        tiles = slice(0, 7) if mt == 6 else slice(7, NM)
                        dve.wait_ge(work_dve, w.taken(k))
                        dve.tensor_reduce(nm[:, tiles], mxp[:, tiles, :], AX_X, ALU.max, negate=True).then_inc(nm_done, 1)
                elif x[0] == "R":
                    c0, c1 = row_cols(x[1])
                    ob = nx if x[1] < 2 else bt
                    if x[1] == 0:
                        dve.wait_ge(q_lo_done, ob.val(4, 4))
                    dve.tensor_scalar(q_hi[ob.par][0:1, c0:c1], src[0:1, 0:c1 - c0], HEADROOM, None, ALU.add).then_inc(work_dve, 1)
                else:
                    half, g = x[1:]
                    ob = bt.next(-1) if half and not w.tail else bt
                    hs = Y_HEADS[g]
                    yv = src[0:S, 0:len(hs) * (D + 1)].rearrange("s (h n) -> s h n", n=D + 1)
                    base = 8 * half + 3 * g
                    if half == 0 and g == 0 and (ob.off >= 1):
                        dve.wait_ge(y_norm, ob.val(4, 0))
                    h0 = 8 * half + hs[0]
                    dve.reciprocal(ry[:, h0:h0 + len(hs)], yv[:, :, D]).then_inc(y_chain, 1)
                    dve.wait_ge(y_chain, ob.val(16, base + 1))
                    for j, _ in enumerate(hs):
                        if half == 0 and g == 0 and j == 0:
                            add = x1[:, bass.ds(ob.index(), 1), :].rearrange("s a d -> s (a d)")
                        else:
                            add = acc[:, :]
                        ins = dve.scalar_tensor_tensor(out=acc[:, :], in0=yv[:, j, 0:D], scalar=ry[:, h0 + j:h0 + j + 1], in1=add,
                                                       op0=ALU.mult, op1=ALU.add)
                        if j < len(hs) - 1:
                            ins.then_inc(y_chain, 1)
                            dve.wait_ge(y_chain, ob.val(16, base + j + 2))
                        else:
                            ins.then_inc(work_dve, 1)
                    if half == 1 and g == 2:
                        dve.wait_ge(work_dve, w.taken(k))
                        dve.bn_stats(yst[:, :], acc[:, :]).then_inc(y_norm, 1)
                        dve.wait_ge(y_norm, ob.val(4, 1))
                        dve.sem_inc(dve_waited, 1)
                        dve.bn_aggr(ymv[:, :], yst[:, :]).then_inc(y_norm, 1)
                        dve.wait_ge(y_norm, ob.val(4, 2))
                        dve.tensor_scalar(yve[:, :], ymv[:, 1:2], EPS, None, ALU.add).then_inc(y_norm, 1)

            def layer_norm(bt):
                dve.wait_ge(y_rstd, bt.val(1, 1))
                dve.tensor_scalar(x2[:, bass.ds(bt.index(), 1), :].rearrange("s a d -> s (a d)"), acc[:, :], ymv[:, 0:1], yrs[:, 0:1],
                                  ALU.subtract, ALU.mult).then_inc(y_norm, 1)

            def one_batch(bt, first, last):
                w, nx = Works(bt, first, last), bt.next()
                for u in range(2):
                    for n in range(NTILE):
                        before = [] if (u, n) == (0, 0) else w.at((u, n - 1) if n else (u - 1, NTILE - 1))
                        before = [k for k, x in before if x[0] not in ("q", "T")]
                        for k in before[:1]:
                            take(bt, nx, w, k)
                        t = NTILE * u + n + 1
                        if n == 0 and u == 0 and 0 not in POOL_TILES[0]:
                            low_half(bt, 0, 0)
                        if t < 2 * NTILE and t % NTILE not in POOL_TILES[t // NTILE]:
                            low_half(bt, *divmod(t, NTILE))
                        for k in before[1:]:
                            take(bt, nx, w, k)
                        if u == 0 and n < 4 and not last:
                            context_stats(dve, cx, nx, n)
                        if u == 0 and n in (5, 6, 7) and not last:
                            context_norm(dve, cx, nx, n - 5)
                        if u == 1 and n == 2 and not first:
                            layer_norm(bt.next(-1))
                for k, x in w.at((1, NTILE - 1)):
                    take(bt, nx, w, k)

            b0 = Batch(None, 0)
            w0 = Works(b0, False, False, start=True)
            dve.wait_ge(init_done, 1)
            for k, (_, x) in enumerate(w0.flat):
                if x[0] not in ("q", "T"):
                    take(b0, b0, w0, k)
            over_batches(dve, one_batch)
            bl = Batch(None, B - 1)
            wt = Works(bl.next(), False, False, tail=True)
            for k in range(3):
                take(bl, bl, wt, k)
            layer_norm(bl)

        @block.tensor
        def _(pe):
            def work(bt, nx, w, k):
                x = w.flat[k][1]
                dst = wbank(w, k)
                if k >= 2:
                    pe.wait_ge(work_act if w.is_act(k - 2) else work_dve, w.taken(k - 2))
                elif w.base[1] or w.base[0]:
                    pe.wait_ge(work_dve, bt_val_dve(w, k))
                if x[0] == "q":
                    tokens = bass.ds(nx.val(S, 0), S)
                    for j in range(4):
                        out, h = dst[:, j * S:(j + 1) * S], 4 * x[1] + j
                        pe.matmul(out, qa_hi[:, h, :], ln_hi[:, tokens], start=True, stop=False)
                        pe.matmul(out, qa_hi[:, h, :], ln_lo[:, tokens], start=False, stop=False)
                        last = pe.matmul(out, qa_lo[:, h, :], ln_hi[:, tokens], start=False, stop=True)
                elif x[0] == "T":
                    j = x[1]
                    src = (xa_hi, xa_lo)[j // 2][nx.par]
                    pe.wait_ge((xa_hi_done, xa_lo_done)[j // 2], nx.val(1, 1))
                    n0, n1 = ((0, 8), (8, NTILE))[j % 2]
                    for n in range(n0, n1):
                        r = rows_of(n)
                        c = (n - n0) * P
                        last = pe.transpose(dst.bitcast(F16)[:, c:c + r], src[0:r, n, :], ident16[0:r, 0:r])
                elif x[0] == "M":
                    mt, c = x[1:]
                    ob = nx if mt < AHEAD else bt
                    r = min(P, HQ - mt * P)
                    if c == 0:
                        pe.wait_ge(q_hi_done, ob.val(4, -(-min((mt + 1) * P, HQ) // CH)))
                    if c == 0 and mt in (0, 7):
                        pe.wait_ge(work_act, ob.val(ACTS, 6))
                    last = pe.matmul(dst[0:r, 0:MCUT[c + 1] - MCUT[c]], q_hi[ob.par][:, mt * P:mt * P + r],
                                     xT_hi[ob.par][:, MCUT[c]:MCUT[c + 1]], start=True, stop=True)
                elif x[0] == "R":
                    c0, c1 = row_cols(x[1])
                    ob = nx if x[1] < 2 else bt
                    pe.wait_ge(nm_done, ob.val(2, 1 + x[1] // 2))
                    for c in range(c0, c1, P):
                        r = min(P, c1 - c)
                        last = pe.matmul(dst[0:1, c - c0:c - c0 + r], nm[0:r, c // P:c // P + 1], ident16[0:r, 0:r], start=True, stop=True)
                else:
                    half, g = x[1:]
                    ob = bt.next(-1) if half and not w.tail else bt
                    if g == 0:
                        pe.wait_ge(u_done, ob.val(4, 2 * half + 2))
                    for j, h in enumerate(Y_HEADS[g]):
                        last = pe.matmul(dst[0:S, j * (D + 1):(j + 1) * (D + 1)],
                                         uT[half][:, :, :].rearrange("d c n -> d (c n)")[:, h * S:(h + 1) * S],
                                         w2h[:, half * 8 + h, :], start=True, stop=True)
                last.then_inc(work_rdy, 1)

            def bt_val_dve(w, k):
                return w.bt.val(w.base_dve[0], w.base_dve[1] - 1 + k)

            def scores(bt, u, n, c):
                t, r = NTILE * u + n, rows_of(n)
                if c == 0:
                    if n == 0:
                        if bt.i is None and bt.off == 0:
                            w = Works(bt, u == 1, False, start=u == 0)
                        else:
                            w = Works(bt, False, bt.is_last()) if u else Works(bt.next(-1), False, False)
                        pe.wait_ge(work_dve, w.taken(w.find(("R", 1 if u == 0 else 3))))
                        pe.wait_ge(q_lo_done, bt.val(4, 4))
                        pe.wait_ge(work_act, bt.val(ACTS, ACTS))
                    if not (bt.i is None and bt.off == 0 and t < 2):
                        pe.wait_ge(exp_done, bt.val(4 * NTILE, 2 * (t - 1)))
                out = ps[0:r, 2 * (t % 2) + c, 0:CH]
                cols = slice(u * HALF + c * CH, u * HALF + (c + 1) * CH)
                hi, lo = xT_hi[bt.par][:, n * P:n * P + r], xT_lo[bt.par][:, n * P:n * P + r]
                pe.matmul(out, hi, q_hi[bt.par][:, cols], start=True, stop=False)
                pe.matmul(out, hi, q_lo[bt.par][:, cols], start=False, stop=False)
                last = pe.matmul(out, lo, q_hi[bt.par][:, cols], start=False, stop=True)
                if c == 1:
                    last.then_inc(s_rdy, 1)

            def values(bt, u, n, c):
                t, r = NTILE * u + n, rows_of(n)
                if c == 0:
                    if n == 0 and not (bt.i is None and bt.off == 0 and u == 0):
                        pe.wait_ge(u_done, bt.val(4, 2 * u))
                    pe.wait_ge(exp_done, bt.val(4 * NTILE, 2 * t + 2))
                out = ps[:, 4 + c, 0:CH]
                hi, lo = xa_hi[bt.par][0:r, n, :], xa_lo[bt.par][0:r, n, :]
                pe.matmul(out, hi, p_hi[t % P_SLOTS][0:r, c, :], start=n == 0, stop=False)
                pe.matmul(out, lo, p_hi[t % P_SLOTS][0:r, c, :], start=False, stop=False)
                if c == 0:
                    pe.wait_ge(lo_pool if n in POOL_TILES[u] else lo_dve, lo_count(bt, u, n))
                last = pe.matmul(out, hi, p_lo[t % P_SLOTS][0:r, c, :], start=False, stop=n == NTILE - 1)
                if c == 1:
                    last.then_inc(pv_done, 1)

            def one_batch(bt, first, last):
                w, nx = Works(bt, first, last), bt.next()
                for u in range(2):
                    for n in range(NTILE):
                        todo = [k for k, _ in w.at((u, n))]
                        t3 = NTILE * u + n + LEAD
                        sb_, st = (bt, t3) if t3 < 2 * NTILE else (nx, t3 - 2 * NTILE)
                        ahead = not (last and t3 >= 2 * NTILE)
                        for part in range(4):
                            if part < 2:
                                values(bt, u, n, part)
                            elif ahead:
                                scores(sb_, st // NTILE, st % NTILE, part - 2)
                            take_n = -(-len(todo) // (4 - part))
                            for k in todo[:take_n]:
                                work(bt, nx, w, k)
                            todo = todo[take_n:]

            b0 = Batch(None, 0)
            w0 = Works(b0, False, False, start=True)
            for k in range(len(w0.flat)):
                work(b0, b0, w0, k)
            for n in range(LEAD):
                for c in range(2):
                    scores(b0, 0, n, c)
            over_batches(pe, one_batch)
            bl = Batch(None, B - 1)
            wt = Works(bl.next(), False, False, tail=True)
            for k in range(3):
                work(bl, bl, wt, k)


def row_cols(r):
    t0 = (0, 4, 7, 11, NM)
    return t0[r] * P, min(t0[r + 1] * P, HQ)


def ffn(nc, a, m, ps, out):
    with ExitStack() as ctx:
        def sb(name, shape, dt=F32):
            return ctx.enter_context(nc.sbuf_tensor(name, shape, dt))

        def sem(name):
            return ctx.enter_context(nc.semaphore(name))

        ident, nhalf, x2 = m["ident"], m["nhalf"], m["x2"]
        NC = NE // P
        K8 = 8
        HK = FH * K8
        QP = 25

        f_wq, f_wqt = sb("f_wq", [D, NB * KD]), sb("f_wqt", [KD, NB, D])
        f_keys, f_down, f_up = sb("f_keys", [KD, NB, KEYS]), sb("f_down", [D, NE]), sb("f_up", [P, NC, D])
        f_gam, f_bet = sb("f_gam", [KD, NB]), sb("f_bet", [KD, NB])
        x2T, xcT, xct = sb("x2T", [D, NT]), sb("xcT", [D, NT]), sb("xct", [S, B, D])
        msum, mean = sb("msum", [D, 1]), sb("mean", [D, 1])
        cov, cw = sb("cov", [D, D]), sb("cw", [KD, NB, D])
        var, vrs, gain = sb("var", [KD, NB]), sb("vrs", [KD, NB]), sb("gain", [KD, NB])
        kscaled, sim_w, sim_c = sb("kscaled", [KD, NB, KEYS]), sb("sim_w", [D, NB * KEYS]), sb("sim_c", [1, NB * KEYS])
        ones_r = sb("ones_r", [1, S])
        off8 = sb("off8", [P, 1])
        iota_i = sb("iota_i", [P, P], mybir.dt.int32)
        iota_f, iota_w = sb("iota_f", [P, P]), sb("iota_w", [P, P, S], F16)
        iota_c, iota_j = sb("iota_c", [P, 2 * NC, S], F16), sb("iota_j", [P, K8, K8], F16)
        ones_col = sb("ones_col", [P, 1])
        xc_cur = sb("xc_cur", [D, 2, S])
        simb = sb("simb", [S, 2, NB, KEYS])
        top, idx, idxf = sb("top", [S, 2, NB, K8]), sb("idx", [S, 2, NB, K8], U32), sb("idxf", [S, 2, NB, K8], F16)
        comb = sb("comb", [S, 2, FH, K8, K8])
        sc, pk = sb("sc", [S, 2, FH, K8]), sb("pk", [S, 2, FH, K8], U32)
        pij, pijf = sb("pij", [S, 2, 2, HK], U32), sb("pijf", [S, 2, 2, HK], F16)
        idxw, eq = sb("idxw", [S, 2 * NB, K8, K8], F16), sb("eq", [S, 2 * NB, K8, K8], F16)
        half4, half2 = sb("half4", [S, 2 * NB, 4, K8], F16), sb("half2", [S, 2 * NB, 2, K8], F16)
        ij = sb("ij", [S, 2, NB, K8], F16)
        eu, erc = sb("eu", [S, 2, HK], U32), sb("erc", [S, 2, 2, HK], U32)
        sel = sb("sel", [S, 3, 2, HK])
        dsc, esc = sb("dsc", [S, 2, FH, K8]), sb("esc", [S, 2, FH, K8])
        ssum, srec = sb("ssum", [S, 2, FH]), sb("srec", [S, 2, FH])
        rT, cT, w_hi, w_lo = sb("rT", [P, S], F16), sb("cT", [P, S], F16), sb("w_hi", [P, S], F16), sb("w_lo", [P, S], F16)
        oneh = sb("oneh", [P, P, S], F16)
        eqc = sb("eqc", [P, 2 * NC, S], F16)
        mv_hi, mv_lo = sb("mv_hi", [P, 2 * NC, S], F16), sb("mv_lo", [P, 2 * NC, S], F16)
        hid, hfac = ([sb(f"{n}{i}", [P, 2, 2 * 2 * S]) for i in range(2)] for n in ("hid", "hfac"))
        gel = [sb(f"gel{i}", [P, NC, 2, S]) for i in range(2)]
        wgt = sb("wgt", [P, NC, 2, S])
        zf, ost = sb("zf", [S, 2, D]), sb("ost", [S, 2, D])
        fst, fmv, fve, frs = sb("fst", [S, 2, 6]), sb("fmv", [S, 2, 2]), sb("fve", [S, 2]), sb("frs", [S, 2])

        f_ld, f_waited = sem("f_ld"), sem("f_waited")
        fc_done, x2T_ps, x2T_done, mean_done, xcT_done = (sem(n) for n in ("fc_done", "x2T_ps", "x2T_done", "mean_done", "xcT_done"))
        xct_ps, xct_done, cov_ps, cov_done = (sem(n) for n in ("xct_ps", "xct_done", "cov_ps", "cov_done"))
        cw_ps, cw_done, var_done, vrs_done, gain_done = (sem(n) for n in ("cw_ps", "cw_done", "var_done", "vrs_done", "gain_done"))
        simw_ps, simw_done, wide_done = sem("simw_ps"), sem("simw_done"), sem("wide_done")
        fcur_done, sim_ps, sim_done, top_done, comb_done, best_done = (sem(n) for n in ("fcur_done", "sim_ps", "sim_done", "top_done", "comb_done", "best_done"))
        dsc_done, esc_done, pick, sel_done, selT_ps, selT_done = (sem(n) for n in ("dsc_done", "esc_done", "pick", "sel_done", "selT_ps", "selT_done"))
        wlo_done, oneh_done, g_ps, g_done, y_ps, z_done, z_rstd, o_done, out_done = (
            sem("f" + n) for n in ("wlo_done", "oneh_done", "g_ps", "g_done", "y_ps", "z_done", "z_rstd", "o_done", "out_done"))
        h_ps, hid_done, hadd_done, hu_done, hth_done, gel_done = (
            sem(n) for n in ("h_ps", "hid_done", "hadd_done", "hu_done", "hth_done", "gel_done"))
        wide_idx, th_done, soft_done = sem("wide_idx"), sem("th_done"), sem("soft_done")

        block = ctx.enter_context(nc.Block())
        NPAIR = B // 2
        BN_C = 0.044715
        TANH_C = (2.0 / 3.141592653589793) ** 0.5

        @block.sync
        def _(sp):
            for dst, src in ((f_wq[:, :], a["L0_ffn_w_q"]),
                             (f_wqt[:, 0:FH, :], a["ffn_wq_t"][0:FH * KD, :].rearrange("(n e) d -> e n d", e=KD)),
                             (f_wqt[:, FH:NB, :], a["ffn_wq_t"][FH * KD:NB * KD, :].rearrange("(n e) d -> e n d", e=KD)),
                             (f_keys[:, :, :], a["ffn_keys_t"].rearrange("e s h k -> e (s h) k")),
                             (f_down[:, :], a["ffn_down_t"]),
                             (f_up[:, :, :], a["L0_ffn_up_embed"].rearrange("(c e) d -> e c d", e=P)),
                             (f_gam[:, :], a["L0_ffn_bn_gamma"]),
                             (f_bet[:, :], a["L0_ffn_bn_beta"])):
                sp.dma_start(dst, src).then_inc(f_ld, 16)
            with sp.Fori(0, NPAIR) as i:
                sp.wait_ge(o_done, i * 1 + 1)
                sp.dma_start(out[bass.ds(i * 2, 2), :, :].rearrange("b s d -> s b d"), ost[:, :, :]).then_inc(out_done, 16)
            sp.wait_ge(out_done, 16 * NPAIR)

        @block.gpsimd
        def _(pool):
            pool.iota(iota_i[:, :], pattern=[[1, P]], base=0, channel_multiplier=0).then_inc(fc_done, 1)
            pool.memset(ones_r[:, :], 1.0).then_inc(fc_done, 1)
            pool.memset(ones_col[:, :], 1.0).then_inc(fc_done, 1)
            pool.memset(off8[:, :], 0.0).then_inc(fc_done, 1)
            pool.wait_ge(fc_done, 4)
            pool.memset(off8[HK:P, :], float(NC)).then_inc(fc_done, 1)
            pool.wait_ge(fc_done, 5)
            pool.tensor_copy(iota_f[:, :], iota_i[:, :]).then_inc(fc_done, 1)
            pool.wait_ge(var_done, 3)
            pool.tensor_tensor(out=vrs[:, :], in0=var[:, :], in1=nhalf[:, 0:NB], op=ALU.pow).then_inc(vrs_done, 1)

            def step(i, par, first, second=False):
                pool.wait_ge(top_done, i * 2 + 1)
                if not first:
                    pool.wait_ge(best_done, i * 2)
                for hf in range(2):
                    ins = pool.tensor_tensor(out=comb[:, hf, :, :, :],
                                             in0=top[:, hf, 0:FH, :].rearrange("s h (i a) -> s h i a", a=1).to_broadcast([S, FH, K8, K8]),
                                             in1=top[:, hf, FH:NB, :].rearrange("s h (a j) -> s h a j", a=1).to_broadcast([S, FH, K8, K8]),
                                             op=ALU.add)
                ins.then_inc(comb_done, 1)
                for r in range(2):
                    pool.wait_ge(hadd_done, i * 2 + r + 1)
                    pool.tensor_tensor(out=hfac[r][:, :, :], in0=hfac[r][:, :, :], in1=hid[r][:, :, :], op=ALU.mult).then_inc(hu_done, 1)
                if not (first or second):
                    pool.wait_ge(g_done, i * 4 - 4)
                for r in range(2):
                    pool.wait_ge(hth_done, i * 2 + r + 1)
                    pool.tensor_tensor(out=gel[par][:, 4 * r:4 * r + 4, :, :].rearrange("e (b c) a s -> e b (c a s)", b=2),
                                       in0=hfac[r][:, :, :], in1=hid[r][:, :, :], op=ALU.mult).then_inc(gel_done, 1)

            def finish(i):
                pool.wait_ge(z_done, i * 4 + 4)
                pool.tensor_tensor(out=frs[:, :], in0=fve[:, :], in1=nhalf[0:S, 0:2], op=ALU.pow).then_inc(z_rstd, 1)

            step(0, 0, True)
            step(1, 1, False, True)
            with pool.Fori(0, (NPAIR - 2) // 2) as k:
                for off in range(2):
                    finish(k * 2 + off)
                    step(k * 2 + 2 + off, off, False)
            finish(NPAIR - 2)
            finish(NPAIR - 1)

        @block.scalar
        def _(act):
            for k in range(NG):
                act.wait_ge(x2T_ps, k + 1)
                act.activation(x2T[:, k * G * S:(k + 1) * G * S], ps[:, k, 0:G * S], ACT.Copy).then_inc(x2T_done, 1)
            for k in range(NG):
                act.wait_ge(xct_ps, k + 1)
                act.activation(xct[:, k * G:(k + 1) * G, :], ps[0:S, 4 + k, :].rearrange("s (b d) -> s b d", b=G), ACT.Copy).then_inc(xct_done, 1)
            act.wait_ge(cov_ps, 1)
            act.activation(cov[:, :], ps[:, 0, 0:D], ACT.Copy, scale=1.0 / NT).then_inc(cov_done, 1)
            act.wait_ge(fc_done, 6)
            act.activation(iota_w[:, :, :], iota_f[:, :].rearrange("p (e a) -> p e a", a=1).to_broadcast([P, P, S]), ACT.Copy)
            act.activation(iota_c[:, :, :], iota_f[:, 0:2 * NC].rearrange("p (e a) -> p e a", a=1).to_broadcast([P, 2 * NC, S]), ACT.Copy)
            act.activation(iota_j[:, :, :], iota_f[:, 0:K8].rearrange("p (j a) -> p j a", a=1).to_broadcast([P, K8, K8]),
                           ACT.Copy).then_inc(wide_done, 1)
            act.wait_ge(simw_ps, 1)
            act.activation(sim_w[:, :], ps[:, 5, :], ACT.Copy).then_inc(simw_done, 1)
            act.activation(sim_c[:, :], ps[0:1, 6, :], ACT.Copy).then_inc(simw_done, 1)
            def step(i, first):
                if not first:
                    act.wait_ge(sim_ps, i * 2)
                act.activation(xc_cur[:, :, :].rearrange("d a s -> d (a s)"), xcT[:, bass.ds(i * (2 * S), 2 * S)],
                               ACT.Copy).then_inc(fcur_done, 1)
                act.wait_ge(sim_ps, i * 2 + 2)
                if not first:
                    act.wait_ge(top_done, i * 2)
                act.activation(simb[:, :, :, :].rearrange("s a n k -> s a (n k)"), ps[0:S, 0:2, :], ACT.Copy).then_inc(sim_done, 1)
                for r in range(2):
                    act.wait_ge(h_ps, i * 2 + r + 1)
                    if not first:
                        act.wait_ge(gel_done, i * 2 + r - 1)
                    act.activation(hid[r][:, :, :], ps[:, 2:4, 0:4 * S], ACT.Copy)
                    act.activation(hfac[r][:, :, :], ps[:, 2:4, 0:4 * S], ACT.Square, scale=BN_C ** 0.5).then_inc(hid_done, 1)
                    act.wait_ge(hid_done, i * 2 + r + 1)
                    act.activation(hfac[r][:, :, :], hfac[r][:, :, :], ACT.Identity, bias=ones_col[:, 0:1]).then_inc(hadd_done, 1)
                act.wait_ge(pick, i * 7 + 1)
                act.activation(idxw[:, :, :, :], idxf[:, :, :, :].rearrange("s a n (j c) -> s (a n) j c", c=1).to_broadcast([S, 2 * NB, K8, K8]),
                               ACT.Copy).then_inc(wide_idx, 1)
                for r in range(2):
                    act.wait_ge(hu_done, i * 2 + r + 1)
                    act.activation(hfac[r][:, :, :], hfac[r][:, :, :], ACT.Tanh, scale=TANH_C).then_inc(th_done, 1)
                    act.wait_ge(th_done, i * 2 + r + 1)
                    act.activation(hfac[r][:, :, :], hfac[r][:, :, :], ACT.Identity, bias=ones_col[:, 0:1]).then_inc(hth_done, 1)
                act.wait_ge(dsc_done, i * 1 + 1)
                act.activation(esc[:, :, :, :], dsc[:, :, :, :], ACT.Exp).then_inc(esc_done, 1)
                act.wait_ge(selT_ps, i * 1 + 1)
                if not first:
                    act.wait_ge(oneh_done, i * 1)
                act.activation(rT[:, :], ps[:, 4, 0:S], ACT.Copy).then_inc(selT_done, 1)
                act.activation(cT[:, :], ps[:, 4, S:2 * S], ACT.Identity, bias=off8[:, 0:1]).then_inc(selT_done, 1)
                act.activation(w_hi[:, :], ps[:, 4, 2 * S:3 * S], ACT.Copy).then_inc(selT_done, 1)

            step(0, True)
            with act.Fori(1, NPAIR) as i:
                step(i, False)

        @block.vector
        def _(dve):
            dve.wait_ge(x2T_done, NG)
            dve.tensor_reduce(msum[:, :], x2T[:, :], AX_X, ALU.add).then_inc(mean_done, 1)
            dve.wait_ge(mean_done, 1)
            dve.tensor_scalar(mean[:, :], msum[:, :], 1.0 / NT, None, ALU.mult).then_inc(mean_done, 1)
            dve.wait_ge(mean_done, 2)
            dve.tensor_scalar(xcT[:, :], x2T[:, :], mean[:, 0:1], None, ALU.subtract).then_inc(xcT_done, 1)
            dve.wait_ge(f_ld, 16 * 8)
            for k in range(4):
                dve.wait_ge(cw_ps, k + 1)
                dve.tensor_tensor(out=cw[:, 4 * k:4 * k + 4, :], in0=ps[:, 1 + k, :].rearrange("e (n d) -> e n d", n=4),
                                  in1=f_wqt[:, 4 * k:4 * k + 4, :], op=ALU.mult).then_inc(cw_done, 1)
            dve.wait_ge(cw_done, 4)
            dve.tensor_reduce(var[:, :], cw[:, :, :], AX_X, ALU.add).then_inc(var_done, 1)
            dve.wait_ge(var_done, 1)
            dve.tensor_scalar(var[:, :], var[:, :], 0.0, None, ALU.max).then_inc(var_done, 1)
            dve.wait_ge(var_done, 2)
            dve.tensor_scalar(var[:, :], var[:, :], EPS, None, ALU.add).then_inc(var_done, 1)
            dve.wait_ge(vrs_done, 1)
            dve.tensor_tensor(out=gain[:, :], in0=vrs[:, :], in1=f_gam[:, :], op=ALU.mult).then_inc(gain_done, 1)
            dve.wait_ge(gain_done, 1)
            dve.tensor_tensor(out=kscaled[:, :, :], in0=f_keys[:, :, :],
                              in1=gain[:, :].rearrange("e (n a) -> e n a", a=1).to_broadcast([KD, NB, KEYS]), op=ALU.mult).then_inc(gain_done, 1)
            dve.wait_ge(wide_done, 1)

            def weigh(i, par, n):
                dve.wait_ge(g_ps, i * 4 + n + 1)
                if n == 0:
                    dve.wait_ge(gel_done, i * 2 + 2)
                cols = slice(n * QP, (n + 1) * QP)
                dve.tensor_tensor(out=wgt[:, :, :, cols].rearrange("e c a s -> e a c s"),
                                  in0=ps[:, 5 + n % 2, 0:QP * 2 * NC].rearrange("e (s a c) -> e a c s", a=2, c=NC),
                                  in1=gel[par][:, :, :, cols].rearrange("e c a s -> e a c s"), op=ALU.mult).then_inc(g_done, 1)

            def step(i, par, first, second=False, third=False):
                dve.wait_ge(sim_done, i * 1 + 1)
                if not first:
                    dve.wait_ge(comb_done, i * 1)
                    dve.wait_ge(pick, i * 7)
                dve.sem_inc(f_waited, 1)
                for hf in range(2):
                    for n in range(NB):
                        ins = dve.max(top[:, hf, n, :], simb[:, hf, n, :])
                    if hf == 1:
                        ins.then_inc(top_done, 1)
                    if not (first or second):
                        norm_stats(i - 2, hf)
                dve.wait_ge(top_done, i * 2 + 1)
                dve.sem_inc(f_waited, 1)
                for hf in range(2):
                    for n in range(NB):
                        ins = dve.max_index(idx[:, hf, n, :], top[:, hf, n, :], simb[:, hf, n, :])
                    if hf == 0 and not (first or second):
                        norm_stats(i - 2, 2)
                ins.then_inc(top_done, 1)
                if not (first or second):
                    last_norm(i - 2, third)
                dve.wait_ge(top_done, i * 2 + 2)
                dve.tensor_copy(idxf[:, :, :, :], idx[:, :, :, :]).then_inc(pick, 1)
                if not first:
                    weigh(i - 1, 1 - par, 0)
                    weigh(i - 1, 1 - par, 1)
                dve.wait_ge(comb_done, i * 1 + 1)
                dve.sem_inc(f_waited, 1)
                for hf in range(2):
                    for h in range(FH):
                        ins = dve.max(sc[:, hf, h, :], comb[:, hf, h, :, :].rearrange("s i j -> s (i j)"))
                ins.then_inc(best_done, 1)
                dve.wait_ge(best_done, i * 2 + 1)
                dve.sem_inc(f_waited, 1)
                for hf in range(2):
                    for h in range(FH):
                        ins = dve.max_index(pk[:, hf, h, :], sc[:, hf, h, :], comb[:, hf, h, :, :].rearrange("s i j -> s (i j)"))
                ins.then_inc(best_done, 1)
                if not first:
                    dve.wait_ge(esc_done, i * 1)
                dve.tensor_tensor(out=dsc[:, :, :, :], in0=sc[:, :, :, :], in1=sc[:, :, :, 0:1].to_broadcast([S, 2, FH, K8]),
                                  op=ALU.subtract).then_inc(dsc_done, 1)
                dve.wait_ge(best_done, i * 2 + 2)
                flat = pk[:, :, :, :].rearrange("s a h k -> s a (h k)")
                dve.tensor_scalar(pij[:, :, 0, :], flat, 3, None, ALU.logical_shift_right)
                dve.tensor_scalar(pij[:, :, 1, :], flat, K8 - 1, None, ALU.bitwise_and).then_inc(pick, 1)
                dve.wait_ge(pick, i * 7 + 2)
                dve.tensor_copy(pijf[:, :, :, :], pij[:, :, :, :]).then_inc(pick, 1)
                if not first:
                    weigh(i - 1, 1 - par, 2)
                dve.wait_ge(pick, i * 7 + 3)
                dve.tensor_tensor(out=eq[:, :, :, :],
                                  in0=pijf[:, :, :, :].rearrange("s a b (h c k) -> s (a b h) c k", h=FH, c=1).to_broadcast([S, 2 * NB, K8, K8]),
                                  in1=iota_j[0:S, :, :].rearrange("s (a j) k -> s a j k", a=1).to_broadcast([S, 2 * NB, K8, K8]),
                                  op=ALU.is_equal).then_inc(pick, 1)
                dve.wait_ge(esc_done, i * 1 + 1)
                dve.tensor_reduce(ssum[:, :, :], esc[:, :, :, :], AX_X, ALU.add).then_inc(soft_done, 1)
                dve.wait_ge(wide_idx, i * 1 + 1)
                dve.wait_ge(pick, i * 7 + 4)
                dve.tensor_tensor(out=eq[:, :, :, :], in0=eq[:, :, :, :], in1=idxw[:, :, :, :], op=ALU.mult).then_inc(pick, 1)
                dve.wait_ge(soft_done, i * 4 + 1)
                dve.reciprocal(srec[:, :, :], ssum[:, :, :]).then_inc(soft_done, 1)
                dve.wait_ge(pick, i * 7 + 5)
                dve.tensor_tensor(out=half4[:, :, :, :], in0=eq[:, :, 0:4, :], in1=eq[:, :, 4:8, :], op=ALU.add).then_inc(pick, 1)
                dve.wait_ge(soft_done, i * 4 + 2)
                dve.tensor_scalar(srec[:, :, :], srec[:, :, :], 0.5, None, ALU.mult).then_inc(soft_done, 1)
                dve.wait_ge(pick, i * 7 + 6)
                dve.tensor_tensor(out=half2[:, :, :, :], in0=half4[:, :, 0:2, :], in1=half4[:, :, 2:4, :], op=ALU.add).then_inc(pick, 1)
                dve.wait_ge(soft_done, i * 4 + 3)
                if not first:
                    dve.wait_ge(selT_ps, i * 1)
                dve.tensor_tensor(out=sel[:, 2, :, :].rearrange("s a (h k) -> s (a h) k", h=FH),
                                  in0=esc[:, :, :, :].rearrange("s a h k -> s (a h) k"),
                                  in1=srec[:, :, :].rearrange("s a (h c) -> s (a h) c", c=1).to_broadcast([S, 2 * FH, K8]),
                                  op=ALU.mult).then_inc(soft_done, 1)
                dve.wait_ge(pick, i * 7 + 7)
                dve.tensor_tensor(out=ij[:, :, :, :].rearrange("s a n k -> s (a n) k"), in0=half2[:, :, 0, :], in1=half2[:, :, 1, :],
                                  op=ALU.add).then_inc(sel_done, 1)
                dve.wait_ge(sel_done, i * 4 + 1)
                dve.scalar_tensor_tensor(out=eu[:, :, :], in0=ij[:, :, 0:FH, :].rearrange("s a h k -> s a (h k)"), scalar=float(KEYS),
                                         in1=ij[:, :, FH:NB, :].rearrange("s a h k -> s a (h k)"), op0=ALU.mult, op1=ALU.add).then_inc(sel_done, 1)
                dve.wait_ge(sel_done, i * 4 + 2)
                dve.tensor_scalar(erc[:, 0, :, :], eu[:, :, :], P - 1, None, ALU.bitwise_and)
                dve.tensor_scalar(erc[:, 1, :, :], eu[:, :, :], 7, None, ALU.logical_shift_right).then_inc(sel_done, 1)
                dve.wait_ge(sel_done, i * 4 + 3)
                dve.tensor_copy(sel[:, 0:2, :, :], erc[:, :, :, :]).then_inc(sel_done, 1)
                if not first:
                    weigh(i - 1, 1 - par, 3)
                dve.wait_ge(selT_done, i * 3 + 1)
                dve.tensor_tensor(out=oneh[:, :, :], in0=iota_w[:, :, :],
                                  in1=rT[:, :].rearrange("p (a s) -> p a s", a=1).to_broadcast([P, P, S]), op=ALU.is_equal)
                dve.wait_ge(selT_done, i * 3 + 3)
                dve.tensor_tensor(out=eqc[:, :, :], in0=iota_c[:, :, :],
                                  in1=cT[:, :].rearrange("p (a s) -> p a s", a=1).to_broadcast([P, 2 * NC, S]), op=ALU.is_equal).then_inc(wlo_done, 1)
                dve.tensor_tensor(out=w_lo[:, :], in0=ps[:, 4, 2 * S:3 * S], in1=w_hi[:, :], op=ALU.subtract).then_inc(wlo_done, 1)
                dve.wait_ge(wlo_done, i * 2 + 1)
                for w, dst in ((w_hi, mv_hi), (w_lo, mv_lo)):
                    if w is w_lo:
                        dve.wait_ge(wlo_done, i * 2 + 2)
                    ins = dve.tensor_tensor(out=dst[:, :, :], in0=eqc[:, :, :],
                                            in1=w[:, :].rearrange("p (a s) -> p a s", a=1).to_broadcast([P, 2 * NC, S]), op=ALU.mult)
                ins.then_inc(oneh_done, 1)

            def add_up(i, first=False):
                if not first:
                    dve.wait_ge(o_done, i * 1)
                dve.wait_ge(y_ps, i * 1 + 1)
                dve.tensor_tensor(out=zf[:, :, :], in0=ps[0:S, 7, 0:2 * D].rearrange("s (a d) -> s a d", a=2),
                                  in1=x2[:, bass.ds(i * 2, 2), :], op=ALU.add).then_inc(z_done, 1)

            def norm_stats(i, part):
                dve.wait_ge(z_done, i * 4 + part + 1)
                if part == 0:
                    for hf in range(2):
                        ins = dve.bn_stats(fst[:, hf, :], zf[:, hf, :])
                elif part == 1:
                    dve.sem_inc(f_waited, 1)
                    for hf in range(2):
                        ins = dve.bn_aggr(fmv[:, hf, :], fst[:, hf, :])
                else:
                    ins = dve.tensor_scalar(fve[:, :], fmv[:, :, 1], EPS, None, ALU.add)
                ins.then_inc(z_done, 1)

            def last_norm(i, first):
                dve.wait_ge(z_rstd, i * 1 + 1)
                if not first:
                    dve.wait_ge(out_done, i * 16)
                for hf in range(2):
                    ins = dve.tensor_scalar(ost[:, hf, :], zf[:, hf, :], fmv[:, hf, 0:1], frs[:, hf:hf + 1], ALU.subtract, ALU.mult)
                ins.then_inc(o_done, 1)

            step(0, 0, True)
            step(1, 1, False, second=True)
            add_up(0, True)
            step(2, 0, False, third=True)
            add_up(1)
            step(3, 1, False)
            add_up(2)
            with dve.Fori(0, (NPAIR - 4) // 2) as k:
                for off in range(2):
                    step(k * 2 + 4 + off, off, False)
                    add_up(k * 2 + 3 + off)
            for n in range(4):
                weigh(NPAIR - 1, (NPAIR - 1) % 2, n)
            for part in range(3):
                norm_stats(NPAIR - 2, part)
            last_norm(NPAIR - 2, False)
            add_up(NPAIR - 1)
            for part in range(3):
                norm_stats(NPAIR - 1, part)
            last_norm(NPAIR - 1, False)

        @block.tensor
        def _(pe):
            for k in range(NG):
                for j in range(G):
                    last = pe.transpose(ps[:, k, j * S:(j + 1) * S], x2[:, k * G + j, :], ident[0:S, 0:S])
                last.then_inc(x2T_ps, 1)
            pe.wait_ge(xcT_done, 1)
            for k in range(NG):
                for j in range(G):
                    b = k * G + j
                    last = pe.transpose(ps[0:S, 4 + k, j * D:(j + 1) * D], xcT[:, b * S:(b + 1) * S], ident[:, :])
                last.then_inc(xct_ps, 1)
            for b in range(B):
                if b % G == 0:
                    pe.wait_ge(xct_done, b // G + 1)
                last = pe.matmul(ps[:, 0, 0:D], xct[:, b, :], xct[:, b, :], start=b == 0, stop=b == B - 1)
            last.then_inc(cov_ps, 1)
            pe.wait_ge(cov_done, 1)
            pe.wait_ge(f_ld, 16 * 8)
            for n in range(NB):
                last = pe.matmul(ps[:, 1 + n // 4, (n % 4) * D:(n % 4 + 1) * D], f_wq[:, n * KD:(n + 1) * KD], cov[:, :], start=True, stop=True)
                if n % 4 == 3:
                    last.then_inc(cw_ps, 1)
            pe.wait_ge(fc_done, 6)
            for n in range(NB):
                last = pe.matmul(ps[0:1, 6, n * KEYS:(n + 1) * KEYS], f_bet[:, n:n + 1], f_keys[:, n, :], start=True, stop=True)
            pe.wait_ge(gain_done, 2)
            for n in range(NB):
                last = pe.matmul(ps[:, 5, n * KEYS:(n + 1) * KEYS], f_wqt[:, n, :], kscaled[:, n, :], start=True, stop=True)
            last.then_inc(simw_ps, 1)
            pe.wait_ge(simw_done, 2)

            def expert_rows(i, n, first):
                if n == 0:
                    pe.wait_ge(oneh_done, i * 1 + 1)
                if n >= 2 or not first:
                    pe.wait_ge(g_done, i * 4 + n - 1)
                for q in range(QP):
                    s = n * QP + q
                    dst = ps[:, 5 + n % 2, q * 2 * NC:(q + 1) * 2 * NC]
                    pe.matmul(dst, oneh[:, :, s], mv_hi[:, :, s], start=True, stop=False)
                    last = pe.matmul(dst, oneh[:, :, s], mv_lo[:, :, s], start=False, stop=True)
                last.then_inc(g_ps, 1)

            def add_experts(i, first):
                pe.wait_ge(g_done, i * 4 + 4)
                if not first:
                    pe.wait_ge(z_done, i * 4 - 3)
                for hf in range(2):
                    for c in range(NC):
                        last = pe.matmul(ps[0:S, 7, hf * D:(hf + 1) * D], wgt[:, c, hf, :], f_up[:, c, :], start=c == 0, stop=c == NC - 1)
                last.then_inc(y_ps, 1)

            def step(i, first, second):
                pe.wait_ge(fcur_done, i * 1 + 1)
                if not first:
                    pe.wait_ge(sim_done, i * 1)
                for hf in range(2):
                    pe.matmul(ps[0:S, hf, :], xc_cur[:, hf, :], sim_w[:, :], start=True, stop=False)
                    pe.matmul(ps[0:S, hf, :], ones_r[:, :], sim_c[:, :], start=False, stop=True).then_inc(sim_ps, 1)
                for r in range(2):
                    if r or not first:
                        pe.wait_ge(hid_done, i * 2 + r)
                    for c in range(4):
                        last = pe.matmul(ps[:, 2 + c // 2, (c % 2) * 2 * S:(c % 2 + 1) * 2 * S],
                                         f_down[:, (4 * r + c) * P:(4 * r + c + 1) * P], x2T[:, bass.ds(i * (2 * S), 2 * S)],
                                         start=True, stop=True)
                    last.then_inc(h_ps, 1)
                    if not first:
                        for n in (2 * r, 2 * r + 1):
                            expert_rows(i - 1, n, second)
                pe.wait_ge(soft_done, i * 4 + 4)
                pe.wait_ge(sel_done, i * 4 + 4)
                if not first:
                    pe.wait_ge(wlo_done, i * 2)
                for n in range(3):
                    last = pe.transpose(ps[:, 4, n * S:(n + 1) * S], sel[:, n, :, :].rearrange("s a k -> s (a k)"), ident[0:S, 0:S])
                last.then_inc(selT_ps, 1)
                if not first:
                    add_experts(i - 1, second)

            step(0, True, False)
            step(1, False, True)
            with pe.Fori(2, NPAIR) as i:
                step(i, False, False)
            for n in range(4):
                expert_rows(NPAIR - 1, n, False)
            add_experts(NPAIR - 1, False)


def decoder(nc, a, out):
    with ExitStack() as whole, ExitStack() as part:
        def sb(name, shape, dt=F32, until=whole):
            return until.enter_context(nc.sbuf_tensor(name, shape, dt))

        ps = whole.enter_context(nc.psum_tensor("ps", [P, 8, 512], F32))
        m = {
            "ident": sb("ident", [P, P]), "nhalf": sb("nhalf", [P, B]),
            "x2": sb("x2", [S, B, D]),
            "ident16": sb("ident16", [P, P], F16, part),
            "qa_hi": sb("qa_hi", [D, H, D], F16, part), "qa_lo": sb("qa_lo", [D, H, D], F16, part),
            "ln_hi": sb("ln_hi", [D, NT], F16, part), "ln_lo": sb("ln_lo", [D, NT], F16, part),
            "w2h": sb("w2h", [D, H, D + 1], F32, part),
            "sc1": sb("sc1", [D, B, H], F32, part),
            "kb": sb("kb", [D, B, H], F32, part),
            "x1": sb("x1", [S, B, D], F32, part),
        }
        m["context"] = Context(lambda name, shape, dt=F32: sb(name, shape, dt, part), lambda name: whole.enter_context(nc.semaphore(name)))
        front(nc, a, m, ps)
        cross(nc, a, m, ps)
        part.close()
        ffn(nc, a, m, ps, out)


def kernel(**inputs):
    import numpy as np
    import concourse.bacc as bacc
    from concourse.bass_utils import run_bass_kernel_spmd

    half = D // 2
    angle = np.arange(S)[None, :] / np.power(10000.0, np.arange(half) / half)[:, None]
    cos, sin = np.round(np.cos(angle)).astype(np.float32), np.round(np.sin(angle)).astype(np.float32)
    arrays = {n: np.asarray(v) for n, v in inputs.items()}
    for n in ("L0_attn_g_norm", "L0_attn_b_qkv", "L0_attn_b_proj", "L0_xattn_ln1_w", "L0_xattn_ln1_b",
              "L0_xattn_ln2_w", "L0_xattn_ln2_b"):
        arrays[n] = arrays[n].reshape(-1, 1)
    wkv = arrays.pop("L0_xattn_Wkv")
    arrays["wk_t"], arrays["wv_t"] = wkv[:, :H * DH].T, wkv[:, H * DH:].T
    arrays["wq_t"] = arrays.pop("L0_xattn_Wq").T
    arrays["ffn_wq_t"] = arrays["L0_ffn_w_q"].T
    arrays["ffn_keys_t"] = arrays.pop("L0_ffn_keys").transpose(3, 2, 0, 1)
    arrays["ffn_down_t"] = arrays.pop("L0_ffn_down_embed").T
    arrays["L0_ffn_bn_gamma"] = arrays["L0_ffn_bn_gamma"].reshape(NB, KD).T
    arrays["L0_ffn_bn_beta"] = arrays["L0_ffn_bn_beta"].reshape(NB, KD).T
    arrays["cos_t"] = np.concatenate([cos, cos])
    arrays["sin_t"] = np.concatenate([-sin, sin])

    nc = bacc.Bacc("TRN2", target_bir_lowering=False, num_devices=1)
    feed, aps = {}, {}
    for n, v in arrays.items():
        v = np.ascontiguousarray(v)
        feed[f"in_{n}"] = v
        aps[n] = nc.dram_tensor(f"in_{n}", v.shape, mybir.dt.from_np(v.dtype), kind="ExternalInput").ap()
    out = nc.dram_tensor("out_x", (B, S, D), F32, kind="ExternalOutput").ap()
    decoder(nc, aps, out)
    r = run_bass_kernel_spmd(nc, [feed], core_ids=[0])
    return r.results[0]["out_x"]
```
